# Optimizing a Trainium2 kernel written in Bass

```python
import numpy as np
import jax
import jax.numpy as jnp

def _softmax(x, axis=-1):
    return jax.nn.softmax(x, axis=axis)

def _gelu(x):
    return jax.nn.gelu(x, approximate=True)

def _silu(x):
    return jax.nn.silu(x)

def _sigmoid(x):
    return jax.nn.sigmoid(x)

def _layernorm(x, axis=-1, eps=1e-05):
    m = jnp.mean(x, axis=axis, keepdims=True)
    v = jnp.var(x, axis=axis, keepdims=True)
    return (x - m) / jnp.sqrt(v + eps)

def _scatter_add(tgt, idx, src, axis=0):
    return tgt.at[idx].add(src)

def _segment_sum(src, seg, n):
    return jax.ops.segment_sum(src, seg, n)
kernel_name = 'mk_gnn_resnorm_d4_gnn_r64_4f5d85'

def setup_inputs(seed: int=0):
    np.random.seed(seed)
    _w = jnp.asarray

    def _rec_inputs():
        import jax
        import jax.numpy as jnp
        _gk = jax.random.key(seed)
        x = -0.0005121 + 1.001 * jax.random.normal(jax.random.fold_in(_gk, 1), (100000, 32), jnp.float32)
        src = jax.random.randint(jax.random.fold_in(_gk, 2), (50000,), 0, 100000, jnp.int32)
        dst = jax.random.randint(jax.random.fold_in(_gk, 3), (50000,), 0, 100000, jnp.int32)
        _o = jnp.argsort(dst, stable=True)
        src = src[_o]
        dst = dst[_o]
        edge_attr_2 = jax.random.uniform(jax.random.fold_in(_gk, 12), (50000, 2), jnp.float32, 0.0, 1)
        edge_attr_32 = -8.16379e-05 + 0.999858 * jax.random.normal(jax.random.fold_in(_gk, 13), (50000, 32), jnp.float32)
        node_vec1 = jax.random.uniform(jax.random.fold_in(_gk, 15), (100000, 1), jnp.float32, 0.0, 0.999991)
        node_vec1_n2 = jax.random.uniform(jax.random.fold_in(_gk, 16), (100000, 1), jnp.float32, 0.0, 0.999991)
        return (x, src, dst, edge_attr_2, edge_attr_32, node_vec1, node_vec1_n2)
    x, src, dst, edge_attr_2, edge_attr_32, node_vec1, node_vec1_n2 = _rec_inputs()

    def _L0_gnn_setup():
        import jax, jax.numpy as jnp
        import numpy as np
        N_NODES = 100000
        N_EDGES = 25000
        F_IN = 32
        F_OUT = 32
        DIM = 2
        K = 5
        KTOT = K ** DIM
        S = 2 ** DIM
        NEG_SLOPE = 0.2
        _OFFSETS = np.array([[s >> d & 1 for d in range(DIM)] for s in range(S)], dtype=np.int32)
        _STRIDES = np.array([K ** d for d in range(DIM)], dtype=np.int32)

        def _spline_basis(pseudo):
            offsets = jnp.asarray(_OFFSETS)
            strides = jnp.asarray(_STRIDES)
            p = pseudo * (K - 1)
            fl = jnp.floor(p)
            frac = p - fl
            b = jnp.where(offsets[None] == 0, 1.0 - frac[:, None, :], frac[:, None, :])
            basis = jnp.prod(b, axis=-1)
            idx = jnp.clip(fl.astype(jnp.int32)[:, None, :] + offsets[None], 0, K - 1)
            widx = jnp.sum(idx * strides, axis=-1)
            return (basis, widx)
        key = jax.random.key(seed)
        ks = jax.random.split(key, 7)
        x = jax.random.normal(ks[0], (N_NODES, F_IN), dtype=jnp.float32)
        edge_index = jax.random.randint(ks[1], (2, N_EDGES), 0, N_NODES)
        pseudo = jax.random.uniform(ks[2], (N_EDGES, DIM), dtype=jnp.float32)
        bound = 1.0 / np.sqrt(KTOT * F_IN)
        weight = jax.random.uniform(ks[3], (KTOT, F_IN, F_OUT), jnp.float32, -bound, bound)
        root_weight = jax.random.uniform(ks[4], (F_IN, F_OUT), jnp.float32, -bound, bound)
        att_weight = jax.random.uniform(ks[5], (2 * F_OUT,), jnp.float32, -bound, bound)
        bias = jax.random.uniform(ks[6], (F_OUT,), jnp.float32, -bound, bound)
        return {'x': x, 'edge_index': edge_index, 'pseudo': pseudo, 'weight': weight, 'root_weight': root_weight, 'att_weight': att_weight, 'bias': bias}
    _L0_gnn_all = _L0_gnn_setup()
    _L0_gnn_in = {k: v for k, v in _L0_gnn_all.items() if k in ('weight', 'root_weight', 'att_weight', 'bias')}
    del _L0_gnn_all

    def _L1_gnn_setup():
        import jax, jax.numpy as jnp
        import numpy as np
        N_NODES = 100000
        N_EDGES = 50000
        D = 32
        N_LAYERS = 5

        def _gine_layer(x, edge_attr, src, dst, eps_l, W1_l, b1_l, W2_l, b2_l, n_nodes):
            msg = jax.nn.relu(x[src] + edge_attr)
            agg = jax.ops.segment_sum(msg, dst, num_segments=n_nodes)
            h = (1.0 + eps_l) * x + agg
            h = jax.nn.relu(h @ W1_l.T + b1_l)
            return h @ W2_l.T + b2_l
        key = jax.random.key(seed)
        ks = jax.random.split(key, 8)
        x = jax.random.normal(ks[0], (N_NODES, D), dtype=jnp.float32)
        edge_attr = jax.random.normal(ks[1], (N_EDGES, D), dtype=jnp.float32)
        edge_index = jax.random.randint(ks[2], (2, N_EDGES), 0, N_NODES, dtype=jnp.int64)
        eps = jnp.zeros((N_LAYERS,), dtype=jnp.float32)
        scale = 1.0 / np.sqrt(D)
        W1 = jax.random.normal(ks[3], (N_LAYERS, D, D), dtype=jnp.float32) * scale
        b1 = jax.random.normal(ks[4], (N_LAYERS, D), dtype=jnp.float32) * scale
        W2 = jax.random.normal(ks[5], (N_LAYERS, D, D), dtype=jnp.float32) * scale
        b2 = jax.random.normal(ks[6], (N_LAYERS, D), dtype=jnp.float32) * scale
        return {'x': x, 'edge_attr': edge_attr, 'eps': eps, 'W1': W1, 'b1': b1, 'W2': W2, 'b2': b2, 'edge_index': edge_index}
    _L1_gnn_all = _L1_gnn_setup()
    _L1_gnn_in = {k: v for k, v in _L1_gnn_all.items() if k in ('eps', 'W1', 'b1', 'W2', 'b2')}
    del _L1_gnn_all

    def _L2_gnn_setup():
        import jax, jax.numpy as jnp
        import numpy as np
        N_NODES = 100000
        key = jax.random.key(seed)
        k1, k2, k3 = jax.random.split(key, 3)
        x = jax.random.normal(k1, (N_NODES, 32), dtype=jnp.float32)
        src = jax.random.randint(k2, (25000,), 0, N_NODES, dtype=jnp.int64)
        dst = jax.random.randint(k3, (25000,), 0, N_NODES, dtype=jnp.int64)
        return {'x': x, 'src': src, 'dst': dst}
    _L2_gnn_all = _L2_gnn_setup()
    _L2_gnn_in = {k: v for k, v in _L2_gnn_all.items() if k in ()}
    del _L2_gnn_all

    def _L3_gnn_setup():
        import jax, jax.numpy as jnp
        import numpy as np
        N_NODES = 100000
        N_EDGES = 25000
        D_FEAT = 32
        key = jax.random.key(seed)
        k1, k2, k3, k4, k5 = jax.random.split(key, 5)
        src_feats = jax.random.normal(k1, (N_NODES, D_FEAT), dtype=jnp.float32)
        cj = jax.random.uniform(k2, (N_NODES, 1), dtype=jnp.float32)
        ci = jax.random.uniform(k3, (N_NODES, 1), dtype=jnp.float32)
        src_idx = jax.random.randint(k4, (N_EDGES,), 0, N_NODES, dtype=jnp.int32)
        dst_idx = jax.random.randint(k5, (N_EDGES,), 0, N_NODES, dtype=jnp.int32)
        return {'src_feats': src_feats, 'cj': cj, 'ci': ci, 'src_idx': src_idx, 'dst_idx': dst_idx}
    _L3_gnn_all = _L3_gnn_setup()
    _L3_gnn_in = {k: v for k, v in _L3_gnn_all.items() if k in ()}
    del _L3_gnn_all
    return {'x': x, 'src': src, 'dst': dst, 'edge_attr_2': edge_attr_2, 'edge_attr_32': edge_attr_32, 'node_vec1': node_vec1, 'node_vec1_n2': node_vec1_n2, 'L0_gnn_weight': _L0_gnn_in['weight'], 'L0_gnn_root_weight': _L0_gnn_in['root_weight'], 'L0_gnn_att_weight': _L0_gnn_in['att_weight'], 'L0_gnn_bias': _L0_gnn_in['bias'], 'L1_gnn_eps': _L1_gnn_in['eps'], 'L1_gnn_W1': _L1_gnn_in['W1'], 'L1_gnn_b1': _L1_gnn_in['b1'], 'L1_gnn_W2': _L1_gnn_in['W2'], 'L1_gnn_b2': _L1_gnn_in['b2']}

def reference(x, src, dst, edge_attr_2, edge_attr_32, node_vec1, node_vec1_n2, L0_gnn_weight, L0_gnn_root_weight, L0_gnn_att_weight, L0_gnn_bias, L1_gnn_eps, L1_gnn_W1, L1_gnn_b1, L1_gnn_W2, L1_gnn_b2):
    import jax
    import jax.numpy as jnp

    def _L0_gnn_ref(x, edge_index, pseudo, weight, root_weight, att_weight, bias):
        import jax, jax.numpy as jnp
        import numpy as np
        N_NODES = 100000
        N_EDGES = 25000
        F_IN = 32
        F_OUT = 32
        DIM = 2
        K = 5
        KTOT = K ** DIM
        S = 2 ** DIM
        NEG_SLOPE = 0.2
        _OFFSETS = np.array([[s >> d & 1 for d in range(DIM)] for s in range(S)], dtype=np.int32)
        _STRIDES = np.array([K ** d for d in range(DIM)], dtype=np.int32)

        def _spline_basis(pseudo):
            offsets = jnp.asarray(_OFFSETS)
            strides = jnp.asarray(_STRIDES)
            p = pseudo * (K - 1)
            fl = jnp.floor(p)
            frac = p - fl
            b = jnp.where(offsets[None] == 0, 1.0 - frac[:, None, :], frac[:, None, :])
            basis = jnp.prod(b, axis=-1)
            idx = jnp.clip(fl.astype(jnp.int32)[:, None, :] + offsets[None], 0, K - 1)
            widx = jnp.sum(idx * strides, axis=-1)
            return (basis, widx)
        row, col = (edge_index[0], edge_index[1])
        basis, widx = _spline_basis(pseudo)
        xw = jnp.einsum('nf,kfo->nko', x, weight)
        flat = col[:, None] * KTOT + widx
        gathered = xw.reshape(-1, F_OUT)[flat]
        msg = jnp.einsum('es,esf->ef', basis, gathered)
        x_root = x @ root_weight
        alpha = x_root[row] @ att_weight[:F_OUT] + msg @ att_weight[F_OUT:]
        alpha = jnp.where(alpha > 0, alpha, NEG_SLOPE * alpha)
        amax = jax.ops.segment_max(alpha, row, num_segments=N_NODES)
        amax = jnp.where(jnp.isfinite(amax), amax, 0.0)
        ex = jnp.exp(alpha - amax[row])
        denom = jax.ops.segment_sum(ex, row, num_segments=N_NODES)
        att = ex / (denom[row] + 1e-16)
        out = jax.ops.segment_sum(msg * att[:, None], row, num_segments=N_NODES)
        return out + x_root + bias

    def _L1_gnn_ref(x, edge_attr, eps, W1, b1, W2, b2, edge_index):
        import jax, jax.numpy as jnp
        import numpy as np
        N_NODES = 100000
        N_EDGES = 50000
        D = 32
        N_LAYERS = 5

        def _gine_layer(x, edge_attr, src, dst, eps_l, W1_l, b1_l, W2_l, b2_l, n_nodes):
            msg = jax.nn.relu(x[src] + edge_attr)
            agg = jax.ops.segment_sum(msg, dst, num_segments=n_nodes)
            h = (1.0 + eps_l) * x + agg
            h = jax.nn.relu(h @ W1_l.T + b1_l)
            return h @ W2_l.T + b2_l
        src = edge_index[0]
        dst = edge_index[1]
        n_nodes = x.shape[0]
        out = x
        for l in range(N_LAYERS):
            out = jax.nn.relu(_gine_layer(x, edge_attr, src, dst, eps[l], W1[l], b1[l], W2[l], b2[l], n_nodes))
        return out

    def _L2_gnn_ref(x, src, dst):
        import jax, jax.numpy as jnp
        import numpy as np
        N_NODES = 100000
        n = x.shape[0]
        msg_sum = jax.ops.segment_sum(x[src], dst, num_segments=n)
        deg = jax.ops.segment_sum(jnp.ones_like(dst, dtype=x.dtype), dst, num_segments=n)
        return msg_sum / jnp.maximum(deg, 1.0)[:, None]

    def _L3_gnn_ref(src_feats, cj, ci, src_idx, dst_idx):
        import jax, jax.numpy as jnp
        import numpy as np
        N_NODES = 100000
        N_EDGES = 25000
        D_FEAT = 32
        weighted = src_feats * cj
        msgs = weighted[src_idx]
        agg = jax.ops.segment_sum(msgs, dst_idx, num_segments=N_NODES)
        return agg * ci
    edge_index = jnp.stack([src, dst])
    x = _layernorm(x + _L0_gnn_ref(x, edge_index, edge_attr_2, L0_gnn_weight, L0_gnn_root_weight, L0_gnn_att_weight, L0_gnn_bias), axis=-1)
    x = _layernorm(x + _L1_gnn_ref(x, edge_attr_32, L1_gnn_eps, L1_gnn_W1, L1_gnn_b1, L1_gnn_W2, L1_gnn_b2, edge_index), axis=-1)
    x = _layernorm(x + _L2_gnn_ref(x, src, dst), axis=-1)
    x = _layernorm(x + _L3_gnn_ref(x, node_vec1, node_vec1_n2, src, dst), axis=-1)
    return x

_drawn_inputs = setup_inputs


def setup_inputs(seed=0):
    import zlib

    import numpy as np

    out = dict(_drawn_inputs(seed))
    spreads = {'L1_gnn_eps': (0.0, 0.1)}
    factors = {}
    for name, (base, spread) in spreads.items():
        noise = np.random.default_rng([zlib.crc32(name.encode()), seed]).standard_normal(out[name].shape)
        drawn = base * np.exp(spread * noise) if base else spread * noise
        out[name] = jnp.asarray(drawn.astype(out[name].dtype))
    for name, factor in factors.items():
        out[name] = (out[name] * factor).astype(out[name].dtype)
    return out
```

```python
from contextlib import ExitStack

import concourse.bass as bass
from concourse import mybir


F32 = mybir.dt.float32
I32 = mybir.dt.int32
ALU = mybir.AluOpType
ACT = mybir.ActivationFunctionType
AX_X = mybir.AxisListType.X

P = 128
G = 4
ROW = G * P
NEG_BIG = -2.0 ** 126
SLOPE = 0.2
LN_EPS = 1e-5
DEN_EPS = 1e-16


def ds(start, size):
    return bass.ds(start, size)


def wait(eng, sem, value):
    if not (isinstance(value, int) and value <= 0):
        eng.wait_ge(sem, value)


class Chain:

    def __init__(self, eng, sem, per, first=0):
        self.eng, self.sem, self.per, self.first = eng, sem, per, first
        self.base, self.n = first, 0

    def body(self, number):
        self.base, self.n = self.first + number * self.per, 0

    def step(self, ins):
        ins.then_inc(self.sem, 1)
        self.n += 1

    def wait(self, n=None):
        self.eng.wait_ge(self.sem, self.base + (self.n if n is None else n))


def gnn_program(nc, x, src, dst, edge_attr_2, edge_attr_32, node_vec1, node_vec1_n2,
                spline_w, root_w, att_w, bias, gine_eps, gine_w1, gine_b1, gine_w2, gine_b2, out):
    N, D = x.shape
    E = src.shape[0]
    K = 5
    LAST = gine_eps.shape[0] - 1
    assert P % D == 0 and spline_w.shape[0] == K * K
    B = P // D

    COLS = -(-N // P)
    NT = COLS * P
    LASTP = N - (P - 1) * COLS
    HEAD = 112
    STEP = 3 * B
    CH = 4 * STEP
    CHUNKS = COLS // CH
    TAIL = COLS - CHUNKS * CH
    assert CHUNKS % 2 == 0 and 0 < TAIL < CH
    HALF = CHUNKS // 2
    STEPS = [list(range(0, CH, STEP)), list(range(0, TAIL, STEP))]
    NSTEP = CHUNKS * len(STEPS[0]) + len(STEPS[1])
    SLOT_USES = (HALF + 1, HALF)

    MAIN = E // P
    REST = E - MAIN * P
    TILES = -(-(MAIN + 1) // (2 * G)) * 2 * G
    NG = TILES // G
    assert TILES > MAIN + 1 - (REST == 0) and MAIN % G == 2

    TRASH = NT
    RT = NT + ROW
    SW = D + 3
    AW = D + 1

    def dram(name, rows, width):
        return nc.dram_tensor(name, (rows, width), F32).ap()

    state = [dram("state_even", RT, SW), dram("state_odd", RT, SW)]
    agg = [None, dram("agg_1", RT, AW), dram("agg_2", RT, D), dram("agg_3", RT, D)]
    xt = [x, dram("x_1", NT, D), dram("x_2", NT, D), dram("x_3", NT, D)]

    with ExitStack() as ctx:
        def sb(name, shape, dt=F32):
            return ctx.enter_context(nc.sbuf_tensor(name, shape, dt))

        def sem(name):
            return ctx.enter_context(nc.semaphore(name))

        def pair(name):
            return [sem(name + "_0"), sem(name + "_1")]

        xs = sb("xs", [P, COLS, D])
        src_row = sb("src_row", [P, TILES], I32)
        dst_row = sb("dst_row", [P, TILES], I32)
        src_key = sb("src_key", [P, TILES])
        dst_key = sb("dst_key", [P, TILES])
        src_rel = sb("src_rel", [P, TILES])
        dst_rel = sb("dst_rel", [P, TILES])
        dst_first = sb("dst_first", [P, TILES], I32)
        attr2 = sb("attr2", [P, TILES, 2])
        hat = [sb("hat0", [P, TILES, K]), sb("hat1", [P, TILES, K])]
        ident = sb("ident", [P, P])
        earlier = sb("earlier", [P, ROW])
        spare_i = sb("spare_i", [P, G], I32)
        spare = sb("spare", [P, G])
        root = sb("root", [P, P + B])
        att1 = sb("att1", [P, D])
        att2 = sb("att2", [P, D])
        bias_b = sb("bias_b", [P, D])
        w_a = sb("w_a", [P, K, D])
        w_b = sb("w_b", [D, K, D])
        w1 = sb("w1", [P, P])
        w2 = sb("w2", [P, P])
        b1 = sb("b1", [P, 1])
        b2 = sb("b2", [P, 1])
        eps1 = sb("eps1", [P, 1])
        one = sb("one", [P, 1])
        ln_eps = sb("ln_eps", [P, 1])
        cj = sb("cj", [P, COLS])
        ci = sb("ci", [P, COLS])
        deg = hat[0][:, :, :].rearrange("p t k -> p (t k)")[:, 0:COLS]

        xg = [sb(f"xg{k}", [P, G, D]) for k in range(2)]
        src_at = [sb(f"src_at{k}", [P, G], I32) for k in range(2)]
        dst_at = [sb(f"dst_at{k}", [P, G], I32) for k in range(2)]
        first_at = [sb(f"first_at{k}", [P, G], I32) for k in range(2)]
        key_at = [sb(f"key_at{k}", [P, G]) for k in range(2)]
        st = [sb(f"st{k}", [P, G, SW]) for k in range(2)]
        st_new = [sb(f"st_new{k}", [P, G, SW]) for k in range(2)]
        msg = [sb(f"msg{k}", [P, G, D]) for k in range(2)]
        val = [sb(f"val{k}", [P, G, AW]) for k in range(2)]
        tmax = [sb(f"tmax{k}", [P, 2, G]) for k in range(2)]
        expo = [sb(f"expo{k}", [P, 2, G]) for k in range(2)]
        count = [sb(f"count{k}", [P, G]) for k in range(2)]
        attr = [sb(f"attr{k}", [P, G, D]) for k in range(2)]
        sums = [sb(f"sums{k}", [P, G, AW]) for k in range(2)]

        ARENA = 13952
        arena = sb("arena", [P, ARENA])
        at = [0]

        def cut(shape, start=None):
            if start is not None:
                at[0] = start
            n = 1
            for s in shape:
                n *= s
            v = arena[:, at[0]:at[0] + n]
            at[0] += n
            assert at[0] <= ARENA
            if len(shape) == 2:
                v = v.rearrange("p (a b) -> p a b", a=shape[0])
            if len(shape) == 3:
                v = v.rearrange("p (a b c) -> p a b c", a=shape[0], b=shape[1])
            return v

        same = [cut([G, ROW], 0), cut([G, ROW])]
        apart = cut([G, ROW])
        junk = cut([sum(range(1, G + 1)) * P])
        z = cut([G, K, D])
        ty = cut([G, K, D])
        zt_a = cut([ROW])
        zt_b = cut([ROW])
        lw = cut([G, D])
        ZERO = 1048
        zeros = cut([ZERO], ARENA - ZERO)
        node_in = [[cut([CH, SW], 0), cut([CH, SW])], [cut([CH, SW]), cut([CH, SW])]]
        y = [cut([CH, D]), cut([CH, D])]
        sq = cut([CH, D])
        xT = [cut([STEP * D]) for _ in range(2)]
        hT = cut([STEP * D])
        oT = cut([STEP * D])
        scratch = sb("scratch", [P, B, D])
        small = sb("small", [P, 2, 8, CH])
        psum = ctx.enter_context(nc.psum_tensor("psum", [P, 8, 512], F32))

        pool_consts = sem("pool_consts")
        cleared = sem("cleared")
        pool_turns, sp_turns = sem("pool_turns"), sem("sp_turns")
        edges_in, consts_in, nodes_in, last_stored = sem("edges_in"), sem("consts_in"), sem("nodes_in"), sem("last_stored")
        setup, setup_steps = sem("setup"), sem("setup_steps")
        zeroed = sem("zeroed")
        x_in = pair("x_in")
        turned, turned_sb, mixed, unmixed = sem("turned"), sem("turned_sb"), sem("mixed"), sem("unmixed")
        rooted = sem("rooted")
        init_stored = pair("init_stored")
        e0 = sem("e0_steps")
        rows_at, keys_at, dst_rows_at = sem("rows_at"), sem("keys_at"), sem("dst_rows_at")
        x_got, st_got = pair("x_got"), pair("st_got")
        z_ready, z_turned, z_turned_sb, y_ready = sem("z_ready"), sem("z_turned"), sem("z_turned_sb"), sem("y_ready")
        y_used, t_ready, t_row, max_ready = sem("y_used"), sem("t_ready"), sem("t_row"), sem("max_ready")
        key_row, apart_ready, same_ready = sem("key_row"), sem("apart_ready"), sem("same_ready")
        expo_in, expo_out, val_ready, sum_ready, st_ready = (sem("expo_in"), sem("expo_out"), sem("val_ready"),
                                                             sem("sum_ready"), sem("st_ready"))
        first_ready = sem("first_ready")
        st_sent = pair("st_sent")
        ge = [None] + [sem(f"e{l}_steps") for l in (1, 2, 3)]
        g_rows_at, g_keys_at, g_firsts_at = sem("g_rows_at"), sem("g_keys_at"), sem("g_firsts_at")
        g_got, attr_in = pair("g_got"), pair("attr_in")
        g_key_row, g_same, g_sent_in, g_relu, g_sum, g_sum_sb = (sem("g_key_row"), sem("g_same"), sem("g_sent_in"),
                                                                 sem("g_relu"), sem("g_sum"), sem("g_sum_sb"))
        agg_sent = pair("agg_sent")
        n_steps = [sem(f"n{l}_steps") for l in range(4)]
        n_in = pair("n_in")
        n_expo_in, n_expo_out, n_share, n_scaled = sem("n_expo_in"), sem("n_expo_out"), sem("n_share"), sem("n_scaled")
        n_y, n_centred, n_squared, n_rstd, n_done = (sem("n_y"), sem("n_centred"), sem("n_squared"), sem("n_rstd"),
                                                     sem("n_done"))
        n_var, n_std = sem("n_var"), sem("n_std")
        n_weighted = sem("n_weighted")
        m_h, m_turned, m_turned_sb, m_hid, m_hid_sb, m_out, m_out_sb, m_back, m_back_used = (
            sem("m_h"), sem("m_turned"), sem("m_turned_sb"), sem("m_hid"), sem("m_hid_sb"), sem("m_out"),
            sem("m_out_sb"), sem("m_back"), sem("m_back_used"))
        x_stored, out_stored = pair("x_stored"), pair("out_stored")

        def table(t, width):
            return t[0:NT, :].rearrange("(p c) w -> p (c w)", p=P)

        x_head = x[0:HEAD * COLS, :].rearrange("(p c) w -> p (c w)", p=HEAD)
        x_mid = x[HEAD * COLS:(P - 1) * COLS, :].rearrange("(p c) w -> p (c w)", p=P - 1 - HEAD)
        x_last = x[(P - 1) * COLS:N, :].rearrange("(p c) w -> p (c w)", p=1)
        out_head = out[0:HEAD * COLS, :].rearrange("(p c) w -> p (c w)", p=HEAD)
        out_mid = out[HEAD * COLS:(P - 1) * COLS, :].rearrange("(p c) w -> p (c w)", p=P - 1 - HEAD)
        out_last = out[(P - 1) * COLS:N, :].rearrange("(p c) w -> p (c w)", p=1)
        xs_flat = xs[:, :, :].rearrange("p c w -> p (c w)")

        def bank(b, width=512):
            return psum[:, b, 0:width]

        def sizes(n, c):
            w = min(STEP, n - c) * D
            assert w % P == 0 or w < P
            return min(P, w), -(-w // P) * P

        def cols(i, s):
            return (2 * i + s) * CH

        def chunks(eng, body):
            body(0, 0, CH)
            body(0, 1, CH)
            with eng.Fori(1, HALF - 1) as i:
                body(i, 0, CH)
                body(i, 1, CH)
            body(HALF - 1, 0, CH)
            body(HALF - 1, 1, CH)
            body(HALF, 0, TAIL)

        def groups(eng, body):
            body(0, 0)
            body(0, 1)
            with eng.Fori(1, NG // 2 - 1) as i:
                body(i, 0)
                body(i, 1)
            body(NG // 2 - 1, 0)
            body(NG // 2 - 1, 1)

        def is_last(i, k, ahead):
            return isinstance(i, int) and 2 * i + k + ahead >= NG

        def after_zeroing(eng):
            eng.wait_ge(zeroed, 16 * 3)

        def after_initial(eng):
            for s in range(2):
                eng.wait_ge(init_stored[s], 32 * SLOT_USES[s] + 32 * (1 - s))

        def after_states(eng):
            for k in range(2):
                eng.wait_ge(st_sent[k], 16 * G * (NG // 2))

        def after_nodes(eng, l):
            for s in range(2):
                eng.wait_ge(x_stored[s], 16 * SLOT_USES[s] * (l + 1))

        def after_edges(eng, l):
            for k in range(2):
                eng.wait_ge(agg_sent[k], 16 * G * (NG // 2) * l)

        def loaded(l, i, s):
            if l == 0:
                return 32 * (i + 1)
            return 32 * SLOT_USES[s] + 16 * ((l - 1) * SLOT_USES[s] + i + 1)

        def last_cols(i, s):
            return max(0, min(CH, LASTP - (2 * i + s) * CH)) if isinstance(i, int) else CH

        assert (2 * HALF - 2) * CH <= LASTP < CHUNKS * CH

        def x_loaded(i, s):
            if not isinstance(i, int):
                return 48 * (i + 1)
            return sum(48 if last_cols(m, s) else 32 for m in range(i + 1))

        def in_layer(l, i, s):
            return l * (CHUNKS + 1) + 2 * i + s

        def attr_loaded(i, k):
            return 16 * (i + 1) + 16 * is_last(i, k, 1)

        E0_STEPS = 8
        N_STEPS = (11, 2, 3, 3)

        block = ctx.enter_context(nc.Block())

        @block.sync
        def _(sp):
            sp.wait_ge(cleared, 1)
            for row, to in ((src, src_row), (dst, dst_row)):
                sp.dma_start(to[:, 0:MAIN], row[0:MAIN * P].rearrange("(p t) -> p t", p=P)).then_inc(edges_in, 16)
                sp.dma_start(to[0:REST, MAIN:MAIN + 1],
                             row[MAIN * P:E].rearrange("(p t) -> p t", t=1)).then_inc(edges_in, 16)
            sp.dma_start(attr2[:, 0:MAIN, :].rearrange("p t a -> p (t a)"),
                         edge_attr_2[0:MAIN * P, :].rearrange("(p t) a -> p (t a)", p=P)).then_inc(edges_in, 16)
            sp.dma_start(attr2[0:REST, MAIN, :], edge_attr_2[MAIN * P:E, :]).then_inc(edges_in, 16)
            def const(to, of):
                sp.dma_start(to, of).then_inc(consts_in, 16)

            for j in range(B):
                const(root[j * D:(j + 1) * D, j * D:(j + 1) * D], root_w)
                with nc.allow_non_contiguous_dma("small transposed weights"):
                    const(w1[j * D:(j + 1) * D, j * D:(j + 1) * D], gine_w1[LAST].rearrange("o f -> f o"))
                    const(w2[j * D:(j + 1) * D, j * D:(j + 1) * D], gine_w2[LAST].rearrange("o f -> f o"))
                const(b1[j * D:(j + 1) * D, :], gine_b1[LAST].rearrange("(o a) -> o a", a=1))
                const(b2[j * D:(j + 1) * D, :], gine_b2[LAST].rearrange("(o a) -> o a", a=1))
            for i in range(K):
                to = w_a[i * D:(i + 1) * D, :, :] if i < B else w_b[:, :, :]
                const(to, spline_w.rearrange("(j i) f o -> i f j o", i=K)[i])
            const(att1[:, :], att_w[0:D].rearrange("(a o) -> a o", a=1).to_broadcast([P, D]))
            const(att2[:, :], att_w[D:2 * D].rearrange("(a o) -> a o", a=1).to_broadcast([P, D]))
            const(bias_b[:, :], bias.rearrange("(a o) -> a o", a=1).to_broadcast([P, D]))
            const(eps1[:, :], gine_eps[LAST:LAST + 1].rearrange("(a o) -> a o", a=1).to_broadcast([P, 1]))

            def load_x(i, s, n):
                wait(sp, turned, (2 * i + s - 1) * len(STEPS[0]))
                sp.sem_inc(sp_turns, 1)
                wait(sp, x_in[s], x_loaded(i - 1, s))
                c = cols(i, s) * D
                to = y[s].rearrange("p c w -> p (c w)")
                sp.dma_start(to[0:HEAD, 0:n * D], x_head[:, ds(c, n * D)]).then_inc(x_in[s], 16)
                sp.dma_start(to[HEAD:P - 1, 0:n * D], x_mid[:, ds(c, n * D)]).then_inc(x_in[s], 16)
                have = last_cols(i, s)
                if have:
                    sp.dma_start(to[P - 1:P, 0:have * D], x_last[:, ds(c, have * D)]).then_inc(x_in[s], 16)

            def store_init(i, s, n):
                sp.wait_ge(rooted, 2 * i + s + 1)
                c = cols(i, s) * SW
                for t in range(2):
                    sp.dma_start(table(state[t], SW)[:, ds(c, n * SW)],
                                 node_in[s][0][:, 0:n, :].rearrange("p c w -> p (c w)")).then_inc(init_stored[s], 16)
                    if n == TAIL:
                        sp.dma_start(state[t][NT:RT, :].rearrange("(p c) w -> p (c w)", p=P),
                                     node_in[s][0][:, 0:G, :].rearrange("p c w -> p (c w)")).then_inc(init_stored[s], 16)

            def load_and_store(i, s, n):
                load_x(i, s, n)
                store_init(i - 1, s, CH)

            load_x(0, 0, CH)
            load_x(0, 1, CH)
            with sp.Fori(1, HALF - 1) as i:
                load_and_store(i, 0, CH)
                load_and_store(i, 1, CH)
            load_and_store(HALF - 1, 0, CH)
            load_and_store(HALF - 1, 1, CH)
            load_and_store(HALF, 0, TAIL)
            store_init(HALF - 1, 1, CH)
            store_init(HALF, 0, TAIL)
            for v, to in ((node_vec1, cj), (node_vec1_n2, ci)):
                sp.dma_start(to[0:P - 1, :], v[0:(P - 1) * COLS, :].rearrange("(p c) a -> p (c a)", p=P - 1)).then_inc(nodes_in, 16)
                sp.dma_start(to[P - 1:P, 0:LASTP], v[(P - 1) * COLS:N, :].rearrange("(p c) a -> p (c a)", p=1)).then_inc(nodes_in, 16)
            sp.wait_ge(setup, 1)
            for t in agg[1:]:
                per = RT // P * t.shape[1]
                piece = max(n for n in range(1, ZERO + 1) if per % n == 0)
                sp.dma_start(t.rearrange("(p c) w -> p (c w)", p=P).rearrange("p (a b) -> p a b", b=piece),
                             zeros[:, 0:piece].unsqueeze(1).to_broadcast([P, per // piece, piece])).then_inc(zeroed, 16)

            def load_attr(i, k):
                wait(sp, g_relu, 2 * i + k - 1)
                if isinstance(i, int) and (2 * i + k + 1) * G > MAIN:
                    left = MAIN - (2 * i + k) * G
                    sp.dma_start(attr[k][:, 0:left, :], edge_attr_32[0:MAIN * P, :].rearrange(
                        "(p t) w -> p t w", p=P)[:, MAIN - left:MAIN, :]).then_inc(attr_in[k], 16)
                    sp.dma_start(attr[k][0:REST, left, :], edge_attr_32[MAIN * P:E, :]).then_inc(attr_in[k], 16)
                    return
                sp.dma_start(attr[k][:, :, :].rearrange("p t w -> p (t w)"),
                             edge_attr_32[0:MAIN * P, :].rearrange("(p t) w -> p (t w)", p=P)[
                                 :, ds((2 * i + k) * (G * D), G * D)]).then_inc(attr_in[k], 16)

            def load_nodes(l):
                def body(i, s, n):
                    wait(sp, n_done, in_layer(l, i, s) - 1)
                    if l == 0:
                        c = cols(i, s) * SW
                        for t in range(2):
                            sp.dma_start(node_in[s][t][:, 0:n, :].rearrange("p c w -> p (c w)"),
                                         table(state[t], SW)[:, ds(c, n * SW)]).then_inc(n_in[s], 16)
                    else:
                        w = AW if l == 1 else D
                        sp.dma_start(node_in[s][0].rearrange("p c w -> p (c w)")[:, 0:n * w],
                                     table(agg[l], w)[:, ds(cols(i, s) * w, n * w)]).then_inc(n_in[s], 16)
                return body

            def store_nodes(l, i, s, n):
                c = cols(i, s) * D
                if l == 2:
                    sp.wait_ge(n_weighted, 2 * i + s + 1)
                    sp.dma_start(table(xt[3], D)[:, ds(c, n * D)],
                                 node_in[s][1].rearrange("p c w -> p (c w)")[:, 0:n * D]).then_inc(x_stored[s], 16)
                    return
                sp.wait_ge(n_done, in_layer(l, i, s) + 1)
                if l < 3:
                    sp.dma_start(table(xt[l + 1], D)[:, ds(c, n * D)], xs_flat[:, ds(c, n * D)]).then_inc(x_stored[s], 16)
                else:
                    sp.dma_start(out_head[:, ds(c, n * D)], xs_flat[0:HEAD, ds(c, n * D)]).then_inc(out_stored[s], 16)
                    sp.dma_start(out_mid[:, ds(c, n * D)], xs_flat[HEAD:P - 1, ds(c, n * D)]).then_inc(out_stored[s], 16)

            def nodes(l):
                load = load_nodes(l)
                load(0, 0, CH)
                load(0, 1, CH)
                with sp.Fori(1, HALF) as i:
                    for s in range(2):
                        load(i, s, CH)
                        store_nodes(l, i - 1, s, CH)
                load(HALF, 0, TAIL)
                store_nodes(l, HALF - 1, 0, CH)
                store_nodes(l, HALF - 1, 1, CH)
                store_nodes(l, HALF, 0, TAIL)

            after_states(sp)
            nodes(0)
            groups(sp, load_attr)
            for l in (1, 2, 3):
                after_edges(sp, l)
                nodes(l)
            sp.dma_start(out_last, xs_flat[P - 1:P, 0:LASTP * D]).then_inc(last_stored, 16)
            for s in range(2):
                sp.wait_ge(out_stored[s], 32 * SLOT_USES[s])
            sp.wait_ge(last_stored, 16)

        @block.gpsimd
        def _(pool):
            nc.gpsimd.memset(ident[:, :], 0.0)
            nc.gpsimd.memset(earlier[:, :], 1.0).then_inc(pool_consts, 1)
            nc.gpsimd.iota(spare_i[:, :], [[P, G]], base=TRASH, channel_multiplier=1)
            pool.wait_ge(pool_consts, 1)
            nc.gpsimd.affine_select(out=ident[:, :], in_=ident[:, :], compare_op=ALU.not_equal, fill=1.0,
                                    base=0, pattern=[[-1, P]], channel_multiplier=1)
            nc.gpsimd.affine_select(out=earlier[:, ROW - P:ROW], in_=earlier[:, ROW - P:ROW], compare_op=ALU.is_gt,
                                    fill=0.0, base=0, pattern=[[-1, P]], channel_multiplier=1).then_inc(pool_consts, 1)

            def gather(to, of, rows, done):
                pool.sem_inc(pool_turns, 1)
                for t in range(G):
                    nc.gpsimd.indirect_dma_start(to[:, t, :], None, of, bass.IndirectOffsetOnAxis(rows[:, t:t + 1], 0),
                                                 bounds_check=of.shape[0] - 1, oob_is_err=True).then_inc(done, 16)

            def scatter(to, rows, of, done, **add):
                pool.sem_inc(pool_turns, 1)
                for t in range(G):
                    nc.gpsimd.indirect_dma_start(to, bass.IndirectOffsetOnAxis(rows[:, t:t + 1], 0), of[:, t, :], None,
                                                 bounds_check=RT - 1, oob_is_err=True, **add).then_inc(done, 16)

            def gather_x(k):
                gather(xg[k], xt[0], dst_at[k], x_got[k])

            def send_states(i, k):
                pool.wait_ge(st_ready, 2 * i + k + 1)
                pool.wait_ge(first_ready, 2 * i + k + 1)
                scatter(state[k], first_at[k], st_new[k], st_sent[k])

            def body0(i, k):
                pool.wait_ge(rows_at, 2 * i + k + 1)
                wait(pool, st_sent[k], 16 * G * i)
                gather(st[k], state[k], src_at[k], st_got[k])
                if not (isinstance(i, int) and 2 * i + k == 0):
                    send_states(i - 1 + k, 1 - k)
                if not is_last(i, k, 2):
                    pool.wait_ge(dst_rows_at, 2 * i + k + 3)
                    pool.wait_ge(z_ready, 2 * i + k + 1)
                    gather_x(k)

            for k in range(2):
                pool.wait_ge(dst_rows_at, k + 1)
                gather_x(k)
            after_initial(pool)
            groups(pool, body0)
            send_states(NG // 2 - 1, 1)

            def nodes(l):
                def body(i, s, n):
                    rst = small[:, s, 7, 0:n].unsqueeze(2).to_broadcast([P, n, D])
                    xc = xs[:, ds(cols(i, s), n), :]
                    if l == 0:
                        pool.wait_ge(n_share, 2 * i + s + 1)
                        share = small[:, s, 3, 0:n].unsqueeze(2).to_broadcast([P, n, D])
                        v = node_in[s][1][:, 0:n, 2:2 + D]
                        nc.gpsimd.tensor_tensor(v, v, share, ALU.mult).then_inc(n_scaled, 1)
                    if l >= 2:
                        pool.wait_ge(n_in[s], loaded(l, i, s))
                        if l == 2:
                            pool.wait_ge(n_share, CHUNKS + 2)
                        by = deg if l == 2 else ci
                        v = node_in[s][0].rearrange("p c w -> p (c w)")[:, 0:n * D].rearrange("p (c w) -> p c w", w=D)
                        nc.gpsimd.tensor_tensor(v, v, by[:, ds(cols(i, s), n)].unsqueeze(2).to_broadcast([P, n, D]),
                                                ALU.mult).then_inc(n_scaled, 1)
                    if l != 2:
                        pool.wait_ge(n_rstd, in_layer(l, i, s) + 1)
                        nc.gpsimd.tensor_tensor(xc, y[s][:, 0:n, :], rst, ALU.mult).then_inc(n_done, 1)
                    else:
                        pool.wait_ge(n_done, in_layer(l, i, s) + 1)
                        wait(pool, x_stored[s], 16 * (2 * SLOT_USES[s] + i))
                        v = node_in[s][1].rearrange("p c w -> p (c w)")[:, 0:n * D].rearrange("p (c w) -> p c w", w=D)
                        nc.gpsimd.tensor_tensor(v, xc, cj[:, ds(cols(i, s), n)].unsqueeze(2).to_broadcast([P, n, D]),
                                                ALU.mult).then_inc(n_weighted, 1)
                chunks(pool, body)

            nodes(0)

            def edges(l):
                def get(i, k):
                    pool.wait_ge(g_rows_at, (l - 1) * NG + 2 * i + k + 1)
                    gather(xg[k], xt[l], src_at[k], g_got[k])

                def body(i, k):
                    g = (l - 1) * NG + 2 * i + k
                    pool.wait_ge(g_sum_sb, g + 1)
                    pool.wait_ge(g_firsts_at, g + 1)
                    wait(pool, agg_sent[1 - k], 16 * G * ((l - 1) * (NG // 2) + i + k))
                    scatter(agg[l], first_at[k], sums[k][:, :, 0:AW if l == 1 else D], agg_sent[k], compute_op=ALU.add)
                    if not is_last(i, k, 2):
                        get(i + 1, k)

                after_nodes(pool, l - 1)
                if l == 1:
                    after_zeroing(pool)
                get(0, 0)
                get(0, 1)
                groups(pool, body)

            for l in (1, 2, 3):
                edges(l)
                after_edges(pool, l)
                if l == 2:
                    pool.wait_ge(nodes_in, 16 * 4)
                nodes(l)

        @block.scalar
        def _(act):
            copy = nc.scalar.copy

            def turned_x(i, s, n):
                for m, c in enumerate(STEPS[n == TAIL]):
                    step = (2 * i + s) * len(STEPS[0]) + m
                    rows, wide = sizes(n, c)
                    act.wait_ge(turned, step + 1)
                    wait(act, mixed, step - 1)
                    copy(xT[m % 2][0:rows, 0:wide], psum[0:rows, m % 2, 0:wide]).then_inc(turned_sb, 1)

            act.wait_ge(setup, 1)

            def stage_dst(i, k):
                copy(dst_at[k][:, :], dst_row[:, ds((2 * i + k) * G, G)]).then_inc(dst_rows_at, 1)

            def stage_keys(i, k, key, done):
                copy(key_at[k][:, :], key[:, ds((2 * i + k) * G, G)]).then_inc(done, 1)

            def stage_src(i, k, done):
                copy(src_at[k][:, :], src_row[:, ds((2 * i + k) * G, G)]).then_inc(done, 1)

            for k in range(2):
                stage_dst(0, k)
                stage_keys(0, k, src_key, keys_at)
                stage_src(0, k, rows_at)
            chunks(act, turned_x)

            def ahead0(i, k):
                g = 2 * i + k
                act.wait_ge(z_turned, g + 1)
                wait(act, y_ready, g)
                copy(zt_a, bank(2))
                copy(zt_b[0:D, :], psum[0:D, 3, :]).then_inc(z_turned_sb, 1)

            def same0(i, k):
                g = 2 * i + k
                act.wait_ge(apart_ready, g + 1)
                wait(act, sum_ready, g - 1)
                for a in range(G):
                    last = nc.scalar.activation(same[k][:, a, 0:(a + 1) * P], apart[:, a, 0:(a + 1) * P],
                                                ACT.Identity, bias=one[:, 0:1], scale=-1.0 / NEG_BIG)
                last.then_inc(same_ready, 1)

            def body0(i, k):
                g = 2 * i + k
                if not is_last(i, k, 2):
                    act.wait_ge(z_ready, g + 1)
                    act.wait_ge(apart_ready, g + 1)
                    act.wait_ge(key_row, g + 1)
                    stage_dst(i + 1, k)
                    stage_keys(i + 1, k, src_key, keys_at)
                if not is_last(i, k, 1):
                    ahead0(i + k, 1 - k)
                act.wait_ge(expo_in, g + 1)
                nc.scalar.activation(expo[k][:, :, :], expo[k][:, :, :], ACT.Exp).then_inc(expo_out, 1)
                if not is_last(i, k, 2):
                    stage_src(i + 1, k, rows_at)
                if not is_last(i, k, 1):
                    same0(i + k, 1 - k)

            after_initial(act)
            ahead0(0, 0)
            same0(0, 0)
            groups(act, body0)

            def nodes(l):
                def body(i, s, n):
                    q = in_layer(l, i, s)
                    if l == 0:
                        act.wait_ge(n_expo_in, 2 * i + s + 1)
                        v = small[:, s, 0:2, 0:n]
                        nc.scalar.activation(v, v, ACT.Exp).then_inc(n_expo_out, 1)
                    if l == 1:
                        act_mlp(i, s, n)
                    act.wait_ge(n_centred, q + 1)
                    wait(act, n_rstd, q)
                    nc.scalar.activation(sq[:, 0:n, :], y[s][:, 0:n, :], ACT.Square, scale=D ** -0.5).then_inc(n_squared, 1)
                    act.wait_ge(n_var, q + 1)
                    nc.scalar.activation(small[:, s, 7, 0:n], small[:, s, 6, 0:n], ACT.Sqrt,
                                         bias=ln_eps[:, 0:1]).then_inc(n_std, 1)

                def act_mlp(i, s, n):
                    for m, c in enumerate(STEPS[n == TAIL]):
                        step = (2 * i + s) * len(STEPS[0]) + m
                        rows, wide = sizes(n, c)
                        act.wait_ge(m_turned, step + 1)
                        wait(act, m_hid, step - 1)
                        copy(xT[m % 2][0:rows, 0:wide], psum[0:rows, m % 2, 0:wide]).then_inc(m_turned_sb, 1)
                        act.wait_ge(m_hid, step + 1)
                        wait(act, m_out, step)
                        nc.scalar.activation(hT[0:rows, 0:wide], psum[0:rows, 2, 0:wide], ACT.Relu,
                                             bias=b1[0:rows, 0:1]).then_inc(m_hid_sb, 1)
                        act.wait_ge(m_out, step + 1)
                        wait(act, m_back, step)
                        nc.scalar.activation(oT[0:rows, 0:wide], psum[0:rows, 3, 0:wide], ACT.Relu,
                                             bias=b2[0:rows, 0:1]).then_inc(m_out_sb, 1)
                chunks(act, body)

            after_states(act)
            nodes(0)

            def edges(l):
                def prepare(i, k):
                    stage_src(i, k, g_rows_at)
                    stage_keys(i, k, dst_key, g_keys_at)

                def body(i, k):
                    g = (l - 1) * NG + 2 * i + k
                    act.wait_ge(g_got[k], 16 * G * ((l - 1) * (NG // 2) + i + 1))
                    if not is_last(i, k, 2):
                        act.wait_ge(g_key_row, g + 1)
                        act.wait_ge(g_same, g + 1)
                        prepare(i + 1, k)
                    if l == 1:
                        act.wait_ge(g_sent_in, g + 1)
                        wait(act, g_sum, g - 1)
                        nc.scalar.activation(val[k][:, :, 0:D], xg[k][:, :, :], ACT.Relu).then_inc(g_relu, 1)
                    wait(act, agg_sent[k], 16 * G * ((l - 1) * (NG // 2) + i))
                    if l > 1:
                        copy(first_at[k][:, :], dst_first[:, ds((2 * i + k) * G, G)]).then_inc(g_firsts_at, 1)
                    act.wait_ge(g_sum, g + 1)
                    w = AW if l == 1 else D
                    copy(sums[k][:, :, 0:w], bank(6 + k, G * w).rearrange("p (t w) -> p t w", w=w)).then_inc(g_sum_sb, 1)

                after_nodes(act, l - 1)
                prepare(0, 0)
                prepare(0, 1)
                groups(act, body)

            for l in (1, 2, 3):
                edges(l)
                after_edges(act, l)
                nodes(l)

        @block.tensor
        def _(pe):
            pe.wait_ge(pool_consts, 2)
            pe.wait_ge(setup, 2)

            def body_x(i, s, n):
                pe.wait_ge(x_in[s], x_loaded(i, s))
                for m, c in enumerate(STEPS[n == TAIL]):
                    step = (2 * i + s) * len(STEPS[0]) + m
                    rows, wide = sizes(n, c)
                    wait(pe, turned_sb, step - 1)
                    for b in range(0, wide, P):
                        last = nc.tensor.transpose(psum[0:rows, m % 2, b:b + P],
                                                   y[s].rearrange("p c w -> p (c w)")[:, c * D + b:c * D + b + rows],
                                                   ident[:, :])
                    last.then_inc(turned, 1)
                    pe.wait_ge(turned_sb, step + 1)
                    wait(pe, unmixed, step - 1)
                    for b in range(0, wide, P):
                        o = psum[:, 2 + m % 2, b // P * (P + B):(b // P + 1) * (P + B)]
                        last = nc.tensor.matmul(o, xT[m % 2][0:rows, b:b + P], root[0:rows, :], start=True, stop=True)
                    last.then_inc(mixed, 1)

            chunks(pe, body_x)

            def rows_of(to, column):
                for t in range(G):
                    last = nc.tensor.transpose(to[:, t * P:(t + 1) * P], column[:, t:t + 1].to_broadcast([P, P]),
                                               ident[:, :])
                return last

            def turn0(i, k):
                g = 2 * i + k
                pe.wait_ge(keys_at, g + 1)
                wait(pe, apart_ready, g)
                rows_of(bank(0), key_at[k]).then_inc(key_row, 1)
                pe.wait_ge(z_ready, g + 1)
                wait(pe, z_turned_sb, g)
                for t in range(G):
                    nc.tensor.transpose(psum[:, 2, t * P:(t + 1) * P],
                                        z[:, t, 0:B, :].rearrange("p k d -> p (k d)"), ident[:, :])
                    last = nc.tensor.transpose(psum[0:D, 3, t * P:(t + 1) * P], z[:, t, B, :], ident[:, :])
                last.then_inc(z_turned, 1)

            def spline0(i, k):
                g = 2 * i + k
                pe.wait_ge(z_turned_sb, g + 1)
                wait(pe, y_used, g)
                for t in range(G):
                    o = psum[:, 4 + t // 2, t % 2 * K * D:(t % 2 + 1) * K * D]
                    nc.tensor.matmul(o, zt_a[:, t * P:(t + 1) * P], w_a[:, :, :].rearrange("p j o -> p (j o)"),
                                     start=True, stop=False)
                    last = nc.tensor.matmul(o, zt_b[0:D, t * P:(t + 1) * P],
                                            w_b[:, :, :].rearrange("p j o -> p (j o)"), start=False, stop=True)
                last.then_inc(y_ready, 1)

            def logits0(i, k):
                g = 2 * i + k
                pe.wait_ge(t_ready, g + 1)
                wait(pe, max_ready, g)
                rows_of(bank(1), tmax[k][:, 0, :]).then_inc(t_row, 1)

            def sum_shared(k, v, w, done):
                for a in range(G):
                    for b in range(a, G):
                        last = nc.tensor.matmul(psum[:, 6 + k, a * w:(a + 1) * w], same[k][:, b, a * P:(a + 1) * P],
                                                v[:, b, 0:w], start=(b == a), stop=(b == G - 1))
                last.then_inc(done, 1)

            def body0(i, k):
                g = 2 * i + k
                ahead = not is_last(i, k, 1)
                if ahead:
                    turn0(i + k, 1 - k)
                    spline0(i + k, 1 - k)
                pe.wait_ge(val_ready, g + 1)
                pe.wait_ge(same_ready, g + 1)
                wait(pe, st_ready, g - 1)
                sum_shared(k, val[k], AW, sum_ready)
                if ahead:
                    logits0(i + k, 1 - k)

            after_initial(pe)
            turn0(0, 0)
            spline0(0, 0)
            logits0(0, 0)
            groups(pe, body0)

            def edges(l):
                def prepare(i, k):
                    g = (l - 1) * NG + 2 * i + k
                    pe.wait_ge(g_keys_at, g + 1)
                    wait(pe, g_same, g - 1)
                    rows_of(bank(k), key_at[k]).then_inc(g_key_row, 1)

                def body(i, k):
                    g = (l - 1) * NG + 2 * i + k
                    if not is_last(i, k, 1):
                        prepare(i + k, 1 - k)
                    pe.wait_ge(g_same, g + 1)
                    if l == 1:
                        pe.wait_ge(g_relu, g + 1)
                    else:
                        pe.wait_ge(g_got[k], 16 * G * ((l - 1) * (NG // 2) + i + 1))
                    wait(pe, g_sum_sb, g - 1)
                    sum_shared(k, val[k] if l == 1 else xg[k], AW if l == 1 else D, g_sum)

                after_nodes(pe, l - 1)
                prepare(0, 0)
                groups(pe, body)

            def mlp(i, s, n):
                for m, c in enumerate(STEPS[n == TAIL]):
                    step = (2 * i + s) * len(STEPS[0]) + m
                    rows, wide = sizes(n, c)
                    if m == 0:
                        pe.wait_ge(m_h, 2 * i + s + 1)
                    wait(pe, m_turned_sb, step - 1)
                    for b in range(0, wide, P):
                        last = nc.tensor.transpose(psum[0:rows, m % 2, b:b + P],
                                                   y[s].rearrange("p c w -> p (c w)")[:, c * D + b:c * D + b + rows],
                                                   ident[:, :])
                    last.then_inc(m_turned, 1)
                    pe.wait_ge(m_turned_sb, step + 1)
                    wait(pe, m_hid_sb, step)
                    nc.tensor.matmul(psum[0:rows, 2, 0:wide], w1[0:rows, 0:rows], xT[m % 2][0:rows, 0:wide],
                                     start=True, stop=True).then_inc(m_hid, 1)
                    pe.wait_ge(m_hid_sb, step + 1)
                    wait(pe, m_out_sb, step)
                    nc.tensor.matmul(psum[0:rows, 3, 0:wide], w2[0:rows, 0:rows], hT[0:rows, 0:wide],
                                     start=True, stop=True).then_inc(m_out, 1)
                    pe.wait_ge(m_out_sb, step + 1)
                    wait(pe, m_back_used, step - 1)
                    for b in range(0, wide, P):
                        last = nc.tensor.transpose(psum[:, 4 + m % 2, b:b + rows], oT[0:rows, b:b + P],
                                                   ident[0:rows, 0:rows])
                    last.then_inc(m_back, 1)

            for l in (1, 2, 3):
                edges(l)
                if l == 1:
                    after_edges(pe, 1)
                    chunks(pe, mlp)

        @block.vector
        def _(dve):
            v = nc.vector
            begin = Chain(dve, setup_steps, 0)

            def link(ins):
                begin.step(ins)
                begin.wait()

            v.memset(src_row[:, MAIN:TILES], -1)
            v.memset(dst_row[:, MAIN:TILES], -1)
            for t in (root, w1, w2):
                v.memset(t[:, :], 0.0)
            v.memset(cj[P - 32:P, LASTP:COLS], 0.0)
            v.memset(ci[P - 32:P, LASTP:COLS], 0.0)
            v.memset(attr2[:, MAIN:TILES, :], 0.0).then_inc(cleared, 1)
            dve.wait_ge(edges_in, 16 * 6)
            dve.wait_ge(pool_consts, 2)
            for row, key in ((src_row, src_key), (dst_row, dst_key)):
                v.tensor_copy(key[:, :], row[:, :])
            link(v.tensor_copy(spare[:, :], spare_i[:, :]))
            for row, key in ((src_row, src_key), (dst_row, dst_key)):
                v.tensor_scalar(row[:, :], key[:, :], 0.0, None, ALU.max)
            v.memset(one[:, :], 1.0)
            v.memset(ln_eps[:, :], LN_EPS)
            link(v.memset(zeros, 0.0))
            for key, rel in ((src_key, src_rel), (dst_key, dst_rel)):
                link(v.tensor_tensor(rel[:, :].rearrange("p (n t) -> p n t", t=G),
                                     key[:, :].rearrange("p (n t) -> p n t", t=G),
                                     spare[:, :].unsqueeze(1).to_broadcast([P, NG, G]), ALU.subtract))
                link(v.scalar_tensor_tensor(out=rel[:, :], in0=key[:, :], scalar=0.0, in1=rel[:, :],
                                            op0=ALU.is_ge, op1=ALU.mult))
            dve.sem_inc(setup, 1)
            dve.wait_ge(consts_in, 16 * (5 * B + K + 4))
            link(v.tensor_tensor(scratch[:, :, :], root[:, 0:P].rearrange("p (a b) -> p a b", a=B),
                                 att1[:, :].unsqueeze(1).to_broadcast([P, B, D]), ALU.mult))
            link(v.tensor_reduce(root[:, P:P + B], scratch[:, :, :], AX_X, ALU.add))
            link(v.tensor_tensor(root[:, 0:P], root[:, 0:P], ident[:, :], ALU.add))
            link(v.tensor_scalar(eps1[:, :], eps1[:, :], 1.0, None, ALU.add))
            for s in range(2):
                link(v.memset(node_in[s][0], 0.0))
                link(v.memset(node_in[s][0][:, :, 1], NEG_BIG))
            dve.sem_inc(setup, 1)

            def root_body(i, s, n):
                wait(dve, init_stored[s], 32 * i)
                for m, c in enumerate(STEPS[n == TAIL]):
                    step = (2 * i + s) * len(STEPS[0]) + m
                    w = min(STEP, n - c)
                    nb, per = -(-w // B), min(B, w)
                    dve.wait_ge(mixed, step + 1)
                    o = psum[:, 2 + m % 2, 0:nb * (P + B)].rearrange("p (b f) -> p b f", f=P + B)
                    v.tensor_tensor(
                        xs[:, ds(cols(i, s) + c, w), :].rearrange("p (b a) d -> p b a d", b=nb),
                        o[:, :, 0:per * D].rearrange("p b (a d) -> p b a d", d=D),
                        bias_b[:, :].unsqueeze(1).unsqueeze(1).to_broadcast([P, nb, per, D]), ALU.add)
                    v.tensor_copy(node_in[s][0][:, c:c + w, 0].rearrange("p (b a) -> p b a", b=nb),
                                  o[:, :, P:P + per]).then_inc(unmixed, 1)
                dve.wait_ge(unmixed, step + 1)
                dve.sem_inc(rooted, 1)

            chunks(dve, root_body)

            p4 = attr2[:, :, :]
            link(v.tensor_scalar(p4, p4, float(K - 1), 0.0, ALU.mult, ALU.max))
            link(v.tensor_scalar(p4, p4, float(K - 1), None, ALU.min))
            up = zt_a[:, 0:TILES]
            for d in range(2):
                for n in range(K):
                    link(v.tensor_scalar(up, attr2[:, :, d], -1.0, float(n + 1), ALU.mult, ALU.add))
                    link(v.tensor_scalar(hat[d][:, :, n], attr2[:, :, d], float(1 - n), None, ALU.add))
                    link(v.tensor_tensor(hat[d][:, :, n], hat[d][:, :, n], up, ALU.min))
                link(v.tensor_scalar(hat[d][:, :, :], hat[d][:, :, :], 0.0, None, ALU.max))

            c = Chain(dve, e0, 0)

            def first_edges(k, rel, to, done):
                c.step(v.scalar_tensor_tensor(out=count[k][:, :], in0=count[k][:, :], scalar=0.0, in1=rel,
                                              op0=ALU.is_equal, op1=ALU.mult))
                c.wait()
                for t in to[1:]:
                    v.tensor_tensor(t, count[k][:, :], spare[:, :], ALU.add)
                v.tensor_tensor(to[0], count[k][:, :], spare[:, :], ALU.add).then_inc(done, 1)

            def count_earlier(k):
                for a in range(G):
                    w = (a + 1) * P
                    at = a * (a + 1) // 2 * P
                    last = v.tensor_tensor_reduce(out=junk[:, at:at + w], in0=same[k][:, a, 0:w],
                                                  in1=earlier[:, ROW - w:ROW], scale=1.0, scalar=0.0,
                                                  op0=ALU.mult, op1=ALU.add, accum_out=count[k][:, a:a + 1])
                c.step(last)

            def knots0(i, k):
                g = 2 * i + k
                dve.wait_ge(x_got[k], 16 * G * (i + 1))
                wait(dve, z_turned, g)
                h = hat[0][:, ds(g * G, G), :]
                v.tensor_tensor(z, xg[k][:, :, :].unsqueeze(2).to_broadcast([P, G, K, D]),
                                h.unsqueeze(3).to_broadcast([P, G, K, D]), ALU.mult).then_inc(z_ready, 1)

            def apart0(i, k):
                g = 2 * i + k
                dve.wait_ge(key_row, g + 1)
                wait(dve, same_ready, g)
                for a in range(G):
                    last = v.tensor_scalar(apart[:, a, :], bank(0), key_at[k][:, a:a + 1], NEG_BIG,
                                           ALU.not_equal, ALU.mult)
                last.then_inc(apart_ready, 1)

            def earlier0(i, k):
                dve.wait_ge(same_ready, 2 * i + k + 1)
                count_earlier(k)

            def message0(i, k):
                g = 2 * i + k
                dve.wait_ge(y_ready, g + 1)
                h = hat[1][:, ds(g * G, G), :]
                for b in range(2):
                    last = v.tensor_tensor(
                        ty[:, 2 * b:2 * b + 2, :, :],
                        psum[:, 4 + b, 0:2 * K * D].rearrange("p (t j o) -> p t j o", t=2, j=K),
                        h[:, 2 * b:2 * b + 2, :].unsqueeze(3).to_broadcast([P, 2, K, D]), ALU.mult)
                last.then_inc(y_used, 1)
                dve.wait_ge(y_used, g + 1)
                c.step(v.tensor_reduce(msg[k][:, :, :], ty.rearrange("p t j o -> p t o j"), AX_X, ALU.add))
                c.wait()
                c.step(v.tensor_tensor(lw, msg[k][:, :, :], att2[:, :].unsqueeze(1).to_broadcast([P, G, D]), ALU.mult))
                c.wait()
                v.tensor_reduce(tmax[k][:, 0, :], lw, AX_X, ALU.add).then_inc(t_ready, 1)

            def first0(i, k):
                wait(dve, st_sent[k], 16 * G * i)
                dve.wait_ge(t_row, 2 * i + k + 1)
                first_edges(k, src_rel[:, ds((2 * i + k) * G, G)], [first_at[k][:, :]], first_ready)

            def max0(i, k):
                for a in range(G):
                    last = v.tensor_tensor_reduce(out=apart[:, a, :], in0=apart[:, a, :], in1=bank(1), scale=1.0,
                                                  scalar=NEG_BIG, op0=ALU.add, op1=ALU.max,
                                                  accum_out=tmax[k][:, 1, a:a + 1])
                last.then_inc(max_ready, 1)

            def body0(i, k):
                g = 2 * i + k
                ahead = not is_last(i, k, 1)
                j, o = i + k, 1 - k
                c.body(g)
                if ahead:
                    knots0(j, o)
                dve.wait_ge(st_got[k], 16 * G * (i + 1))
                dve.wait_ge(max_ready, g + 1)
                u = tmax[k][:, :, :]
                old_max, new_max = st[k][:, :, 1], st_new[k][:, :, 1]
                c.step(v.tensor_tensor(u, u, st[k][:, :, 0].unsqueeze(1).to_broadcast([P, 2, G]), ALU.add))
                c.wait()
                c.step(v.scalar_tensor_tensor(out=u, in0=u, scalar=SLOPE, in1=u, op0=ALU.mult, op1=ALU.max))
                c.wait()
                c.step(v.tensor_tensor(new_max, u[:, 1, :], old_max, ALU.max))
                v.tensor_copy(st_new[k][:, :, 0], st[k][:, :, 0])
                c.wait()
                v.tensor_tensor(expo[k][:, 0, :], u[:, 0, :], new_max, ALU.subtract)
                v.tensor_tensor(expo[k][:, 1, :], old_max, new_max, ALU.subtract).then_inc(expo_in, 1)
                if ahead:
                    dve.wait_ge(max_ready, g + 1)
                    apart0(j, o)
                dve.wait_ge(expo_out, g + 1)
                wait(dve, sum_ready, g - 1)
                v.tensor_tensor(val[k][:, :, 0:D], msg[k][:, :, :],
                                expo[k][:, 0, :].unsqueeze(2).to_broadcast([P, G, D]), ALU.mult)
                v.tensor_copy(val[k][:, :, D], expo[k][:, 0, :]).then_inc(val_ready, 1)
                c.step(v.tensor_tensor(st_new[k][:, :, 2:SW], st[k][:, :, 2:SW],
                                       expo[k][:, 1, :].unsqueeze(2).to_broadcast([P, G, AW]), ALU.mult))
                if ahead:
                    earlier0(j, o)
                dve.wait_ge(sum_ready, g + 1)
                c.wait()
                v.tensor_tensor(st_new[k][:, :, 2:SW], st_new[k][:, :, 2:SW],
                                bank(6 + k, G * AW).rearrange("p (t w) -> p t w", w=AW), ALU.add).then_inc(st_ready, 1)
                if ahead:
                    message0(j, o)
                    first0(j, o)
                    max0(j, o)

            after_initial(dve)
            c.per = 0
            knots0(0, 0)
            apart0(0, 0)
            earlier0(0, 0)
            message0(0, 0)
            c.wait()
            first0(0, 0)
            max0(0, 0)
            c.first, c.per = c.n, E0_STEPS
            groups(dve, body0)

            def nodes(l):
                c = Chain(dve, n_steps[l], N_STEPS[l])

                def body(i, s, n):
                    c.body(2 * i + s)
                    q = in_layer(l, i, s)
                    sm = lambda j: small[:, s, j, 0:n]
                    wide = lambda a: a.unsqueeze(2).to_broadcast([P, n, D])
                    x_now = xs[:, ds(cols(i, s), n), :]
                    yy = y[s][:, 0:n, :]
                    if l != 2:
                        wait(dve, n_done, q - 1)
                    if l < 2:
                        dve.wait_ge(n_in[s], loaded(l, i, s))
                    if l == 0:
                        a, b = (t[:, 0:n, :] for t in node_in[s])
                        c.step(v.tensor_tensor(sm(2), a[:, :, 1], b[:, :, 1], ALU.max))
                        c.wait()
                        v.tensor_tensor(sm(0), a[:, :, 1], sm(2), ALU.subtract)
                        v.tensor_tensor(sm(1), b[:, :, 1], sm(2), ALU.subtract).then_inc(n_expo_in, 1)
                        dve.wait_ge(n_expo_out, 2 * i + s + 1)
                        v.tensor_tensor(sm(5), a[:, :, 2 + D], sm(0), ALU.mult)
                        c.step(v.tensor_tensor(sm(6), b[:, :, 2 + D], sm(1), ALU.mult))
                        c.wait()
                        c.step(v.tensor_tensor(sm(2), sm(5), sm(6), ALU.add))
                        c.wait()
                        c.step(v.tensor_scalar(sm(2), sm(2), DEN_EPS, None, ALU.add))
                        c.wait()
                        c.step(v.reciprocal(sm(2), sm(2)))
                        c.wait()
                        v.tensor_tensor(sm(3), sm(1), sm(2), ALU.mult).then_inc(n_share, 1)
                        c.step(v.tensor_tensor(sm(4), sm(0), sm(2), ALU.mult))
                        c.wait()
                        c.step(v.tensor_tensor(a[:, :, 2:2 + D], a[:, :, 2:2 + D], wide(sm(4)), ALU.mult))
                        c.wait()
                        c.step(v.tensor_tensor(yy, a[:, :, 2:2 + D], x_now, ALU.add))
                        c.wait()
                        dve.wait_ge(n_scaled, 2 * i + s + 1)
                        c.step(v.tensor_tensor(yy, yy, b[:, :, 2:2 + D], ALU.add))
                    elif l == 1:
                        a = node_in[s][0].rearrange("p c w -> p (c w)")[:, 0:n * AW].rearrange("p (c w) -> p c w", w=AW)
                        v.tensor_copy(deg[:, ds(cols(i, s), n)], a[:, :, D])
                        v.scalar_tensor_tensor(out=yy, in0=x_now, scalar=eps1[:, 0:1], in1=a[:, :, 0:D],
                                               op0=ALU.mult, op1=ALU.add).then_inc(m_h, 1)
                        for m, c0 in enumerate(STEPS[n == TAIL]):
                            step = (2 * i + s) * len(STEPS[0]) + m
                            w = min(STEP, n - c0)
                            dve.wait_ge(m_back, step + 1)
                            ins = v.tensor_tensor(
                                y[s][:, c0:c0 + w, :], psum[:, 4 + m % 2, 0:w * D].rearrange("p (c d) -> p c d", d=D),
                                xs[:, ds(cols(i, s) + c0, w), :], ALU.add)
                            ins.then_inc(m_back_used, 1)
                        dve.wait_ge(m_back_used, step + 1)
                    else:
                        a = node_in[s][0].rearrange("p c w -> p (c w)")[:, 0:n * D].rearrange("p (c w) -> p c w", w=D)
                        dve.wait_ge(n_scaled, (l - 1) * (CHUNKS + 1) + 2 * i + s + 1)
                        c.step(v.tensor_tensor(yy, a, x_now, ALU.add))
                    if l != 1:
                        c.wait()
                    c.step(v.tensor_reduce(sm(5), yy, AX_X, ALU.add))
                    c.wait()
                    c.step(v.tensor_scalar(sm(5), sm(5), 1.0 / D, None, ALU.mult))
                    c.wait()
                    v.tensor_tensor(yy, yy, wide(sm(5)), ALU.subtract).then_inc(n_centred, 1)
                    dve.wait_ge(n_squared, q + 1)
                    v.tensor_reduce(sm(6), sq[:, 0:n, :], AX_X, ALU.add).then_inc(n_var, 1)
                    dve.wait_ge(n_std, q + 1)
                    v.reciprocal(sm(7), sm(7)).then_inc(n_rstd, 1)
                    if l == 2:
                        dve.wait_ge(n_rstd, q + 1)
                        v.tensor_tensor(x_now, yy, wide(sm(7)), ALU.mult).then_inc(n_done, 1)
                    assert c.n == N_STEPS[l]

                chunks(dve, body)

            after_states(dve)
            nodes(0)
            for k in range(2):
                v.memset(val[k][:, :, D], 1.0)

            def edges(l):
                nonlocal c
                c = Chain(dve, ge[l], 2)

                def body(i, k):
                    c.body(2 * i + k)
                    g = (l - 1) * NG + 2 * i + k
                    dve.wait_ge(g_key_row, g + 1)
                    wait(dve, g_sum, g - 1)
                    for a in range(G):
                        w = (a + 1) * P
                        last = v.tensor_scalar(same[k][:, a, 0:w], bank(k)[:, 0:w], key_at[k][:, a:a + 1], None,
                                               ALU.is_equal)
                    last.then_inc(g_same, 1)
                    if l == 1:
                        dve.wait_ge(attr_in[k], attr_loaded(i, k))
                        dve.wait_ge(g_got[k], 16 * G * (i + 1))
                        v.tensor_tensor(xg[k][:, :, :], xg[k][:, :, :], attr[k][:, :, :], ALU.add).then_inc(g_sent_in, 1)
                        dve.wait_ge(g_same, g + 1)
                        count_earlier(k)
                        c.wait()
                        wait(dve, agg_sent[k], 16 * G * i)
                        cs = ds((2 * i + k) * G, G)
                        first_edges(k, dst_rel[:, cs], [first_at[k][:, :], dst_first[:, cs]], g_firsts_at)

                after_nodes(dve, l - 1)
                groups(dve, body)

            for l in (1, 2, 3):
                edges(l)
                after_edges(dve, l)
                nodes(l)
                if l == 1:
                    after_nodes(dve, 1)
                    link(v.tensor_scalar(deg[:, :], deg[:, :], 1.0, None, ALU.max))
                    v.reciprocal(deg[:, :], deg[:, :]).then_inc(n_share, 1)


_INS = ['x', 'src', 'dst', 'edge_attr_2', 'edge_attr_32', 'node_vec1', 'node_vec1_n2', 'L0_gnn_weight',
        'L0_gnn_root_weight', 'L0_gnn_att_weight', 'L0_gnn_bias', 'L1_gnn_eps', 'L1_gnn_W1', 'L1_gnn_b1',
        'L1_gnn_W2', 'L1_gnn_b2']
_OUTS = [((100000, 32), 'float32')]


def kernel(**inputs):
    import numpy as _np
    import concourse.bacc as _bacc
    from concourse import mybir as _mybir
    from concourse.bass_utils import run_bass_kernel_spmd as _run

    nc = _bacc.Bacc("TRN2", target_bir_lowering=False, num_devices=1)
    arrays, args = {}, []
    for name in _INS:
        a = _np.ascontiguousarray(inputs[name])
        arrays[f"in_{name}_dram"] = a
        args.append(nc.dram_tensor(f"in_{name}_dram", a.shape, _mybir.dt.from_np(a.dtype), kind="ExternalInput").ap())
    for i, (shape, dtype) in enumerate(_OUTS):
        dt = _mybir.dt.from_np(_np.dtype(dtype))
        args.append(nc.dram_tensor(f"out_{i}_dram", shape, dt, kind="ExternalOutput").ap())
    gnn_program(nc, *args)
    r = _run(nc, [arrays], core_ids=[0])
    got = tuple(r.results[0][f"out_{i}_dram"] for i in range(len(_OUTS)))
    return got[0]
```

```python
from contextlib import ExitStack

import concourse.bass as bass
from concourse import mybir


F32 = mybir.dt.float32
I32 = mybir.dt.int32
ALU = mybir.AluOpType
ACT = mybir.ActivationFunctionType
AX_X = mybir.AxisListType.X

P = 128
G = 4
ROW = G * P
NEG_BIG = -2.0 ** 126
SLOPE = 0.2
LN_EPS = 1e-5
DEN_EPS = 1e-16


def ds(start, size):
    return bass.ds(start, size)


def wait(eng, sem, value):
    if not (isinstance(value, int) and value <= 0):
        eng.wait_ge(sem, value)


class Chain:

    def __init__(self, eng, sem, per, first=0):
        self.eng, self.sem, self.per, self.first = eng, sem, per, first
        self.base, self.n = first, 0

    def body(self, number):
        self.base, self.n = self.first + number * self.per, 0

    def step(self, ins):
        ins.then_inc(self.sem, 1)
        self.n += 1

    def wait(self, n=None):
        self.eng.wait_ge(self.sem, self.base + (self.n if n is None else n))


def gnn_program(nc, x, src, dst, edge_attr_2, edge_attr_32, node_vec1, node_vec1_n2,
                spline_w, root_w, att_w, bias, gine_eps, gine_w1, gine_b1, gine_w2, gine_b2, out):
    N, D = x.shape
    E = src.shape[0]
    K = 5
    LAST = gine_eps.shape[0] - 1
    assert P % D == 0 and spline_w.shape[0] == K * K
    B = P // D

    COLS = -(-N // P)
    NT = COLS * P
    LASTP = N - (P - 1) * COLS
    HEAD = 112
    STEP = 3 * B
    CH = 4 * STEP
    CHUNKS = COLS // CH
    TAIL = COLS - CHUNKS * CH
    assert CHUNKS % 2 == 0 and 0 < TAIL < CH
    HALF = CHUNKS // 2
    STEPS = [list(range(0, CH, STEP)), list(range(0, TAIL, STEP))]
    NSTEP = CHUNKS * len(STEPS[0]) + len(STEPS[1])
    SLOT_USES = (HALF + 1, HALF)

    MAIN = E // P
    REST = E - MAIN * P
    TILES = -(-(MAIN + 1) // (2 * G)) * 2 * G
    NG = TILES // G
    assert TILES > MAIN + 1 - (REST == 0) and MAIN % G == 2

    TRASH = NT
    RT = NT + ROW
    SW = D + 3
    AW = D + 1

    def dram(name, rows, width):
        return nc.dram_tensor(name, (rows, width), F32).ap()

    state = [dram("state_even", RT, SW), dram("state_odd", RT, SW)]
    agg = [None, dram("agg_1", RT, AW), dram("agg_2", RT, D), dram("agg_3", RT, D)]
    xt = [x, dram("x_1", NT, D), dram("x_2", NT, D), dram("x_3", NT, D)]

    with ExitStack() as ctx:
        def sb(name, shape, dt=F32):
            return ctx.enter_context(nc.sbuf_tensor(name, shape, dt))

        def sem(name):
            return ctx.enter_context(nc.semaphore(name))

        def pair(name):
            return [sem(name + "_0"), sem(name + "_1")]

        xs = sb("xs", [P, COLS, D])
        src_row = sb("src_row", [P, TILES], I32)
        dst_row = sb("dst_row", [P, TILES], I32)
        src_key = sb("src_key", [P, TILES])
        dst_key = sb("dst_key", [P, TILES])
        src_rel = sb("src_rel", [P, TILES])
        dst_rel = sb("dst_rel", [P, TILES])
        dst_first = sb("dst_first", [P, TILES], I32)
        attr2 = sb("attr2", [P, TILES, 2])
        hat = [sb("hat0", [P, TILES, K]), sb("hat1", [P, TILES, K])]
        ident = sb("ident", [P, P])
        earlier = sb("earlier", [P, ROW])
        spare_i = sb("spare_i", [P, G], I32)
        spare = sb("spare", [P, G])
        root = sb("root", [P, P + B])
        att1 = sb("att1", [P, D])
        att2 = sb("att2", [P, D])
        bias_b = sb("bias_b", [P, D])
        w_a = sb("w_a", [P, K, D])
        w_b = sb("w_b", [D, K, D])
        w1 = sb("w1", [P, P])
        w2 = sb("w2", [P, P])
        b1 = sb("b1", [P, 1])
        b2 = sb("b2", [P, 1])
        eps1 = sb("eps1", [P, 1])
        one = sb("one", [P, 1])
        ln_eps = sb("ln_eps", [P, 1])
        cj = hat[0][:, :, :].rearrange("p t k -> p (t k)")[:, 0:COLS]
        deg = hat[0][:, :, :].rearrange("p t k -> p (t k)")[:, COLS:2 * COLS]
        ci = hat[1][:, :, :].rearrange("p t k -> p (t k)")[:, 0:COLS]

        xg = [sb(f"xg{k}", [P, G, D]) for k in range(2)]
        src_at = [sb(f"src_at{k}", [P, G], I32) for k in range(2)]
        dst_at = [sb(f"dst_at{k}", [P, G], I32) for k in range(2)]
        first_at = [sb(f"first_at{k}", [P, G], I32) for k in range(2)]
        key_at = [sb(f"key_at{k}", [P, G]) for k in range(2)]
        st = [sb(f"st{k}", [P, G, SW]) for k in range(2)]
        st_new = [sb(f"st_new{k}", [P, G, SW]) for k in range(2)]
        msg = [sb(f"msg{k}", [P, G, D]) for k in range(2)]
        val = [sb(f"val{k}", [P, G, AW]) for k in range(2)]
        tmax = [sb(f"tmax{k}", [P, 2, G]) for k in range(2)]
        expo = [sb(f"expo{k}", [P, 2, G]) for k in range(2)]
        count = [sb(f"count{k}", [P, G]) for k in range(2)]
        attr = [sb(f"attr{k}", [P, G, D]) for k in range(2)]
        sums = [sb(f"sums{k}", [P, G, AW]) for k in range(2)]

        ARENA = 15168
        arena = sb("arena", [P, ARENA])
        at = [0]

        def cut(shape, start=None):
            if start is not None:
                at[0] = start
            n = 1
            for s in shape:
                n *= s
            v = arena[:, at[0]:at[0] + n]
            at[0] += n
            assert at[0] <= ARENA
            if len(shape) == 2:
                v = v.rearrange("p (a b) -> p a b", a=shape[0])
            if len(shape) == 3:
                v = v.rearrange("p (a b c) -> p a b c", a=shape[0], b=shape[1])
            return v

        same = [cut([G, ROW], 0), cut([G, ROW])]
        apart = cut([G, ROW])
        junk = cut([sum(range(1, G + 1)) * P])
        z = cut([G, K, D])
        ty = cut([G, K, D])
        zt_a = cut([ROW])
        zt_b = cut([ROW])
        lw = cut([G, D])
        ZERO = 1048
        zeros = cut([ZERO], ARENA - ZERO)
        node_in = [[cut([CH, SW], 0), cut([CH, SW])], [cut([CH, SW]), cut([CH, SW])]]
        y = [cut([CH, D]), cut([CH, D])]
        sq = [cut([CH, D]), cut([CH, D])]
        xT, hT, oT = ([cut([STEP * D]) for _ in range(2)] for _ in range(3))
        scratch = sb("scratch", [P, B, D])
        small = sb("small", [P, 2, 8, CH])
        psum = ctx.enter_context(nc.psum_tensor("psum", [P, 8, 512], F32))

        pool_consts = sem("pool_consts")
        cleared = sem("cleared")
        factors_cleared = sem("factors_cleared")
        pool_turns, sp_turns = sem("pool_turns"), sem("sp_turns")
        edges_in, consts_in, nodes_in, last_stored = sem("edges_in"), sem("consts_in"), sem("nodes_in"), sem("last_stored")
        setup, setup_steps = sem("setup"), sem("setup_steps")
        zeroed = sem("zeroed")
        x_in = pair("x_in")
        turned, turned_sb, mixed, unmixed = sem("turned"), sem("turned_sb"), sem("mixed"), sem("unmixed")
        rooted = sem("rooted")
        init_stored = pair("init_stored")
        e0 = sem("e0_steps")
        rows_at, keys_at, dst_rows_at = sem("rows_at"), sem("keys_at"), sem("dst_rows_at")
        x_got, st_got = pair("x_got"), pair("st_got")
        z_ready, z_turned, z_turned_sb, y_ready = sem("z_ready"), sem("z_turned"), sem("z_turned_sb"), sem("y_ready")
        y_used, t_ready, t_row, max_ready = sem("y_used"), sem("t_ready"), sem("t_row"), sem("max_ready")
        key_row, apart_ready, same_ready = sem("key_row"), sem("apart_ready"), sem("same_ready")
        expo_in, expo_out, val_ready, sum_ready, st_ready = (sem("expo_in"), sem("expo_out"), sem("val_ready"),
                                                             sem("sum_ready"), sem("st_ready"))
        first_ready = sem("first_ready")
        st_sent = pair("st_sent")
        ge = [None] + [sem(f"e{l}_steps") for l in (1, 2, 3)]
        g_rows_at, g_keys_at, g_firsts_at = sem("g_rows_at"), sem("g_keys_at"), sem("g_firsts_at")
        g_got, attr_in = pair("g_got"), pair("attr_in")
        g_key_row, g_same, g_sent_in, g_relu, g_sum, g_sum_sb = (sem("g_key_row"), sem("g_same"), sem("g_sent_in"),
                                                                 sem("g_relu"), sem("g_sum"), sem("g_sum_sb"))
        agg_sent = pair("agg_sent")
        n_steps = [sem(f"n{l}_steps") for l in range(4)]
        n_in = pair("n_in")
        n_expo_in, n_expo_out, n_share, n_scaled = sem("n_expo_in"), sem("n_expo_out"), sem("n_share"), sem("n_scaled")
        n_y, n_centred, n_squared, n_rstd, n_done = (sem("n_y"), sem("n_centred"), sem("n_squared"), sem("n_rstd"),
                                                     sem("n_done"))
        n_shared = sem("n_shared")
        n_var, n_std = sem("n_var"), sem("n_std")
        n_weighted = sem("n_weighted")
        m_h, m_turned, m_turned_sb, m_hid, m_hid_sb, m_out, m_out_sb, m_back, m_back_used = (
            sem("m_h"), sem("m_turned"), sem("m_turned_sb"), sem("m_hid"), sem("m_hid_sb"), sem("m_out"),
            sem("m_out_sb"), sem("m_back"), sem("m_back_used"))
        x_stored, out_stored = pair("x_stored"), pair("out_stored")

        def table(t, width):
            return t[0:NT, :].rearrange("(p c) w -> p (c w)", p=P)

        x_head = x[0:HEAD * COLS, :].rearrange("(p c) w -> p (c w)", p=HEAD)
        x_mid = x[HEAD * COLS:(P - 1) * COLS, :].rearrange("(p c) w -> p (c w)", p=P - 1 - HEAD)
        x_last = x[(P - 1) * COLS:N, :].rearrange("(p c) w -> p (c w)", p=1)
        out_head = out[0:HEAD * COLS, :].rearrange("(p c) w -> p (c w)", p=HEAD)
        out_mid = out[HEAD * COLS:(P - 1) * COLS, :].rearrange("(p c) w -> p (c w)", p=P - 1 - HEAD)
        out_last = out[(P - 1) * COLS:N, :].rearrange("(p c) w -> p (c w)", p=1)
        xs_flat = xs[:, :, :].rearrange("p c w -> p (c w)")

        def bank(b, width=512):
            return psum[:, b, 0:width]

        def sizes(n, c):
            w = min(STEP, n - c) * D
            assert w % P == 0 or w < P
            return min(P, w), -(-w // P) * P

        def cols(i, s):
            return (2 * i + s) * CH

        def chunks(eng, body):
            body(0, 0, CH)
            body(0, 1, CH)
            with eng.Fori(1, HALF - 1) as i:
                body(i, 0, CH)
                body(i, 1, CH)
            body(HALF - 1, 0, CH)
            body(HALF - 1, 1, CH)
            body(HALF, 0, TAIL)

        def before(i, s):
            if isinstance(i, int) and 2 * i + s == 0:
                return None
            return (i, 0, CH) if s else (i - 1, 1, CH)

        def behind(i, s):
            if isinstance(i, int) and i == HALF:
                return None
            if not s:
                return (i, 1, CH)
            return (i + 1, 0, TAIL if isinstance(i, int) and i == HALF - 1 else CH)

        def steps_at(i, s, n, lag):
            per = len(STEPS[0])
            for m in range(len(STEPS[n == TAIL])):
                number = (2 * i + s) * per + m - lag
                if isinstance(number, int) and number < 0:
                    yield None
                elif m >= lag:
                    yield number, (m - lag) % 2, STEPS[0][m - lag], n
                else:
                    yield number, (m - lag) % 2, STEPS[0][m - lag], CH

        def steps_left(lag):
            for m in range(len(STEPS[1]) - lag, len(STEPS[1])):
                number = CHUNKS * len(STEPS[0]) + m
                yield (number, m % 2, STEPS[1][m], TAIL) if m >= 0 else (number, m % 2, STEPS[0][m], CH)

        def groups(eng, body):
            body(0, 0)
            body(0, 1)
            with eng.Fori(1, NG // 2 - 1) as i:
                body(i, 0)
                body(i, 1)
            body(NG // 2 - 1, 0)
            body(NG // 2 - 1, 1)

        def is_last(i, k, ahead):
            return isinstance(i, int) and 2 * i + k + ahead >= NG

        def after_zeroing(eng):
            eng.wait_ge(zeroed, 16 * 3)

        def after_initial(eng):
            for s in range(2):
                eng.wait_ge(init_stored[s], 32 * SLOT_USES[s] + 32 * (1 - s))

        def after_states(eng):
            for k in range(2):
                eng.wait_ge(st_sent[k], 16 * G * (NG // 2))

        def after_nodes(eng, l):
            for s in range(2):
                eng.wait_ge(x_stored[s], 16 * SLOT_USES[s] * (l + 1))

        def after_edges(eng, l):
            for k in range(2):
                eng.wait_ge(agg_sent[k], 16 * G * (NG // 2) * l)

        def loaded(l, i, s):
            if l == 0:
                return 32 * (i + 1)
            return 32 * SLOT_USES[s] + 16 * ((l - 1) * SLOT_USES[s] + i + 1)

        def last_cols(i, s):
            return max(0, min(CH, LASTP - (2 * i + s) * CH)) if isinstance(i, int) else CH

        assert (2 * HALF - 2) * CH <= LASTP < CHUNKS * CH

        def x_loaded(i, s):
            if not isinstance(i, int):
                return 48 * (i + 1)
            return sum(48 if last_cols(m, s) else 32 for m in range(i + 1))

        def in_layer(l, i, s):
            return l * (CHUNKS + 1) + 2 * i + s

        def attr_loaded(i, k):
            return 16 * (i + 1) + 16 * is_last(i, k, 1)

        E0_STEPS = 8
        N_STEPS = (10, 2, 3, 3)

        block = ctx.enter_context(nc.Block())

        @block.sync
        def _(sp):
            sp.wait_ge(cleared, 1)
            for row, to in ((src, src_row), (dst, dst_row)):
                sp.dma_start(to[:, 0:MAIN], row[0:MAIN * P].rearrange("(p t) -> p t", p=P)).then_inc(edges_in, 16)
                sp.dma_start(to[0:REST, MAIN:MAIN + 1],
                             row[MAIN * P:E].rearrange("(p t) -> p t", t=1)).then_inc(edges_in, 16)
            sp.dma_start(attr2[:, 0:MAIN, :].rearrange("p t a -> p (t a)"),
                         edge_attr_2[0:MAIN * P, :].rearrange("(p t) a -> p (t a)", p=P)).then_inc(edges_in, 16)
            sp.dma_start(attr2[0:REST, MAIN, :], edge_attr_2[MAIN * P:E, :]).then_inc(edges_in, 16)
            def const(to, of):
                sp.dma_start(to, of).then_inc(consts_in, 16)

            for j in range(B):
                const(root[j * D:(j + 1) * D, j * D:(j + 1) * D], root_w)
                with nc.allow_non_contiguous_dma("small transposed weights"):
                    const(w1[j * D:(j + 1) * D, j * D:(j + 1) * D], gine_w1[LAST].rearrange("o f -> f o"))
                    const(w2[j * D:(j + 1) * D, j * D:(j + 1) * D], gine_w2[LAST].rearrange("o f -> f o"))
                const(b1[j * D:(j + 1) * D, :], gine_b1[LAST].rearrange("(o a) -> o a", a=1))
                const(b2[j * D:(j + 1) * D, :], gine_b2[LAST].rearrange("(o a) -> o a", a=1))
            for i in range(K):
                to = w_a[i * D:(i + 1) * D, :, :] if i < B else w_b[:, :, :]
                const(to, spline_w.rearrange("(j i) f o -> i f j o", i=K)[i])
            const(att1[:, :], att_w[0:D].rearrange("(a o) -> a o", a=1).to_broadcast([P, D]))
            const(att2[:, :], att_w[D:2 * D].rearrange("(a o) -> a o", a=1).to_broadcast([P, D]))
            const(bias_b[:, :], bias.rearrange("(a o) -> a o", a=1).to_broadcast([P, D]))
            const(eps1[:, :], gine_eps[LAST:LAST + 1].rearrange("(a o) -> a o", a=1).to_broadcast([P, 1]))

            def load_x(i, s, n):
                wait(sp, turned, (2 * i + s - 1) * len(STEPS[0]))
                sp.sem_inc(sp_turns, 1)
                wait(sp, x_in[s], x_loaded(i - 1, s))
                c = cols(i, s) * D
                to = y[s].rearrange("p c w -> p (c w)")
                sp.dma_start(to[0:HEAD, 0:n * D], x_head[:, ds(c, n * D)]).then_inc(x_in[s], 16)
                sp.dma_start(to[HEAD:P - 1, 0:n * D], x_mid[:, ds(c, n * D)]).then_inc(x_in[s], 16)
                have = last_cols(i, s)
                if have:
                    sp.dma_start(to[P - 1:P, 0:have * D], x_last[:, ds(c, have * D)]).then_inc(x_in[s], 16)

            def store_init(i, s, n):
                sp.wait_ge(rooted, 2 * i + s + 1)
                c = cols(i, s) * SW
                for t in range(2):
                    sp.dma_start(table(state[t], SW)[:, ds(c, n * SW)],
                                 node_in[s][0][:, 0:n, :].rearrange("p c w -> p (c w)")).then_inc(init_stored[s], 16)
                    if n == TAIL:
                        sp.dma_start(state[t][NT:RT, :].rearrange("(p c) w -> p (c w)", p=P),
                                     node_in[s][0][:, 0:G, :].rearrange("p c w -> p (c w)")).then_inc(init_stored[s], 16)

            def load_and_store(i, s, n):
                load_x(i, s, n)
                store_init(i - 1, s, CH)

            load_x(0, 0, CH)
            load_x(0, 1, CH)
            with sp.Fori(1, HALF - 1) as i:
                load_and_store(i, 0, CH)
                load_and_store(i, 1, CH)
            load_and_store(HALF - 1, 0, CH)
            load_and_store(HALF - 1, 1, CH)
            load_and_store(HALF, 0, TAIL)
            store_init(HALF - 1, 1, CH)
            store_init(HALF, 0, TAIL)
            def load_attr(i, k):
                wait(sp, g_relu, 2 * i + k - 1)
                if isinstance(i, int) and (2 * i + k + 1) * G > MAIN:
                    left = MAIN - (2 * i + k) * G
                    sp.dma_start(attr[k][:, 0:left, :], edge_attr_32[0:MAIN * P, :].rearrange(
                        "(p t) w -> p t w", p=P)[:, MAIN - left:MAIN, :]).then_inc(attr_in[k], 16)
                    sp.dma_start(attr[k][0:REST, left, :], edge_attr_32[MAIN * P:E, :]).then_inc(attr_in[k], 16)
                    return
                sp.dma_start(attr[k][:, :, :].rearrange("p t w -> p (t w)"),
                             edge_attr_32[0:MAIN * P, :].rearrange("(p t) w -> p (t w)", p=P)[
                                 :, ds((2 * i + k) * (G * D), G * D)]).then_inc(attr_in[k], 16)

            def load_nodes(l):
                def body(i, s, n):
                    if l == 1:
                        wait(sp, m_h, 2 * i + s - 1)
                    else:
                        wait(sp, n_centred, in_layer(l, i, s) - 1)
                    if l == 0:
                        c = cols(i, s) * SW
                        for t in range(2):
                            sp.dma_start(node_in[s][t][:, 0:n, :].rearrange("p c w -> p (c w)"),
                                         table(state[t], SW)[:, ds(c, n * SW)]).then_inc(n_in[s], 16)
                    else:
                        w = AW if l == 1 else D
                        sp.dma_start(node_in[s][0].rearrange("p c w -> p (c w)")[:, 0:n * w],
                                     table(agg[l], w)[:, ds(cols(i, s) * w, n * w)]).then_inc(n_in[s], 16)
                return body

            def store_nodes(l, i, s, n):
                c = cols(i, s) * D
                if l == 2:
                    sp.wait_ge(n_weighted, 2 * i + s + 1)
                    sp.dma_start(table(xt[3], D)[:, ds(c, n * D)],
                                 node_in[s][1].rearrange("p c w -> p (c w)")[:, 0:n * D]).then_inc(x_stored[s], 16)
                    return
                sp.wait_ge(n_done, in_layer(l, i, s) + 1)
                if l < 3:
                    sp.dma_start(table(xt[l + 1], D)[:, ds(c, n * D)], xs_flat[:, ds(c, n * D)]).then_inc(x_stored[s], 16)
                else:
                    sp.dma_start(out_head[:, ds(c, n * D)], xs_flat[0:HEAD, ds(c, n * D)]).then_inc(out_stored[s], 16)
                    sp.dma_start(out_mid[:, ds(c, n * D)], xs_flat[HEAD:P - 1, ds(c, n * D)]).then_inc(out_stored[s], 16)

            def nodes(l):
                load = load_nodes(l)
                for i in range(2):
                    for s in range(2):
                        load(i, s, CH)
                with sp.Fori(2, HALF) as i:
                    for s in range(2):
                        load(i, s, CH)
                        store_nodes(l, i - 2, s, CH)
                load(HALF, 0, TAIL)
                for i in (HALF - 2, HALF - 1):
                    for s in range(2):
                        store_nodes(l, i, s, CH)
                store_nodes(l, HALF, 0, TAIL)

            after_initial(sp)
            for t in agg[1:]:
                per = RT // P * t.shape[1]
                piece = max(n for n in range(1, ZERO + 1) if per % n == 0)
                sp.dma_start(t.rearrange("(p c) w -> p (c w)", p=P).rearrange("p (a b) -> p a b", b=piece),
                             zeros[:, 0:piece].unsqueeze(1).to_broadcast([P, per // piece, piece])).then_inc(zeroed, 16)
            after_states(sp)
            nodes(0)
            sp.wait_ge(factors_cleared, 1)
            for v, to in ((node_vec1, cj), (node_vec1_n2, ci)):
                for a, b in ((0, HEAD), (HEAD, P - 1)):
                    sp.dma_start(to[a:b, :], v[a * COLS:b * COLS, :].rearrange("(p c) a -> p (c a)", p=b - a)).then_inc(nodes_in, 16)
                sp.dma_start(to[P - 1:P, 0:LASTP], v[(P - 1) * COLS:N, :].rearrange("(p c) a -> p (c a)", p=1)).then_inc(nodes_in, 16)
            groups(sp, load_attr)
            for l in (1, 2, 3):
                after_edges(sp, l)
                nodes(l)
            sp.dma_start(out_last, xs_flat[P - 1:P, 0:LASTP * D]).then_inc(last_stored, 16)
            for s in range(2):
                sp.wait_ge(out_stored[s], 32 * SLOT_USES[s])
            sp.wait_ge(last_stored, 16)

        @block.gpsimd
        def _(pool):
            nc.gpsimd.memset(ident[:, :], 0.0)
            nc.gpsimd.memset(earlier[:, :], 1.0).then_inc(pool_consts, 1)
            nc.gpsimd.iota(spare_i[:, :], [[P, G]], base=TRASH, channel_multiplier=1)
            pool.wait_ge(pool_consts, 1)
            nc.gpsimd.affine_select(out=ident[:, :], in_=ident[:, :], compare_op=ALU.not_equal, fill=1.0,
                                    base=0, pattern=[[-1, P]], channel_multiplier=1)
            nc.gpsimd.affine_select(out=earlier[:, ROW - P:ROW], in_=earlier[:, ROW - P:ROW], compare_op=ALU.is_gt,
                                    fill=0.0, base=0, pattern=[[-1, P]], channel_multiplier=1).then_inc(pool_consts, 1)

            def gather(to, of, rows, done):
                pool.sem_inc(pool_turns, 1)
                for t in range(G):
                    nc.gpsimd.indirect_dma_start(to[:, t, :], None, of, bass.IndirectOffsetOnAxis(rows[:, t:t + 1], 0),
                                                 bounds_check=of.shape[0] - 1, oob_is_err=True).then_inc(done, 16)

            def scatter(to, rows, of, done, **add):
                pool.sem_inc(pool_turns, 1)
                for t in range(G):
                    nc.gpsimd.indirect_dma_start(to, bass.IndirectOffsetOnAxis(rows[:, t:t + 1], 0), of[:, t, :], None,
                                                 bounds_check=RT - 1, oob_is_err=True, **add).then_inc(done, 16)

            def gather_x(k):
                gather(xg[k], xt[0], dst_at[k], x_got[k])

            def send_states(i, k):
                pool.wait_ge(st_ready, 2 * i + k + 1)
                pool.wait_ge(first_ready, 2 * i + k + 1)
                scatter(state[k], first_at[k], st_new[k], st_sent[k])

            def body0(i, k):
                pool.wait_ge(rows_at, 2 * i + k + 1)
                wait(pool, st_sent[k], 16 * G * i)
                gather(st[k], state[k], src_at[k], st_got[k])
                if not (isinstance(i, int) and 2 * i + k == 0):
                    send_states(i - 1 + k, 1 - k)
                if not is_last(i, k, 2):
                    pool.wait_ge(dst_rows_at, 2 * i + k + 3)
                    pool.wait_ge(z_ready, 2 * i + k + 1)
                    gather_x(k)

            for k in range(2):
                pool.wait_ge(dst_rows_at, k + 1)
                gather_x(k)
            after_initial(pool)
            groups(pool, body0)
            send_states(NG // 2 - 1, 1)

            def nodes(l):
                def flat(t, n):
                    return t.rearrange("p c w -> p (c w)")[:, 0:n * D].rearrange("p (c w) -> p c w", w=D)

                def factor(f, n):
                    return f.unsqueeze(2).to_broadcast([P, n, D])

                def scale(i, s, n):
                    if l == 0:
                        pool.wait_ge(n_share, 2 * i + s + 1)
                        v, f = node_in[s][1][:, 0:n, 2:2 + D], small[:, s, 3, 0:n]
                    else:
                        pool.wait_ge(n_in[s], loaded(l, i, s))
                        v, f = flat(node_in[s][0], n), (deg if l == 2 else ci)[:, ds(cols(i, s), n)]
                    ins = nc.gpsimd.tensor_tensor(v, v, factor(f, n), ALU.mult)
                    if l == 0:
                        ins.then_inc(n_shared, 1)
                        pool.wait_ge(n_shared, 2 * i + s + 1)
                        pool.sem_inc(pool_turns, 1)
                        ins = nc.gpsimd.tensor_tensor(v, v, xs[:, ds(cols(i, s), n), :], ALU.add)
                    ins.then_inc(n_scaled, 1)

                def finish(i, s, n):
                    x_now = xs[:, ds(cols(i, s), n), :]
                    if l != 2:
                        pool.wait_ge(n_rstd, in_layer(l, i, s) + 1)
                        pool.sem_inc(pool_turns, 1)
                        nc.gpsimd.tensor_tensor(x_now, y[s][:, 0:n, :], factor(small[:, s, 7, 0:n], n),
                                                ALU.mult).then_inc(n_done, 1)
                    else:
                        pool.wait_ge(n_done, in_layer(l, i, s) + 1)
                        wait(pool, x_stored[s], 16 * (2 * SLOT_USES[s] + i))
                        nc.gpsimd.tensor_tensor(flat(node_in[s][1], n), x_now, factor(cj[:, ds(cols(i, s), n)], n),
                                                ALU.mult).then_inc(n_weighted, 1)

                def body(i, s, n):
                    if l == 0:
                        scale(i, s, n)
                    if l >= 2 and behind(i, s):
                        scale(*behind(i, s))
                    if before(i, s):
                        finish(*before(i, s))

                if l == 2:
                    pool.wait_ge(n_share, CHUNKS + 2)
                if l >= 2:
                    scale(0, 0, CH)
                chunks(pool, body)
                finish(HALF, 0, TAIL)

            nodes(0)

            def edges(l):
                def get(i, k):
                    pool.wait_ge(g_rows_at, (l - 1) * NG + 2 * i + k + 1)
                    gather(xg[k], xt[l], src_at[k], g_got[k])

                def body(i, k):
                    g = (l - 1) * NG + 2 * i + k
                    pool.wait_ge(g_sum_sb, g + 1)
                    pool.wait_ge(g_firsts_at, g + 1)
                    wait(pool, agg_sent[1 - k], 16 * G * ((l - 1) * (NG // 2) + i + k))
                    scatter(agg[l], first_at[k], sums[k][:, :, 0:AW if l == 1 else D], agg_sent[k], compute_op=ALU.add)
                    if not is_last(i, k, 2):
                        get(i + 1, k)

                after_nodes(pool, l - 1)
                if l == 1:
                    after_zeroing(pool)
                get(0, 0)
                get(0, 1)
                groups(pool, body)

            for l in (1, 2, 3):
                edges(l)
                after_edges(pool, l)
                if l == 2:
                    pool.wait_ge(nodes_in, 16 * 6)
                nodes(l)

        @block.scalar
        def _(act):
            copy = nc.scalar.copy

            def turned_x(i, s, n):
                for step, k, c, n in steps_at(i, s, n, 0):
                    rows, wide = sizes(n, c)
                    act.wait_ge(turned, step + 1)
                    wait(act, mixed, step - 1)
                    copy(xT[k][0:rows, 0:wide], psum[0:rows, k, 0:wide]).then_inc(turned_sb, 1)

            act.wait_ge(setup, 1)

            def stage_dst(i, k):
                copy(dst_at[k][:, :], dst_row[:, ds((2 * i + k) * G, G)]).then_inc(dst_rows_at, 1)

            def stage_keys(i, k, key, done):
                copy(key_at[k][:, :], key[:, ds((2 * i + k) * G, G)]).then_inc(done, 1)

            def stage_src(i, k, done):
                copy(src_at[k][:, :], src_row[:, ds((2 * i + k) * G, G)]).then_inc(done, 1)

            for k in range(2):
                stage_dst(0, k)
                stage_keys(0, k, src_key, keys_at)
                stage_src(0, k, rows_at)
            chunks(act, turned_x)

            def ahead0(i, k):
                g = 2 * i + k
                act.wait_ge(z_turned, g + 1)
                wait(act, y_ready, g)
                copy(zt_a, bank(2))
                copy(zt_b[0:D, :], psum[0:D, 3, :]).then_inc(z_turned_sb, 1)

            def same0(i, k):
                g = 2 * i + k
                act.wait_ge(apart_ready, g + 1)
                wait(act, sum_ready, g - 1)
                for a in range(G):
                    last = nc.scalar.activation(same[k][:, a, 0:(a + 1) * P], apart[:, a, 0:(a + 1) * P],
                                                ACT.Identity, bias=one[:, 0:1], scale=-1.0 / NEG_BIG)
                last.then_inc(same_ready, 1)

            def body0(i, k):
                g = 2 * i + k
                if not is_last(i, k, 2):
                    act.wait_ge(z_ready, g + 1)
                    act.wait_ge(apart_ready, g + 1)
                    act.wait_ge(key_row, g + 1)
                    stage_dst(i + 1, k)
                    stage_keys(i + 1, k, src_key, keys_at)
                if not is_last(i, k, 1):
                    ahead0(i + k, 1 - k)
                act.wait_ge(expo_in, g + 1)
                nc.scalar.activation(expo[k][:, :, :], expo[k][:, :, :], ACT.Exp).then_inc(expo_out, 1)
                if not is_last(i, k, 2):
                    stage_src(i + 1, k, rows_at)
                if not is_last(i, k, 1):
                    same0(i + k, 1 - k)

            after_initial(act)
            ahead0(0, 0)
            same0(0, 0)
            groups(act, body0)

            def nodes(l):
                def square(i, s, n):
                    q = in_layer(l, i, s)
                    act.wait_ge(n_centred, q + 1)
                    wait(act, n_var, q - 1)
                    nc.scalar.activation(sq[s][:, 0:n, :], y[s][:, 0:n, :], ACT.Square, scale=D ** -0.5).then_inc(n_squared, 1)

                def deviation(i, s, n):
                    act.wait_ge(n_var, in_layer(l, i, s) + 1)
                    nc.scalar.activation(small[:, s, 7, 0:n], small[:, s, 6, 0:n], ACT.Sqrt,
                                         bias=ln_eps[:, 0:1]).then_inc(n_std, 1)

                def turn(step, k, c, n):
                    rows, wide = sizes(n, c)
                    act.wait_ge(m_turned, step + 1)
                    wait(act, m_hid, step - 1)
                    copy(xT[k][0:rows, 0:wide], psum[0:rows, k, 0:wide]).then_inc(m_turned_sb, 1)

                def hidden(step, k, c, n):
                    rows, wide = sizes(n, c)
                    act.wait_ge(m_hid, step + 1)
                    wait(act, m_out, step - 1)
                    nc.scalar.activation(hT[k][0:rows, 0:wide], psum[0:rows, 2 + k, 0:wide], ACT.Relu,
                                         bias=b1[0:rows, 0:1]).then_inc(m_hid_sb, 1)

                def result(step, k, c, n):
                    rows, wide = sizes(n, c)
                    act.wait_ge(m_out, step + 1)
                    wait(act, m_back, step - 1)
                    nc.scalar.activation(oT[k][0:rows, 0:wide], psum[0:rows, 4 + k, 0:wide], ACT.Relu,
                                         bias=b2[0:rows, 0:1]).then_inc(m_out_sb, 1)

                def body(i, s, n):
                    if before(i, s):
                        deviation(*before(i, s))
                    if l == 0:
                        act.wait_ge(n_expo_in, 2 * i + s + 1)
                        v = small[:, s, 0:2, 0:n]
                        nc.scalar.activation(v, v, ACT.Exp).then_inc(n_expo_out, 1)
                    square(i, s, n)

                def body_mlp(i, s, n):
                    two = before(i, s) and before(*before(i, s)[:2])
                    for m, (a, b, c) in enumerate(zip(*(steps_at(i, s, n, lag) for lag in range(3)))):
                        turn(*a)
                        if b:
                            hidden(*b)
                        if c:
                            result(*c)
                        if m == 0 and two:
                            square(*two)
                    if two:
                        deviation(*two)

                if l == 1:
                    chunks(act, body_mlp)
                    for st_ in steps_left(1):
                        hidden(*st_)
                    for st_ in steps_left(2):
                        result(*st_)
                    for q in ((HALF - 1, 1, CH), (HALF, 0, TAIL)):
                        square(*q)
                        deviation(*q)
                else:
                    chunks(act, body)
                    deviation(HALF, 0, TAIL)

            after_states(act)
            nodes(0)

            def edges(l):
                def prepare(i, k):
                    stage_src(i, k, g_rows_at)
                    stage_keys(i, k, dst_key, g_keys_at)

                def body(i, k):
                    g = (l - 1) * NG + 2 * i + k
                    act.wait_ge(g_got[k], 16 * G * ((l - 1) * (NG // 2) + i + 1))
                    if not is_last(i, k, 2):
                        act.wait_ge(g_key_row, g + 1)
                        act.wait_ge(g_same, g + 1)
                        prepare(i + 1, k)
                    if l == 1:
                        act.wait_ge(g_sent_in, g + 1)
                        wait(act, g_sum, g - 1)
                        nc.scalar.activation(val[k][:, :, 0:D], xg[k][:, :, :], ACT.Relu).then_inc(g_relu, 1)
                    wait(act, agg_sent[k], 16 * G * ((l - 1) * (NG // 2) + i))
                    if l > 1:
                        copy(first_at[k][:, :], dst_first[:, ds((2 * i + k) * G, G)]).then_inc(g_firsts_at, 1)
                    act.wait_ge(g_sum, g + 1)
                    w = AW if l == 1 else D
                    copy(sums[k][:, :, 0:w], bank(6 + k, G * w).rearrange("p (t w) -> p t w", w=w)).then_inc(g_sum_sb, 1)

                after_nodes(act, l - 1)
                prepare(0, 0)
                prepare(0, 1)
                groups(act, body)

            for l in (1, 2, 3):
                edges(l)
                after_edges(act, l)
                nodes(l)

        @block.tensor
        def _(pe):
            pe.wait_ge(pool_consts, 2)
            pe.wait_ge(setup, 2)

            def turn_x(step, k, c, n, s):
                rows, wide = sizes(n, c)
                wait(pe, turned_sb, step - 1)
                for b in range(0, wide, P):
                    last = nc.tensor.transpose(psum[0:rows, k, b:b + P],
                                               y[s].rearrange("p c w -> p (c w)")[:, c * D + b:c * D + b + rows],
                                               ident[:, :])
                last.then_inc(turned, 1)

            def mix_x(step, k, c, n):
                rows, wide = sizes(n, c)
                pe.wait_ge(turned_sb, step + 1)
                wait(pe, unmixed, step - 1)
                for b in range(0, wide, P):
                    o = psum[:, 2 + k, b // P * (P + B):(b // P + 1) * (P + B)]
                    last = nc.tensor.matmul(o, xT[k][0:rows, b:b + P], root[0:rows, :], start=True, stop=True)
                last.then_inc(mixed, 1)

            def body_x(i, s, n):
                pe.wait_ge(x_in[s], x_loaded(i, s))
                for a, b in zip(steps_at(i, s, n, 0), steps_at(i, s, n, 1)):
                    turn_x(*a, s)
                    if b:
                        mix_x(*b)

            chunks(pe, body_x)
            for st_ in steps_left(1):
                mix_x(*st_)

            def rows_of(to, column):
                for t in range(G):
                    last = nc.tensor.transpose(to[:, t * P:(t + 1) * P], column[:, t:t + 1].to_broadcast([P, P]),
                                               ident[:, :])
                return last

            def turn0(i, k):
                g = 2 * i + k
                pe.wait_ge(keys_at, g + 1)
                wait(pe, apart_ready, g)
                rows_of(bank(0), key_at[k]).then_inc(key_row, 1)
                pe.wait_ge(z_ready, g + 1)
                wait(pe, z_turned_sb, g)
                for t in range(G):
                    nc.tensor.transpose(psum[:, 2, t * P:(t + 1) * P],
                                        z[:, t, 0:B, :].rearrange("p k d -> p (k d)"), ident[:, :])
                    last = nc.tensor.transpose(psum[0:D, 3, t * P:(t + 1) * P], z[:, t, B, :], ident[:, :])
                last.then_inc(z_turned, 1)

            def spline0(i, k):
                g = 2 * i + k
                pe.wait_ge(z_turned_sb, g + 1)
                wait(pe, y_used, g)
                for t in range(G):
                    o = psum[:, 4 + t // 2, t % 2 * K * D:(t % 2 + 1) * K * D]
                    nc.tensor.matmul(o, zt_a[:, t * P:(t + 1) * P], w_a[:, :, :].rearrange("p j o -> p (j o)"),
                                     start=True, stop=False)
                    last = nc.tensor.matmul(o, zt_b[0:D, t * P:(t + 1) * P],
                                            w_b[:, :, :].rearrange("p j o -> p (j o)"), start=False, stop=True)
                last.then_inc(y_ready, 1)

            def logits0(i, k):
                g = 2 * i + k
                pe.wait_ge(t_ready, g + 1)
                wait(pe, max_ready, g)
                rows_of(bank(1), tmax[k][:, 0, :]).then_inc(t_row, 1)

            def sum_shared(k, v, w, done):
                for a in range(G):
                    for b in range(a, G):
                        last = nc.tensor.matmul(psum[:, 6 + k, a * w:(a + 1) * w], same[k][:, b, a * P:(a + 1) * P],
                                                v[:, b, 0:w], start=(b == a), stop=(b == G - 1))
                last.then_inc(done, 1)

            def body0(i, k):
                g = 2 * i + k
                ahead = not is_last(i, k, 1)
                if ahead:
                    turn0(i + k, 1 - k)
                    spline0(i + k, 1 - k)
                pe.wait_ge(val_ready, g + 1)
                pe.wait_ge(same_ready, g + 1)
                wait(pe, st_ready, g - 1)
                sum_shared(k, val[k], AW, sum_ready)
                if ahead:
                    logits0(i + k, 1 - k)

            after_initial(pe)
            turn0(0, 0)
            spline0(0, 0)
            logits0(0, 0)
            groups(pe, body0)

            def edges(l):
                def prepare(i, k):
                    g = (l - 1) * NG + 2 * i + k
                    pe.wait_ge(g_keys_at, g + 1)
                    wait(pe, g_same, g - 1)
                    rows_of(bank(k), key_at[k]).then_inc(g_key_row, 1)

                def body(i, k):
                    g = (l - 1) * NG + 2 * i + k
                    if not is_last(i, k, 1):
                        prepare(i + k, 1 - k)
                    pe.wait_ge(g_same, g + 1)
                    if l == 1:
                        pe.wait_ge(g_relu, g + 1)
                    else:
                        pe.wait_ge(g_got[k], 16 * G * ((l - 1) * (NG // 2) + i + 1))
                    wait(pe, g_sum_sb, g - 1)
                    sum_shared(k, val[k] if l == 1 else xg[k], AW if l == 1 else D, g_sum)

                after_nodes(pe, l - 1)
                prepare(0, 0)
                groups(pe, body)

            def turn(step, k, c, n, s):
                rows, wide = sizes(n, c)
                wait(pe, m_turned_sb, step - 1)
                for b in range(0, wide, P):
                    last = nc.tensor.transpose(
                        psum[0:rows, k, b:b + P],
                        node_in[s][1].rearrange("p c w -> p (c w)")[:, c * D + b:c * D + b + rows], ident[:, :])
                last.then_inc(m_turned, 1)

            def hidden(step, k, c, n):
                rows, wide = sizes(n, c)
                pe.wait_ge(m_turned_sb, step + 1)
                wait(pe, m_hid_sb, step - 1)
                nc.tensor.matmul(psum[0:rows, 2 + k, 0:wide], w1[0:rows, 0:rows], xT[k][0:rows, 0:wide],
                                 start=True, stop=True).then_inc(m_hid, 1)

            def result(step, k, c, n):
                rows, wide = sizes(n, c)
                pe.wait_ge(m_hid_sb, step + 1)
                wait(pe, m_out_sb, step - 1)
                nc.tensor.matmul(psum[0:rows, 4 + k, 0:wide], w2[0:rows, 0:rows], hT[k][0:rows, 0:wide],
                                 start=True, stop=True).then_inc(m_out, 1)

            def turn_back(step, k, c, n):
                rows, wide = sizes(n, c)
                pe.wait_ge(m_out_sb, step + 1)
                wait(pe, m_back_used, step - 1)
                for b in range(0, wide, P):
                    last = nc.tensor.transpose(psum[:, 6 + k, b:b + rows], oT[k][0:rows, b:b + P],
                                               ident[0:rows, 0:rows])
                last.then_inc(m_back, 1)

            def mlp(i, s, n):
                pe.wait_ge(m_h, 2 * i + s + 1)
                for a, *rest in zip(*(steps_at(i, s, n, lag) for lag in range(4))):
                    turn(*a, s)
                    for stage, b in zip((hidden, result, turn_back), rest):
                        if b:
                            stage(*b)

            for l in (1, 2, 3):
                edges(l)
                if l == 1:
                    after_edges(pe, 1)
                    chunks(pe, mlp)
                    left = [list(steps_left(lag)) for lag in (1, 2, 3)]
                    while any(left):
                        for stage, steps in zip((hidden, result, turn_back), left):
                            if steps:
                                stage(*steps.pop(0))

        @block.vector
        def _(dve):
            v = nc.vector
            begin = Chain(dve, setup_steps, 0)

            def link(ins):
                begin.step(ins)
                begin.wait()

            v.memset(src_row[:, MAIN:TILES], -1)
            v.memset(dst_row[:, MAIN:TILES], -1)
            for t in (root, w1, w2):
                v.memset(t[:, :], 0.0)
            v.memset(attr2[:, MAIN:TILES, :], 0.0).then_inc(cleared, 1)
            dve.wait_ge(edges_in, 16 * 6)
            dve.wait_ge(pool_consts, 2)
            for row, key in ((src_row, src_key), (dst_row, dst_key)):
                v.tensor_copy(key[:, :], row[:, :])
            link(v.tensor_copy(spare[:, :], spare_i[:, :]))
            for row, key in ((src_row, src_key), (dst_row, dst_key)):
                v.tensor_scalar(row[:, :], key[:, :], 0.0, None, ALU.max)
            v.memset(one[:, :], 1.0)
            v.memset(ln_eps[:, :], LN_EPS)
            link(v.memset(zeros, 0.0))
            for key, rel in ((src_key, src_rel), (dst_key, dst_rel)):
                link(v.tensor_tensor(rel[:, :].rearrange("p (n t) -> p n t", t=G),
                                     key[:, :].rearrange("p (n t) -> p n t", t=G),
                                     spare[:, :].unsqueeze(1).to_broadcast([P, NG, G]), ALU.subtract))
                link(v.scalar_tensor_tensor(out=rel[:, :], in0=key[:, :], scalar=0.0, in1=rel[:, :],
                                            op0=ALU.is_ge, op1=ALU.mult))
            dve.sem_inc(setup, 1)
            dve.wait_ge(consts_in, 16 * (5 * B + K + 4))
            link(v.tensor_tensor(scratch[:, :, :], root[:, 0:P].rearrange("p (a b) -> p a b", a=B),
                                 att1[:, :].unsqueeze(1).to_broadcast([P, B, D]), ALU.mult))
            link(v.tensor_reduce(root[:, P:P + B], scratch[:, :, :], AX_X, ALU.add))
            link(v.tensor_tensor(root[:, 0:P], root[:, 0:P], ident[:, :], ALU.add))
            link(v.tensor_scalar(eps1[:, :], eps1[:, :], 1.0, None, ALU.add))
            for s in range(2):
                link(v.memset(node_in[s][0], 0.0))
                link(v.memset(node_in[s][0][:, :, 1], NEG_BIG))
            dve.sem_inc(setup, 1)

            def root_body(i, s, n):
                wait(dve, init_stored[s], 32 * i)
                for step, k, c, n in steps_at(i, s, n, 0):
                    w = min(STEP, n - c)
                    nb, per = -(-w // B), min(B, w)
                    dve.wait_ge(mixed, step + 1)
                    o = psum[:, 2 + k, 0:nb * (P + B)].rearrange("p (b f) -> p b f", f=P + B)
                    v.tensor_tensor(
                        xs[:, ds(cols(i, s) + c, w), :].rearrange("p (b a) d -> p b a d", b=nb),
                        o[:, :, 0:per * D].rearrange("p b (a d) -> p b a d", d=D),
                        bias_b[:, :].unsqueeze(1).unsqueeze(1).to_broadcast([P, nb, per, D]), ALU.add)
                    v.tensor_copy(node_in[s][0][:, c:c + w, 0].rearrange("p (b a) -> p b a", b=nb),
                                  o[:, :, P:P + per]).then_inc(unmixed, 1)
                dve.wait_ge(unmixed, step + 1)
                dve.sem_inc(rooted, 1)

            chunks(dve, root_body)

            p4 = attr2[:, :, :]
            link(v.tensor_scalar(p4, p4, float(K - 1), 0.0, ALU.mult, ALU.max))
            link(v.tensor_scalar(p4, p4, float(K - 1), None, ALU.min))
            up = zt_a[:, 0:TILES]
            for d in range(2):
                for n in range(K):
                    link(v.tensor_scalar(up, attr2[:, :, d], -1.0, float(n + 1), ALU.mult, ALU.add))
                    link(v.tensor_scalar(hat[d][:, :, n], attr2[:, :, d], float(1 - n), None, ALU.add))
                    link(v.tensor_tensor(hat[d][:, :, n], hat[d][:, :, n], up, ALU.min))
                link(v.tensor_scalar(hat[d][:, :, :], hat[d][:, :, :], 0.0, None, ALU.max))

            c = Chain(dve, e0, 0)

            def first_edges(k, rel, to, done):
                c.step(v.scalar_tensor_tensor(out=count[k][:, :], in0=count[k][:, :], scalar=0.0, in1=rel,
                                              op0=ALU.is_equal, op1=ALU.mult))
                c.wait()
                for t in to[1:]:
                    v.tensor_tensor(t, count[k][:, :], spare[:, :], ALU.add)
                v.tensor_tensor(to[0], count[k][:, :], spare[:, :], ALU.add).then_inc(done, 1)

            def count_earlier(k):
                for a in range(G):
                    w = (a + 1) * P
                    at = a * (a + 1) // 2 * P
                    last = v.tensor_tensor_reduce(out=junk[:, at:at + w], in0=same[k][:, a, 0:w],
                                                  in1=earlier[:, ROW - w:ROW], scale=1.0, scalar=0.0,
                                                  op0=ALU.mult, op1=ALU.add, accum_out=count[k][:, a:a + 1])
                c.step(last)

            def knots0(i, k):
                g = 2 * i + k
                dve.wait_ge(x_got[k], 16 * G * (i + 1))
                wait(dve, z_turned, g)
                h = hat[0][:, ds(g * G, G), :]
                v.tensor_tensor(z, xg[k][:, :, :].unsqueeze(2).to_broadcast([P, G, K, D]),
                                h.unsqueeze(3).to_broadcast([P, G, K, D]), ALU.mult).then_inc(z_ready, 1)

            def apart0(i, k):
                g = 2 * i + k
                dve.wait_ge(key_row, g + 1)
                wait(dve, same_ready, g)
                for a in range(G):
                    last = v.tensor_scalar(apart[:, a, :], bank(0), key_at[k][:, a:a + 1], NEG_BIG,
                                           ALU.not_equal, ALU.mult)
                last.then_inc(apart_ready, 1)

            def earlier0(i, k):
                dve.wait_ge(same_ready, 2 * i + k + 1)
                count_earlier(k)

            def message0(i, k):
                g = 2 * i + k
                dve.wait_ge(y_ready, g + 1)
                h = hat[1][:, ds(g * G, G), :]
                for b in range(2):
                    last = v.tensor_tensor(
                        ty[:, 2 * b:2 * b + 2, :, :],
                        psum[:, 4 + b, 0:2 * K * D].rearrange("p (t j o) -> p t j o", t=2, j=K),
                        h[:, 2 * b:2 * b + 2, :].unsqueeze(3).to_broadcast([P, 2, K, D]), ALU.mult)
                last.then_inc(y_used, 1)
                dve.wait_ge(y_used, g + 1)
                c.step(v.tensor_reduce(msg[k][:, :, :], ty.rearrange("p t j o -> p t o j"), AX_X, ALU.add))
                c.wait()
                c.step(v.tensor_tensor(lw, msg[k][:, :, :], att2[:, :].unsqueeze(1).to_broadcast([P, G, D]), ALU.mult))
                c.wait()
                v.tensor_reduce(tmax[k][:, 0, :], lw, AX_X, ALU.add).then_inc(t_ready, 1)

            def first0(i, k):
                wait(dve, st_sent[k], 16 * G * i)
                dve.wait_ge(t_row, 2 * i + k + 1)
                first_edges(k, src_rel[:, ds((2 * i + k) * G, G)], [first_at[k][:, :]], first_ready)

            def max0(i, k):
                for a in range(G):
                    last = v.tensor_tensor_reduce(out=apart[:, a, :], in0=apart[:, a, :], in1=bank(1), scale=1.0,
                                                  scalar=NEG_BIG, op0=ALU.add, op1=ALU.max,
                                                  accum_out=tmax[k][:, 1, a:a + 1])
                last.then_inc(max_ready, 1)

            def body0(i, k):
                g = 2 * i + k
                ahead = not is_last(i, k, 1)
                j, o = i + k, 1 - k
                c.body(g)
                if ahead:
                    knots0(j, o)
                dve.wait_ge(st_got[k], 16 * G * (i + 1))
                dve.wait_ge(max_ready, g + 1)
                u = tmax[k][:, :, :]
                old_max, new_max = st[k][:, :, 1], st_new[k][:, :, 1]
                c.step(v.tensor_tensor(u, u, st[k][:, :, 0].unsqueeze(1).to_broadcast([P, 2, G]), ALU.add))
                c.wait()
                c.step(v.scalar_tensor_tensor(out=u, in0=u, scalar=SLOPE, in1=u, op0=ALU.mult, op1=ALU.max))
                c.wait()
                c.step(v.tensor_tensor(new_max, u[:, 1, :], old_max, ALU.max))
                v.tensor_copy(st_new[k][:, :, 0], st[k][:, :, 0])
                c.wait()
                v.tensor_tensor(expo[k][:, 0, :], u[:, 0, :], new_max, ALU.subtract)
                v.tensor_tensor(expo[k][:, 1, :], old_max, new_max, ALU.subtract).then_inc(expo_in, 1)
                if ahead:
                    dve.wait_ge(max_ready, g + 1)
                    apart0(j, o)
                dve.wait_ge(expo_out, g + 1)
                wait(dve, sum_ready, g - 1)
                v.tensor_tensor(val[k][:, :, 0:D], msg[k][:, :, :],
                                expo[k][:, 0, :].unsqueeze(2).to_broadcast([P, G, D]), ALU.mult)
                v.tensor_copy(val[k][:, :, D], expo[k][:, 0, :]).then_inc(val_ready, 1)
                c.step(v.tensor_tensor(st_new[k][:, :, 2:SW], st[k][:, :, 2:SW],
                                       expo[k][:, 1, :].unsqueeze(2).to_broadcast([P, G, AW]), ALU.mult))
                if ahead:
                    earlier0(j, o)
                dve.wait_ge(sum_ready, g + 1)
                c.wait()
                v.tensor_tensor(st_new[k][:, :, 2:SW], st_new[k][:, :, 2:SW],
                                bank(6 + k, G * AW).rearrange("p (t w) -> p t w", w=AW), ALU.add).then_inc(st_ready, 1)
                if ahead:
                    message0(j, o)
                    first0(j, o)
                    max0(j, o)

            after_initial(dve)
            c.per = 0
            knots0(0, 0)
            apart0(0, 0)
            earlier0(0, 0)
            message0(0, 0)
            c.wait()
            first0(0, 0)
            max0(0, 0)
            c.first, c.per = c.n, E0_STEPS
            groups(dve, body0)

            def nodes(l):
                c = Chain(dve, n_steps[l], N_STEPS[l])

                def front(i, s, n, halfway):
                    q = in_layer(l, i, s)
                    sm = lambda j: small[:, s, j, 0:n]
                    wide = lambda a: a.unsqueeze(2).to_broadcast([P, n, D])
                    x_now = xs[:, ds(cols(i, s), n), :]
                    yy = y[s][:, 0:n, :]
                    if l == 0:
                        dve.wait_ge(n_in[s], loaded(l, i, s))
                        a, b = (t[:, 0:n, :] for t in node_in[s])
                        c.step(v.tensor_tensor(sm(2), a[:, :, 1], b[:, :, 1], ALU.max))
                        c.wait()
                        v.tensor_tensor(sm(0), a[:, :, 1], sm(2), ALU.subtract)
                        v.tensor_tensor(sm(1), b[:, :, 1], sm(2), ALU.subtract).then_inc(n_expo_in, 1)
                        dve.wait_ge(n_expo_out, 2 * i + s + 1)
                        v.tensor_tensor(sm(5), a[:, :, 2 + D], sm(0), ALU.mult)
                        c.step(v.tensor_tensor(sm(6), b[:, :, 2 + D], sm(1), ALU.mult))
                        c.wait()
                        c.step(v.tensor_tensor(sm(2), sm(5), sm(6), ALU.add))
                        c.wait()
                        c.step(v.tensor_scalar(sm(2), sm(2), DEN_EPS, None, ALU.add))
                        c.wait()
                        c.step(v.reciprocal(sm(2), sm(2)))
                        c.wait()
                        v.tensor_tensor(sm(3), sm(1), sm(2), ALU.mult).then_inc(n_share, 1)
                        c.step(v.tensor_tensor(sm(4), sm(0), sm(2), ALU.mult))
                        c.wait()
                        c.step(v.tensor_tensor(a[:, :, 2:2 + D], a[:, :, 2:2 + D], wide(sm(4)), ALU.mult))
                        halfway()
                        c.wait()
                        wait(dve, n_done, q - 1)
                        dve.wait_ge(n_scaled, 2 * i + s + 1)
                        c.step(v.tensor_tensor(yy, a[:, :, 2:2 + D], b[:, :, 2:2 + D], ALU.add))
                        c.wait()
                    elif l == 1:
                        wait(dve, n_done, q - 1)
                        for step, k, c0, n_ in steps_at(i, s, n, 0):
                            w = min(STEP, n_ - c0)
                            dve.wait_ge(m_back, step + 1)
                            v.tensor_tensor(y[s][:, c0:c0 + w, :],
                                            psum[:, 6 + k, 0:w * D].rearrange("p (c d) -> p c d", d=D),
                                            xs[:, ds(cols(i, s) + c0, w), :], ALU.add).then_inc(m_back_used, 1)
                        halfway()
                        dve.wait_ge(m_back_used, step + 1)
                    else:
                        a = node_in[s][0].rearrange("p c w -> p (c w)")[:, 0:n * D].rearrange("p (c w) -> p c w", w=D)
                        dve.wait_ge(n_scaled, (l - 1) * (CHUNKS + 1) + 2 * i + s + 1)
                        wait(dve, n_done, q - 1)
                        c.step(v.tensor_tensor(yy, a, x_now, ALU.add))
                        halfway()
                        c.wait()
                    c.step(v.tensor_reduce(sm(5), yy, AX_X, ALU.add))
                    c.wait()
                    c.step(v.tensor_scalar(sm(5), sm(5), 1.0 / D, None, ALU.mult))
                    c.wait()
                    v.tensor_tensor(yy, yy, wide(sm(5)), ALU.subtract).then_inc(n_centred, 1)

                def variance(i, s, n):
                    dve.wait_ge(n_squared, in_layer(l, i, s) + 1)
                    v.tensor_reduce(small[:, s, 6, 0:n], sq[s][:, 0:n, :], AX_X, ALU.add).then_inc(n_var, 1)

                def back(i, s, n):
                    q = in_layer(l, i, s)
                    dve.wait_ge(n_std, q + 1)
                    v.reciprocal(small[:, s, 7, 0:n], small[:, s, 7, 0:n]).then_inc(n_rstd, 1)
                    if l == 2:
                        dve.wait_ge(n_rstd, q + 1)
                        v.tensor_tensor(xs[:, ds(cols(i, s), n), :], y[s][:, 0:n, :],
                                        small[:, s, 7, 0:n].unsqueeze(2).to_broadcast([P, n, D]),
                                        ALU.mult).then_inc(n_done, 1)

                def mlp_input(i, s, n):
                    dve.wait_ge(n_in[s], loaded(l, i, s))
                    wait(dve, m_turned, (2 * i + s - 1) * len(STEPS[0]))
                    a = node_in[s][0].rearrange("p c w -> p (c w)")[:, 0:n * AW].rearrange("p (c w) -> p c w", w=AW)
                    v.tensor_copy(deg[:, ds(cols(i, s), n)], a[:, :, D])
                    v.scalar_tensor_tensor(
                        out=node_in[s][1].rearrange("p c w -> p (c w)")[:, 0:n * D].rearrange("p (c w) -> p c w", w=D),
                        in0=xs[:, ds(cols(i, s), n), :], scalar=eps1[:, 0:1], in1=a[:, :, 0:D],
                        op0=ALU.mult, op1=ALU.add).then_inc(m_h, 1)

                def body(i, s, n):
                    c.body(2 * i + s)
                    if l == 1 and not (isinstance(i, int) and 2 * i + s + 2 > CHUNKS):
                        mlp_input(i + 1, s, TAIL if isinstance(i, int) and i == HALF - 1 else CH)
                    last = before(i, s)
                    if last:
                        variance(*last)
                    front(i, s, n, lambda: last and back(*last))
                    assert c.n == N_STEPS[l]

                if l == 1:
                    mlp_input(0, 0, CH)
                    mlp_input(0, 1, CH)
                chunks(dve, body)
                variance(HALF, 0, TAIL)
                back(HALF, 0, TAIL)

            after_states(dve)
            nodes(0)
            for f in (cj, ci):
                last = v.memset(f[P - 32:P, LASTP:COLS], 0.0)
            last.then_inc(factors_cleared, 1)
            for k in range(2):
                v.memset(val[k][:, :, D], 1.0)

            def edges(l):
                nonlocal c
                c = Chain(dve, ge[l], 2)

                def body(i, k):
                    c.body(2 * i + k)
                    g = (l - 1) * NG + 2 * i + k
                    dve.wait_ge(g_key_row, g + 1)
                    wait(dve, g_sum, g - 1)
                    for a in range(G):
                        w = (a + 1) * P
                        last = v.tensor_scalar(same[k][:, a, 0:w], bank(k)[:, 0:w], key_at[k][:, a:a + 1], None,
                                               ALU.is_equal)
                    last.then_inc(g_same, 1)
                    if l == 1:
                        dve.wait_ge(attr_in[k], attr_loaded(i, k))
                        dve.wait_ge(g_got[k], 16 * G * (i + 1))
                        v.tensor_tensor(xg[k][:, :, :], xg[k][:, :, :], attr[k][:, :, :], ALU.add).then_inc(g_sent_in, 1)
                        dve.wait_ge(g_same, g + 1)
                        count_earlier(k)
                        c.wait()
                        wait(dve, agg_sent[k], 16 * G * i)
                        cs = ds((2 * i + k) * G, G)
                        first_edges(k, dst_rel[:, cs], [first_at[k][:, :], dst_first[:, cs]], g_firsts_at)

                after_nodes(dve, l - 1)
                groups(dve, body)

            for l in (1, 2, 3):
                edges(l)
                after_edges(dve, l)
                nodes(l)
                if l == 1:
                    after_nodes(dve, 1)
                    link(v.tensor_scalar(deg[:, :], deg[:, :], 1.0, None, ALU.max))
                    v.reciprocal(deg[:, :], deg[:, :]).then_inc(n_share, 1)


_INS = ['x', 'src', 'dst', 'edge_attr_2', 'edge_attr_32', 'node_vec1', 'node_vec1_n2', 'L0_gnn_weight',
        'L0_gnn_root_weight', 'L0_gnn_att_weight', 'L0_gnn_bias', 'L1_gnn_eps', 'L1_gnn_W1', 'L1_gnn_b1',
        'L1_gnn_W2', 'L1_gnn_b2']
_OUTS = [((100000, 32), 'float32')]


def kernel(**inputs):
    import numpy as _np
    import concourse.bacc as _bacc
    from concourse import mybir as _mybir
    from concourse.bass_utils import run_bass_kernel_spmd as _run

    nc = _bacc.Bacc("TRN2", target_bir_lowering=False, num_devices=1)
    arrays, args = {}, []
    for name in _INS:
        a = _np.ascontiguousarray(inputs[name])
        arrays[f"in_{name}_dram"] = a
        args.append(nc.dram_tensor(f"in_{name}_dram", a.shape, _mybir.dt.from_np(a.dtype), kind="ExternalInput").ap())
    for i, (shape, dtype) in enumerate(_OUTS):
        dt = _mybir.dt.from_np(_np.dtype(dtype))
        args.append(nc.dram_tensor(f"out_{i}_dram", shape, dt, kind="ExternalOutput").ap())
    gnn_program(nc, *args)
    r = _run(nc, [arrays], core_ids=[0])
    got = tuple(r.results[0][f"out_{i}_dram"] for i in range(len(_OUTS)))
    return got[0]
```

```python
from contextlib import ExitStack
from itertools import zip_longest

import concourse.bass as bass
from concourse import mybir


F32 = mybir.dt.float32
BF16 = mybir.dt.bfloat16
I32 = mybir.dt.int32
ALU = mybir.AluOpType
ACT = mybir.ActivationFunctionType
AX_X = mybir.AxisListType.X

P = 128
G = 4
ROW = G * P
NEG_BIG = -2.0 ** 126
SLOPE = 0.2
LN_EPS = 1e-5
DEN_EPS = 1e-16
PARTS = 3


def ds(start, size):
    return bass.ds(start, size)


def wait(eng, sem, value):
    if not (isinstance(value, int) and value <= 0):
        eng.wait_ge(sem, value)


class Chain:

    def __init__(self, eng, sem, per, first=0):
        self.eng, self.sem, self.per, self.first = eng, sem, per, first
        self.base, self.n = first, 0

    def body(self, number):
        self.base, self.n = self.first + number * self.per, 0

    def step(self, ins):
        ins.then_inc(self.sem, 1)
        self.n += 1

    def wait(self, n=None):
        self.eng.wait_ge(self.sem, self.base + (self.n if n is None else n))


def gnn_program(nc, x, src, dst, edge_attr_2, edge_attr_32, node_vec1, node_vec1_n2,
                spline_w, root_w, att_w, bias, gine_eps, gine_w1, gine_b1, gine_w2, gine_b2, out):
    N, D = x.shape
    E = src.shape[0]
    K = 5
    LAST = gine_eps.shape[0] - 1
    assert P % D == 0 and spline_w.shape[0] == K * K
    B = P // D

    COLS = -(-N // P)
    NT = COLS * P
    LASTP = N - (P - 1) * COLS
    HEAD = 112
    STEP = 3 * B
    CH = 4 * STEP
    CHUNKS = COLS // CH
    TAIL = COLS - CHUNKS * CH
    assert CHUNKS % 2 == 0 and 0 < TAIL < CH
    HALF = CHUNKS // 2
    STEPS = [list(range(0, CH, STEP)), list(range(0, TAIL, STEP))]
    NSTEP = CHUNKS * len(STEPS[0]) + len(STEPS[1])
    SLOT_USES = (HALF + 1, HALF)

    MAIN = E // P
    REST = E - MAIN * P
    TILES = -(-(MAIN + 1) // (2 * G)) * 2 * G
    NG = TILES // G
    assert TILES > MAIN + 1 - (REST == 0) and MAIN % G == 2
    UNUSED = TILES - (MAIN + 1)

    TRASH = NT
    RT = NT + ROW
    SW = D + 3
    AW = D + 1

    def dram(name, rows, width):
        return nc.dram_tensor(name, (rows, width), F32).ap()

    state = [dram("state_even", RT, SW), dram("state_odd", RT, SW)]
    agg = [None, dram("agg_1", RT, AW), dram("agg_2", RT, D), dram("agg_3", RT, D)]
    xt = [x, dram("x_1", NT, D), dram("x_2", NT, D), dram("x_3", NT, D)]

    with ExitStack() as ctx:
        def sb(name, shape, dt=F32):
            return ctx.enter_context(nc.sbuf_tensor(name, shape, dt))

        def sem(name):
            return ctx.enter_context(nc.semaphore(name))

        def pair(name):
            return [sem(name + "_0"), sem(name + "_1")]

        xs = sb("xs", [P, COLS, D])
        src_row = sb("src_row", [P, TILES], I32)
        dst_row = sb("dst_row", [P, TILES], I32)
        src_key = sb("src_key", [P, TILES])
        dst_key = sb("dst_key", [P, TILES])
        src_rel = sb("src_rel", [P, TILES])
        dst_rel = sb("dst_rel", [P, TILES])
        dst_first = sb("dst_first", [P, TILES], I32)
        attr2 = sb("attr2", [P, TILES, 2])
        hat = [sb("hat0", [P, TILES, K]), sb("hat1", [P, TILES, K])]
        ident = sb("ident", [P, P])
        earlier = sb("earlier", [P, ROW])
        earlier_own = sb("earlier_own", [P, P], BF16)
        one16 = sb("one16", [P, 1], BF16)
        spare_i = sb("spare_i", [P, G], I32)
        spare = sb("spare", [P, G])
        root = sb("root", [P, P + B])
        att1 = sb("att1", [P, D])
        att2 = sb("att2", [P, D])
        bias_b = sb("bias_b", [P, D])
        w_a = sb("w_a", [P, K, D])
        w_b = sb("w_b", [D, K, D])
        w1 = sb("w1", [P, P])
        w2 = sb("w2", [P, P])
        b1 = sb("b1", [P, 1])
        b2 = sb("b2", [P, 1])
        eps1 = sb("eps1", [P, 1])
        one = sb("one", [P, 1])
        ln_eps = sb("ln_eps", [P, 1])
        cj = hat[0][:, :, :].rearrange("p t k -> p (t k)")[:, 0:COLS]
        deg = hat[0][:, :, :].rearrange("p t k -> p (t k)")[:, COLS:2 * COLS]
        ci = hat[1][:, :, :].rearrange("p t k -> p (t k)")[:, 0:COLS]

        xg = [sb(f"xg{k}", [P, G, D]) for k in range(2)]
        src_at = [sb(f"src_at{k}", [P, G], I32) for k in range(2)]
        dst_at = [sb(f"dst_at{k}", [P, G], I32) for k in range(2)]
        first_at = [sb(f"first_at{k}", [P, G], I32) for k in range(2)]
        key_at = [sb(f"key_at{k}", [P, G]) for k in range(2)]
        st = [sb(f"st{k}", [P, G, SW]) for k in range(2)]
        st_new = [sb(f"st_new{k}", [P, G, SW]) for k in range(2)]
        msg = [sb(f"msg{k}", [P, G, D]) for k in range(2)]
        val = [sb(f"val{k}", [P, G, AW]) for k in range(2)]
        tmax = [sb(f"tmax{k}", [P, 2, G]) for k in range(2)]
        expo = [sb(f"expo{k}", [P, 2, G]) for k in range(2)]
        count = [sb(f"count{k}", [P, G]) for k in range(2)]
        attr = [sb(f"attr{k}", [P, G, D]) for k in range(2)]
        sums = [sb(f"sums{k}", [P, G, AW]) for k in range(2)]

        ARENA = 15168
        arena = sb("arena", [P, ARENA])
        at = [0]

        def cut(shape, start=None):
            if start is not None:
                at[0] = start
            n = 1
            for s in shape:
                n *= s
            v = arena[:, at[0]:at[0] + n]
            at[0] += n
            assert at[0] <= ARENA
            if len(shape) == 2:
                v = v.rearrange("p (a b) -> p a b", a=shape[0])
            if len(shape) == 3:
                v = v.rearrange("p (a b c) -> p a b c", a=shape[0], b=shape[1])
            return v

        same = [cut([G, ROW], 0), cut([G, ROW])]
        same16 = [cut([G * ROW // 2], k * G * ROW).bitcast(BF16).rearrange("p (a b) -> p a b", a=G) for k in range(2)]
        apart = cut([G * ROW // 2], 2 * G * ROW).bitcast(BF16).rearrange("p (a b) -> p a b", a=G)
        key_sb = cut([ROW])
        own = cut([G * P // 2]).bitcast(BF16).rearrange("p (a b) -> p a b", a=G)
        rest = cut([G, AW])
        parts = cut([G * PARTS * AW // 2]).bitcast(BF16).rearrange("p (a c w) -> p a c w", a=G, c=PARTS)
        products = cut([sum(range(1, G + 1)) * P])
        logits16 = products[:, 0:G * ROW // 2].bitcast(BF16).rearrange("p (a b) -> p a b", a=G)
        z = cut([G, K, D])
        ty = cut([G, K, D])
        zt_a = cut([ROW])
        zt_b = cut([ROW])
        lw = cut([G, D])
        ZERO_COLS = -(-(RT // P) // (NG - 8))
        zeros = cut([ZERO_COLS * AW])
        node_in = [[cut([CH, SW], 0), cut([CH, SW])], [cut([CH, SW]), cut([CH, SW])]]
        y = [cut([CH, D]), cut([CH, D])]
        sq = [cut([CH, D]), cut([CH, D])]
        xT, hT, oT = ([cut([STEP * D]) for _ in range(2)] for _ in range(3))
        scratch = sb("scratch", [P, B, D])
        small = sb("small", [P, 2, 10, CH])
        psum = ctx.enter_context(nc.psum_tensor("psum", [P, 8, 512], F32))

        pool_consts = sem("pool_consts")
        cleared = sem("cleared")
        factors_cleared = sem("factors_cleared")
        pool_turns, sp_turns, dve_turns = sem("pool_turns"), sem("sp_turns"), sem("dve_turns")
        edges_in, root_in, spline_in, mlp_in = sem("edges_in"), sem("root_in"), sem("spline_in"), sem("mlp_in")
        nodes_in, last_stored = sem("nodes_in"), sem("last_stored")
        root_ready, keys_ready, setup_steps = sem("root_ready"), sem("keys_ready"), sem("setup_steps")
        zeroed = sem("zeroed")
        x_in = pair("x_in")
        turned, turned_sb, mixed, unmixed = sem("turned"), sem("turned_sb"), sem("mixed"), sem("unmixed")
        rooted = sem("rooted")
        hat_steps, hats_ready = sem("hat_steps"), sem("hats_ready")
        init_stored = pair("init_stored")
        e0 = sem("e0_steps")
        rows_at, keys_at, dst_rows_at = sem("rows_at"), sem("keys_at"), sem("dst_rows_at")
        x_got, st_got = pair("x_got"), pair("st_got")
        z_ready, z_turned, z_turned_sb, y_ready = sem("z_ready"), sem("z_turned"), sem("z_turned_sb"), sem("y_ready")
        y_used, t_ready, t_row, max_ready = sem("y_used"), sem("t_ready"), sem("t_row"), sem("max_ready")
        key_row, apart_ready, same_ready = sem("key_row"), sem("apart_ready"), sem("same_ready")
        expo_in, expo_out, val_ready, sum_ready, st_ready = (sem("expo_in"), sem("expo_out"), sem("val_ready"),
                                                             sem("sum_ready"), sem("st_ready"))
        key_copied, own_ready, count_ready = sem("key_copied"), sem("own_ready"), sem("count_ready")
        first_ready = sem("first_ready")
        st_sent = pair("st_sent")
        ge = [None] + [sem(f"e{l}_steps") for l in (1, 2, 3)]
        g_rows_at, g_keys_at, g_firsts_at = sem("g_rows_at"), sem("g_keys_at"), sem("g_firsts_at")
        g_got, attr_in = pair("g_got"), pair("attr_in")
        g_key_row, g_same, g_sent_in, g_relu, g_sum, g_sum_sb = (sem("g_key_row"), sem("g_same"), sem("g_sent_in"),
                                                                 sem("g_relu"), sem("g_sum"), sem("g_sum_sb"))
        agg_sent = pair("agg_sent")
        n_steps = [sem(f"n{l}_steps") for l in range(4)]
        n_in = pair("n_in")
        n_expo_in, n_expo_out, n_share, n_scaled = sem("n_expo_in"), sem("n_expo_out"), sem("n_share"), sem("n_scaled")
        n_centred, n_squared, n_rstd, n_done = sem("n_centred"), sem("n_squared"), sem("n_rstd"), sem("n_done")
        n_shared, n_added, n_weight_steps = sem("n_shared"), sem("n_added"), sem("n_weight_steps")
        n_var, n_std = sem("n_var"), sem("n_std")
        n_weighted = sem("n_weighted")
        m_h, m_turned, m_turned_sb, m_hid, m_hid_sb, m_out, m_out_sb, m_back, m_back_used = (
            sem("m_h"), sem("m_turned"), sem("m_turned_sb"), sem("m_hid"), sem("m_hid_sb"), sem("m_out"),
            sem("m_out_sb"), sem("m_back"), sem("m_back_used"))
        x_stored, out_stored = pair("x_stored"), pair("out_stored")

        def table(t, width):
            return t[0:NT, :].rearrange("(p c) w -> p (c w)", p=P)

        x_head = x[0:HEAD * COLS, :].rearrange("(p c) w -> p (c w)", p=HEAD)
        x_mid = x[HEAD * COLS:(P - 1) * COLS, :].rearrange("(p c) w -> p (c w)", p=P - 1 - HEAD)
        x_last = x[(P - 1) * COLS:N, :].rearrange("(p c) w -> p (c w)", p=1)
        out_head = out[0:HEAD * COLS, :].rearrange("(p c) w -> p (c w)", p=HEAD)
        out_mid = out[HEAD * COLS:(P - 1) * COLS, :].rearrange("(p c) w -> p (c w)", p=P - 1 - HEAD)
        out_last = out[(P - 1) * COLS:N, :].rearrange("(p c) w -> p (c w)", p=1)
        xs_flat = xs[:, :, :].rearrange("p c w -> p (c w)")

        def bank(b, width=512):
            return psum[:, b, 0:width]

        def sizes(n, c):
            w = min(STEP, n - c) * D
            assert w % P == 0 or w < P
            return min(P, w), -(-w // P) * P

        def cols(i, s):
            return (2 * i + s) * CH

        def chunks(eng, body):
            body(0, 0, CH)
            body(0, 1, CH)
            with eng.Fori(1, HALF - 1) as i:
                body(i, 0, CH)
                body(i, 1, CH)
            body(HALF - 1, 0, CH)
            body(HALF - 1, 1, CH)
            body(HALF, 0, TAIL)

        def before(i, s):
            if isinstance(i, int) and 2 * i + s == 0:
                return None
            return (i, 0, CH) if s else (i - 1, 1, CH)

        def behind(i, s):
            if isinstance(i, int) and i == HALF:
                return None
            if not s:
                return (i, 1, CH)
            return (i + 1, 0, TAIL if isinstance(i, int) and i == HALF - 1 else CH)

        def steps_at(i, s, n, lag):
            per = len(STEPS[0])
            for m in range(len(STEPS[n == TAIL])):
                number = (2 * i + s) * per + m - lag
                if isinstance(number, int) and number < 0:
                    yield None
                elif m >= lag:
                    yield number, (m - lag) % 2, STEPS[0][m - lag], n
                else:
                    yield number, (m - lag) % 2, STEPS[0][m - lag], CH

        def steps_left(lag):
            for m in range(len(STEPS[1]) - lag, len(STEPS[1])):
                number = CHUNKS * len(STEPS[0]) + m
                yield (number, m % 2, STEPS[1][m], TAIL) if m >= 0 else (number, m % 2, STEPS[0][m], CH)

        def groups(eng, body):
            body(0, 0)
            body(0, 1)
            with eng.Fori(1, NG // 2 - 2) as i:
                body(i, 0)
                body(i, 1)
            for i in (NG // 2 - 2, NG // 2 - 1):
                body(i, 0)
                body(i, 1)

        def is_last(i, k, ahead):
            return isinstance(i, int) and 2 * i + k + ahead >= NG

        ZERO_GROUPS = RT // P // ZERO_COLS
        ZERO_REST = RT // P - ZERO_GROUPS * ZERO_COLS

        def transferred(l, i, k):
            ends = l + (isinstance(i, int) and i == NG // 2)
            return 16 * (G * (l * (NG // 2) + i) - k * UNUSED * ends)

        def after_zeroing(eng):
            eng.wait_ge(zeroed, 16 * 3 * (ZERO_GROUPS + (ZERO_REST > 0)))

        def after_initial(eng):
            for s in range(2):
                eng.wait_ge(init_stored[s], 32 * SLOT_USES[s] + 32 * (1 - s))

        def after_states(eng):
            for k in range(2):
                eng.wait_ge(st_sent[k], transferred(0, NG // 2, k))

        def after_nodes(eng, l):
            for s in range(2):
                eng.wait_ge(x_stored[s], 16 * SLOT_USES[s] * (l + 1))

        def after_edges(eng, l):
            for k in range(2):
                eng.wait_ge(agg_sent[k], transferred(l - 1, NG // 2, k))

        def loaded(l, i, s):
            if l == 0:
                return 32 * (i + 1)
            return 32 * SLOT_USES[s] + 16 * ((l - 1) * SLOT_USES[s] + i + 1)

        def last_cols(i, s):
            return max(0, min(CH, LASTP - (2 * i + s) * CH)) if isinstance(i, int) else CH

        assert (2 * HALF - 2) * CH <= LASTP < CHUNKS * CH

        def x_loaded(i, s):
            if not isinstance(i, int):
                return 48 * (i + 1)
            return sum(48 if last_cols(m, s) else 32 for m in range(i + 1))

        def in_layer(l, i, s):
            return l * (CHUNKS + 1) + 2 * i + s

        def beside(l, i, s):
            return in_layer(max(l - 1, 0), i, s)

        def attr_loaded(i, k):
            return 16 * (i + 1) + 16 * is_last(i, k, 1)

        E0_STEPS = 12
        N_STEPS = 2
        WEIGHT_STEPS = 7

        block = ctx.enter_context(nc.Block())

        @block.sync
        def _(sp):
            sp.wait_ge(cleared, 1)
            for j in range(B):
                sp.dma_start(root[j * D:(j + 1) * D, j * D:(j + 1) * D], root_w).then_inc(root_in, 16)
            sp.dma_start(att1[:, :], att_w[0:D].rearrange("(a o) -> a o", a=1).to_broadcast([P, D])).then_inc(root_in, 16)
            sp.dma_start(bias_b[:, :], bias.rearrange("(a o) -> a o", a=1).to_broadcast([P, D])).then_inc(root_in, 16)

            def load_x(i, s, n):
                wait(sp, turned, (2 * i + s - 1) * len(STEPS[0]))
                sp.sem_inc(sp_turns, 1)
                wait(sp, x_in[s], x_loaded(i - 1, s))
                c = cols(i, s) * D
                to = y[s].rearrange("p c w -> p (c w)")
                sp.dma_start(to[0:HEAD, 0:n * D], x_head[:, ds(c, n * D)]).then_inc(x_in[s], 16)
                sp.dma_start(to[HEAD:P - 1, 0:n * D], x_mid[:, ds(c, n * D)]).then_inc(x_in[s], 16)
                have = last_cols(i, s)
                if have:
                    sp.dma_start(to[P - 1:P, 0:have * D], x_last[:, ds(c, have * D)]).then_inc(x_in[s], 16)

            def load_edges():
                for row, to in ((src, src_row), (dst, dst_row)):
                    sp.dma_start(to[:, 0:MAIN], row[0:MAIN * P].rearrange("(p t) -> p t", p=P)).then_inc(edges_in, 16)
                    sp.dma_start(to[0:REST, MAIN:MAIN + 1],
                                 row[MAIN * P:E].rearrange("(p t) -> p t", t=1)).then_inc(edges_in, 16)
                sp.dma_start(attr2[:, 0:MAIN, :].rearrange("p t a -> p (t a)"),
                             edge_attr_2[0:MAIN * P, :].rearrange("(p t) a -> p (t a)", p=P)).then_inc(edges_in, 16)
                sp.dma_start(attr2[0:REST, MAIN, :], edge_attr_2[MAIN * P:E, :]).then_inc(edges_in, 16)

            def const(to, of, done):
                sp.dma_start(to, of).then_inc(done, 16)

            def load_spline():
                for i in range(K):
                    to = w_a[i * D:(i + 1) * D, :, :] if i < B else w_b[:, :, :]
                    const(to, spline_w.rearrange("(j i) f o -> i f j o", i=K)[i], spline_in)
                const(att2[:, :], att_w[D:2 * D].rearrange("(a o) -> a o", a=1).to_broadcast([P, D]), spline_in)

            def load_mlp():
                for j in range(B):
                    with nc.allow_non_contiguous_dma("small transposed weights"):
                        const(w1[j * D:(j + 1) * D, j * D:(j + 1) * D], gine_w1[LAST].rearrange("o f -> f o"), mlp_in)
                        const(w2[j * D:(j + 1) * D, j * D:(j + 1) * D], gine_w2[LAST].rearrange("o f -> f o"), mlp_in)
                    const(b1[j * D:(j + 1) * D, :], gine_b1[LAST].rearrange("(o a) -> o a", a=1), mlp_in)
                    const(b2[j * D:(j + 1) * D, :], gine_b2[LAST].rearrange("(o a) -> o a", a=1), mlp_in)
                const(eps1[:, :], gine_eps[LAST:LAST + 1].rearrange("(a o) -> a o", a=1).to_broadcast([P, 1]), mlp_in)

            def store_init(i, s, n):
                sp.wait_ge(rooted, 2 * i + s + 1)
                c = cols(i, s) * SW
                for t in range(2):
                    sp.dma_start(table(state[t], SW)[:, ds(c, n * SW)],
                                 node_in[s][0][:, 0:n, :].rearrange("p c w -> p (c w)")).then_inc(init_stored[s], 16)
                    if n == TAIL:
                        sp.dma_start(state[t][NT:RT, :].rearrange("(p c) w -> p (c w)", p=P),
                                     node_in[s][0][:, 0:G, :].rearrange("p c w -> p (c w)")).then_inc(init_stored[s], 16)

            def load_and_store(i, s, n):
                load_x(i, s, n)
                store_init(i - 1, s, CH)

            load_x(0, 0, CH)
            load_x(0, 1, CH)
            load_edges()
            load_spline()
            with sp.Fori(1, HALF - 1) as i:
                load_and_store(i, 0, CH)
                load_and_store(i, 1, CH)
            load_and_store(HALF - 1, 0, CH)
            load_and_store(HALF - 1, 1, CH)
            load_and_store(HALF, 0, TAIL)
            store_init(HALF - 1, 1, CH)
            store_init(HALF, 0, TAIL)
            load_mlp()

            def load_attr(i, k):
                wait(sp, g_relu, 2 * i + k - 1)
                if isinstance(i, int) and (2 * i + k + 1) * G > MAIN:
                    left = MAIN - (2 * i + k) * G
                    sp.dma_start(attr[k][:, 0:left, :], edge_attr_32[0:MAIN * P, :].rearrange(
                        "(p t) w -> p t w", p=P)[:, MAIN - left:MAIN, :]).then_inc(attr_in[k], 16)
                    sp.dma_start(attr[k][0:REST, left, :], edge_attr_32[MAIN * P:E, :]).then_inc(attr_in[k], 16)
                    return
                sp.dma_start(attr[k][:, :, :].rearrange("p t w -> p (t w)"),
                             edge_attr_32[0:MAIN * P, :].rearrange("(p t) w -> p (t w)", p=P)[
                                 :, ds((2 * i + k) * (G * D), G * D)]).then_inc(attr_in[k], 16)

            def load_nodes(l):
                def body(i, s, n):
                    if l == 1:
                        wait(sp, m_h, 2 * i + s - 1)
                    else:
                        wait(sp, n_added, beside(l, i, s) - 1)
                    if l == 0:
                        c = cols(i, s) * SW
                        for t in range(2):
                            sp.dma_start(node_in[s][t][:, 0:n, :].rearrange("p c w -> p (c w)"),
                                         table(state[t], SW)[:, ds(c, n * SW)]).then_inc(n_in[s], 16)
                    else:
                        w = AW if l == 1 else D
                        sp.dma_start(node_in[s][0].rearrange("p c w -> p (c w)")[:, 0:n * w],
                                     table(agg[l], w)[:, ds(cols(i, s) * w, n * w)]).then_inc(n_in[s], 16)
                return body

            def store_nodes(l, i, s, n):
                c = cols(i, s) * D
                if l == 2:
                    sp.wait_ge(n_weighted, 2 * i + s + 1)
                    sp.dma_start(table(xt[3], D)[:, ds(c, n * D)],
                                 node_in[s][1].rearrange("p c w -> p (c w)")[:, 0:n * D]).then_inc(x_stored[s], 16)
                    return
                sp.wait_ge(n_done, in_layer(l, i, s) + 1)
                if l < 3:
                    sp.dma_start(table(xt[l + 1], D)[:, ds(c, n * D)], xs_flat[:, ds(c, n * D)]).then_inc(x_stored[s], 16)
                else:
                    sp.dma_start(out_head[:, ds(c, n * D)], xs_flat[0:HEAD, ds(c, n * D)]).then_inc(out_stored[s], 16)
                    sp.dma_start(out_mid[:, ds(c, n * D)], xs_flat[HEAD:P - 1, ds(c, n * D)]).then_inc(out_stored[s], 16)

            def nodes(l):
                load = load_nodes(l)
                for i in range(2):
                    for s in range(2):
                        load(i, s, CH)
                with sp.Fori(2, HALF) as i:
                    for s in range(2):
                        load(i, s, CH)
                        store_nodes(l, i - 2, s, CH)
                load(HALF, 0, TAIL)
                for i in (HALF - 2, HALF - 1):
                    for s in range(2):
                        store_nodes(l, i, s, CH)
                store_nodes(l, HALF, 0, TAIL)

            def clear(first, n):
                for t in agg[1:]:
                    w = t.shape[1]
                    sp.dma_start(t.rearrange("(p c) w -> p (c w)", p=P)[:, ds(first * w, n * w)],
                                 zeros[:, 0:n * w]).then_inc(zeroed, 16)

            after_initial(sp)
            with sp.Fori(0, ZERO_GROUPS) as i:
                sp.wait_ge(z_ready, i + 1)
                sp.sem_inc(sp_turns, 1)
                clear(i * ZERO_COLS, ZERO_COLS)
            if ZERO_REST:
                clear(ZERO_GROUPS * ZERO_COLS, ZERO_REST)
            after_states(sp)
            nodes(0)
            sp.wait_ge(factors_cleared, 1)
            for v, to in ((node_vec1, cj), (node_vec1_n2, ci)):
                for a, b in ((0, HEAD), (HEAD, P - 1)):
                    sp.dma_start(to[a:b, :],
                                 v[a * COLS:b * COLS, :].rearrange("(p c) a -> p (c a)", p=b - a)).then_inc(nodes_in, 16)
                sp.dma_start(to[P - 1:P, 0:LASTP],
                             v[(P - 1) * COLS:N, :].rearrange("(p c) a -> p (c a)", p=1)).then_inc(nodes_in, 16)
            groups(sp, load_attr)
            for l in (1, 2, 3):
                after_edges(sp, l)
                nodes(l)
            sp.dma_start(out_last, xs_flat[P - 1:P, 0:LASTP * D]).then_inc(last_stored, 16)
            for s in range(2):
                sp.wait_ge(out_stored[s], 32 * SLOT_USES[s])
            sp.wait_ge(last_stored, 16)

        @block.gpsimd
        def _(pool):
            nc.gpsimd.memset(ident[:, :], 0.0)
            nc.gpsimd.memset(earlier[:, :], 1.0).then_inc(pool_consts, 1)
            nc.gpsimd.iota(spare_i[:, :], [[P, G]], base=TRASH, channel_multiplier=1)
            pool.wait_ge(pool_consts, 1)
            nc.gpsimd.affine_select(out=ident[:, :], in_=ident[:, :], compare_op=ALU.not_equal, fill=1.0,
                                    base=0, pattern=[[-1, P]], channel_multiplier=1)
            nc.gpsimd.affine_select(out=earlier[:, ROW - P:ROW], in_=earlier[:, ROW - P:ROW], compare_op=ALU.is_gt,
                                    fill=0.0, base=0, pattern=[[-1, P]], channel_multiplier=1)
            nc.gpsimd.affine_select(out=key_sb[:, 0:P], in_=earlier[:, 0:P], compare_op=ALU.is_gt,
                                    fill=0.0, base=0, pattern=[[1, P]], channel_multiplier=-1).then_inc(pool_consts, 1)

            def tiles_of(i, k):
                return range(G - UNUSED if is_last(i, k, 1) else G)

            def gather(i, k, to, of, rows, done):
                pool.sem_inc(pool_turns, 1)
                for t in tiles_of(i, k):
                    nc.gpsimd.indirect_dma_start(to[:, t, :], None, of, bass.IndirectOffsetOnAxis(rows[:, t:t + 1], 0),
                                                 bounds_check=of.shape[0] - 1, oob_is_err=True).then_inc(done, 16)

            def scatter(i, k, to, rows, of, done, **add):
                pool.sem_inc(pool_turns, 1)
                for t in tiles_of(i, k):
                    nc.gpsimd.indirect_dma_start(to, bass.IndirectOffsetOnAxis(rows[:, t:t + 1], 0), of[:, t, :], None,
                                                 bounds_check=RT - 1, oob_is_err=True, **add).then_inc(done, 16)

            def knot_weights():
                hats = Chain(pool, hat_steps, 0)
                above, below = (t.rearrange("p c w -> p (c w)")[:, 0:TILES * (K - 2)].rearrange(
                    "p (t n) -> p t n", n=K - 2) for t in sq)

                def scaled(out, of, a, b, *ops):
                    hats.step(nc.gpsimd.tensor_scalar(out, of, a, b, *ops))

                scaled(attr2[:, :, :], attr2[:, :, :], float(K - 1), 0.0, ALU.mult, ALU.max)
                hats.wait()
                scaled(attr2[:, :, :], attr2[:, :, :], float(K - 1), None, ALU.min)
                for d in range(2):
                    hats.wait()
                    for n in range(K - 1):
                        scaled(above[:, :, n] if n < K - 2 else hat[d][:, :, K - 1], attr2[:, :, d],
                               -float(n), 0.0, ALU.add, ALU.max)
                    hats.wait()
                    scaled(above, above, 1.0, None, ALU.min)
                    scaled(hat[d][:, :, K - 1], hat[d][:, :, K - 1], 1.0, None, ALU.min)
                    hats.wait()
                    scaled(hat[d][:, :, 0], above[:, :, 0], -1.0, 1.0, ALU.mult, ALU.add)
                    scaled(below[:, :, 0:K - 3], above[:, :, 1:K - 2], -1.0, 1.0, ALU.mult, ALU.add)
                    scaled(below[:, :, K - 3], hat[d][:, :, K - 1], -1.0, 1.0, ALU.mult, ALU.add)
                    hats.wait()
                    hats.step(nc.gpsimd.tensor_tensor(hat[d][:, :, 1:K - 1], above, below, ALU.mult))
                hats.wait()
                pool.sem_inc(hats_ready, 1)

            def gather_x(i, k):
                gather(i, k, xg[k], xt[0], dst_at[k], x_got[k])

            def send_states(i, k):
                pool.wait_ge(st_ready, 2 * i + k + 1)
                pool.wait_ge(first_ready, 2 * i + k + 1)
                scatter(i, k, state[k], first_at[k], st_new[k], st_sent[k])

            def body0(i, k):
                pool.wait_ge(rows_at, 2 * i + k + 1)
                wait(pool, st_sent[k], transferred(0, i, k))
                gather(i, k, st[k], state[k], src_at[k], st_got[k])
                if not (isinstance(i, int) and 2 * i + k == 0):
                    send_states(i - 1 + k, 1 - k)
                for ahead in (2, 3) if isinstance(i, int) and 2 * i + k == 0 else (3,):
                    if not is_last(i, k, ahead):
                        pool.wait_ge(dst_rows_at, 2 * i + k + ahead + 1)
                        pool.wait_ge(z_ready, 2 * i + k + ahead - 1)
                        gather_x(i + (k + ahead) // 2, (k + ahead) % 2)

            for k in range(2):
                pool.wait_ge(dst_rows_at, k + 1)
                gather_x(0, k)
            knot_weights()
            after_initial(pool)
            groups(pool, body0)
            send_states(NG // 2 - 1, 1)

            def nodes(l):
                def flat(t, n):
                    return t.rearrange("p c w -> p (c w)")[:, 0:n * D].rearrange("p (c w) -> p c w", w=D)

                def factor(f, n):
                    return f.unsqueeze(2).to_broadcast([P, n, D])

                def scale(i, s, n):
                    if l == 0:
                        pool.wait_ge(n_share, 2 * i + s + 1)
                        v, f = node_in[s][1][:, 0:n, 2:2 + D], small[:, s, 3, 0:n]
                    else:
                        pool.wait_ge(n_in[s], loaded(l, i, s))
                        v, f = flat(node_in[s][0], n), (deg if l == 2 else ci)[:, ds(cols(i, s), n)]
                    ins = nc.gpsimd.tensor_tensor(v, v, factor(f, n), ALU.mult)
                    if l == 0:
                        ins.then_inc(n_shared, 1)
                        pool.wait_ge(n_shared, 2 * i + s + 1)
                        pool.sem_inc(pool_turns, 1)
                        ins = nc.gpsimd.tensor_tensor(v, v, xs[:, ds(cols(i, s), n), :], ALU.add)
                    ins.then_inc(n_scaled, 1)

                def finish(i, s, n):
                    x_now = xs[:, ds(cols(i, s), n), :]
                    pool.wait_ge(n_rstd, in_layer(l, i, s) + 1)
                    pool.sem_inc(pool_turns, 1)
                    nc.gpsimd.tensor_tensor(x_now, y[s][:, 0:n, :], factor(small[:, s, 7, 0:n], n),
                                            ALU.mult).then_inc(n_done, 1)
                    if l == 2:
                        pool.wait_ge(n_done, in_layer(l, i, s) + 1)
                        wait(pool, x_stored[s], 16 * (2 * SLOT_USES[s] + i))
                        nc.gpsimd.tensor_tensor(flat(node_in[s][1], n), x_now, factor(cj[:, ds(cols(i, s), n)], n),
                                                ALU.mult).then_inc(n_weighted, 1)

                def body(i, s, n):
                    if l != 1 and behind(i, s):
                        scale(*behind(i, s))
                    if before(i, s):
                        finish(*before(i, s))

                if l == 2:
                    pool.wait_ge(n_share, CHUNKS + 2)
                if l != 1:
                    scale(0, 0, CH)
                chunks(pool, body)
                finish(HALF, 0, TAIL)

            nodes(0)

            def edges(l):
                def get(i, k):
                    pool.wait_ge(g_rows_at, (l - 1) * NG + 2 * i + k + 1)
                    gather(i, k, xg[k], xt[l], src_at[k], g_got[k])

                def body(i, k):
                    g = (l - 1) * NG + 2 * i + k
                    pool.wait_ge(g_sum_sb, g + 1)
                    pool.wait_ge(g_firsts_at, g + 1)
                    wait(pool, agg_sent[1 - k], transferred(l - 1, i + k, 1 - k))
                    scatter(i, k, agg[l], first_at[k], sums[k][:, :, 0:AW if l == 1 else D], agg_sent[k], compute_op=ALU.add)
                    if not is_last(i, k, 2):
                        get(i + 1, k)

                after_nodes(pool, l - 1)
                if l == 1:
                    after_zeroing(pool)
                get(0, 0)
                get(0, 1)
                groups(pool, body)

            for l in (1, 2, 3):
                edges(l)
                after_edges(pool, l)
                if l == 2:
                    pool.wait_ge(nodes_in, 16 * 6)
                nodes(l)

        @block.scalar
        def _(act):
            copy = nc.scalar.copy

            def turned_x(i, s, n):
                for step, k, c, n in steps_at(i, s, n, 0):
                    rows, wide = sizes(n, c)
                    act.wait_ge(turned, step + 1)
                    wait(act, mixed, step - 1)
                    copy(xT[k][0:rows, 0:wide], psum[0:rows, k, 0:wide]).then_inc(turned_sb, 1)

            act.wait_ge(keys_ready, 1)

            def stage_dst(i, k):
                copy(dst_at[k][:, :], dst_row[:, ds((2 * i + k) * G, G)]).then_inc(dst_rows_at, 1)

            def stage_keys(i, k, key, done):
                copy(key_at[k][:, :], key[:, ds((2 * i + k) * G, G)]).then_inc(done, 1)

            def stage_src(i, k, done):
                copy(src_at[k][:, :], src_row[:, ds((2 * i + k) * G, G)]).then_inc(done, 1)

            for k in range(2):
                stage_dst(0, k)
                stage_keys(0, k, src_key, keys_at)
                stage_src(0, k, rows_at)
            chunks(act, turned_x)

            def turned0(i, k):
                g = 2 * i + k
                act.wait_ge(z_turned, g + 1)
                wait(act, y_ready, g)
                copy(zt_a, bank(2))
                copy(zt_b[0:D, :], psum[0:D, 3, :]).then_inc(z_turned_sb, 1)

            def key_row0(i, k):
                g = 2 * i + k
                act.wait_ge(key_row, g + 1)
                wait(act, apart_ready, g)
                copy(key_sb, bank(0)).then_inc(key_copied, 1)

            def same0(i, k):
                g = 2 * i + k
                act.wait_ge(apart_ready, g + 1)
                wait(act, sum_ready, g - 1)
                for a in range(G):
                    last = nc.scalar.activation(same16[k][:, a, :], apart[:, a, :],
                                                ACT.Identity, bias=one[:, 0:1], scale=-1.0 / NEG_BIG)
                last.then_inc(same_ready, 1)

            def body0(i, k):
                g = 2 * i + k
                if not is_last(i, k, 3):
                    act.wait_ge(z_ready, g + 2)
                    stage_dst(i + 1 + k, 1 - k)
                if not is_last(i, k, 2):
                    act.wait_ge(apart_ready, g + 1)
                    act.wait_ge(key_row, g + 1)
                    stage_keys(i + 1, k, src_key, keys_at)
                if not is_last(i, k, 2):
                    turned0(i + 1, k)
                act.wait_ge(expo_in, g + 1)
                nc.scalar.activation(expo[k][:, :, :], expo[k][:, :, :], ACT.Exp).then_inc(expo_out, 1)
                if not is_last(i, k, 2):
                    stage_src(i + 1, k, rows_at)
                if not is_last(i, k, 1):
                    same0(i + k, 1 - k)
                if not is_last(i, k, 2):
                    key_row0(i + 1, k)

            turned0(0, 0)
            key_row0(0, 0)
            act.wait_ge(z_ready, 1)
            stage_dst(1, 0)
            turned0(0, 1)
            same0(0, 0)
            key_row0(0, 1)
            groups(act, body0)

            def nodes(l):
                def square(i, s, n):
                    q = in_layer(l, i, s)
                    act.wait_ge(n_centred, q + 1)
                    wait(act, n_var, q - 1)
                    nc.scalar.activation(sq[s][:, 0:n, :], y[s][:, 0:n, :], ACT.Square, scale=D ** -0.5).then_inc(n_squared, 1)

                def deviation(i, s, n):
                    act.wait_ge(n_var, in_layer(l, i, s) + 1)
                    nc.scalar.activation(small[:, s, 7, 0:n], small[:, s, 6, 0:n], ACT.Sqrt,
                                         bias=ln_eps[:, 0:1]).then_inc(n_std, 1)

                def turn(step, k, c, n):
                    rows, wide = sizes(n, c)
                    act.wait_ge(m_turned, step + 1)
                    wait(act, m_hid, step - 1)
                    copy(xT[k][0:rows, 0:wide], psum[0:rows, k, 0:wide]).then_inc(m_turned_sb, 1)

                def hidden(step, k, c, n):
                    rows, wide = sizes(n, c)
                    act.wait_ge(m_hid, step + 1)
                    wait(act, m_out, step - 1)
                    nc.scalar.activation(hT[k][0:rows, 0:wide], psum[0:rows, 2 + k, 0:wide], ACT.Relu,
                                         bias=b1[0:rows, 0:1]).then_inc(m_hid_sb, 1)

                def result(step, k, c, n):
                    rows, wide = sizes(n, c)
                    act.wait_ge(m_out, step + 1)
                    wait(act, m_back, step - 1)
                    nc.scalar.activation(oT[k][0:rows, 0:wide], psum[0:rows, 4 + k, 0:wide], ACT.Relu,
                                         bias=b2[0:rows, 0:1]).then_inc(m_out_sb, 1)

                def exponentials(i, s, n):
                    act.wait_ge(n_expo_in, 2 * i + s + 1)
                    v = small[:, s, 0:2, 0:n]
                    nc.scalar.activation(v, v, ACT.Exp).then_inc(n_expo_out, 1)

                def body(i, s, n):
                    if l == 0 and behind(i, s):
                        exponentials(*behind(i, s))
                    if before(i, s):
                        deviation(*before(i, s))
                    square(i, s, n)

                def body_mlp(i, s, n):
                    two = before(i, s) and before(*before(i, s)[:2])
                    for m, (a, b, c) in enumerate(zip(*(steps_at(i, s, n, lag) for lag in range(3)))):
                        turn(*a)
                        if b:
                            hidden(*b)
                        if c:
                            result(*c)
                        if m == min(2, len(STEPS[n == TAIL]) - 1) and two:
                            square(*two)
                    if two:
                        deviation(*two)

                if l == 1:
                    chunks(act, body_mlp)
                    for step in steps_left(1):
                        hidden(*step)
                    for step in steps_left(2):
                        result(*step)
                    for q in ((HALF - 1, 1, CH), (HALF, 0, TAIL)):
                        square(*q)
                        deviation(*q)
                else:
                    if l == 0:
                        exponentials(0, 0, CH)
                    chunks(act, body)
                    deviation(HALF, 0, TAIL)

            after_states(act)
            act.wait_ge(mlp_in, 16 * (4 * B + 1))
            nodes(0)

            def edges(l):
                def prepare(i, k):
                    stage_src(i, k, g_rows_at)
                    stage_keys(i, k, dst_key, g_keys_at)

                def body(i, k):
                    g = (l - 1) * NG + 2 * i + k
                    act.wait_ge(g_got[k], transferred(l - 1, i + 1, k))
                    if not is_last(i, k, 2):
                        act.wait_ge(g_key_row, g + 1)
                        act.wait_ge(g_same, g + 1)
                        prepare(i + 1, k)
                    if l == 1:
                        act.wait_ge(g_sent_in, g + 1)
                        wait(act, g_sum, g - 1)
                        nc.scalar.activation(val[k][:, :, 0:D], xg[k][:, :, :], ACT.Relu).then_inc(g_relu, 1)
                    wait(act, agg_sent[k], transferred(l - 1, i, k))
                    if l > 1:
                        copy(first_at[k][:, :], dst_first[:, ds((2 * i + k) * G, G)]).then_inc(g_firsts_at, 1)
                    act.wait_ge(g_sum, g + 1)
                    w = AW if l == 1 else D
                    copy(sums[k][:, :, 0:w], bank(6 + k, G * w).rearrange("p (t w) -> p t w", w=w)).then_inc(g_sum_sb, 1)

                after_nodes(act, l - 1)
                prepare(0, 0)
                prepare(0, 1)
                groups(act, body)

            for l in (1, 2, 3):
                edges(l)
                after_edges(act, l)
                nodes(l)

        @block.tensor
        def _(pe):
            pe.wait_ge(pool_consts, 2)
            pe.wait_ge(root_ready, 1)

            def turn_x(step, k, c, n, s):
                rows, wide = sizes(n, c)
                wait(pe, turned_sb, step - 1)
                for b in range(0, wide, P):
                    last = nc.tensor.transpose(psum[0:rows, k, b:b + P],
                                               y[s].rearrange("p c w -> p (c w)")[:, c * D + b:c * D + b + rows],
                                               ident[:, :])
                last.then_inc(turned, 1)

            def mix_x(step, k, c, n):
                rows, wide = sizes(n, c)
                pe.wait_ge(turned_sb, step + 1)
                wait(pe, unmixed, step - 1)
                for b in range(0, wide, P):
                    o = psum[:, 2 + k, b // P * (P + B):(b // P + 1) * (P + B)]
                    last = nc.tensor.matmul(o, xT[k][0:rows, b:b + P], root[0:rows, :], start=True, stop=True)
                last.then_inc(mixed, 1)

            def body_x(i, s, n):
                pe.wait_ge(x_in[s], x_loaded(i, s))
                for a, b in zip(steps_at(i, s, n, 0), steps_at(i, s, n, 1)):
                    turn_x(*a, s)
                    if b:
                        mix_x(*b)

            chunks(pe, body_x)
            for step in steps_left(1):
                mix_x(*step)

            def rows_of(to, column):
                for t in range(G):
                    last = nc.tensor.transpose(to[:, t * P:(t + 1) * P], column[:, t:t + 1].to_broadcast([P, P]),
                                               ident[:, :])
                return last

            def keys0(i, k):
                g = 2 * i + k
                pe.wait_ge(keys_at, g + 1)
                wait(pe, key_copied, g)
                rows_of(bank(0), key_at[k]).then_inc(key_row, 1)

            def turn0(i, k):
                g = 2 * i + k
                pe.wait_ge(z_ready, g + 1)
                wait(pe, z_turned_sb, g)
                for t in range(G):
                    nc.tensor.transpose(psum[:, 2, t * P:(t + 1) * P],
                                        z[:, t, 0:B, :].rearrange("p k d -> p (k d)"), ident[:, :])
                    last = nc.tensor.transpose(psum[0:D, 3, t * P:(t + 1) * P], z[:, t, B, :], ident[:, :])
                last.then_inc(z_turned, 1)

            def spline0(i, k):
                g = 2 * i + k
                pe.wait_ge(z_turned_sb, g + 1)
                wait(pe, y_used, g)
                for t in range(G):
                    o = psum[:, 4 + t // 2, t % 2 * K * D:(t % 2 + 1) * K * D]
                    nc.tensor.matmul(o, zt_a[:, t * P:(t + 1) * P], w_a[:, :, :].rearrange("p j o -> p (j o)"),
                                     start=True, stop=False)
                    last = nc.tensor.matmul(o, zt_b[0:D, t * P:(t + 1) * P],
                                            w_b[:, :, :].rearrange("p j o -> p (j o)"), start=False, stop=True)
                last.then_inc(y_ready, 1)

            def logits0(i, k):
                g = 2 * i + k
                pe.wait_ge(t_ready, g + 1)
                wait(pe, max_ready, g)
                rows_of(bank(1), tmax[k][:, 0, :]).then_inc(t_row, 1)

            def count0(i, k):
                g = 2 * i + k
                pe.wait_ge(own_ready, g + 1)
                wait(pe, st_ready, g - 1)
                for a in range(G):
                    o = psum[:, 6 + k, 500 + a:501 + a]
                    for b in range(a):
                        nc.tensor.matmul(o, same16[k][:, b, a * P:(a + 1) * P], one16[:, :], start=(b == 0), stop=False)
                    last = nc.tensor.matmul(o, own[:, a, :], one16[:, :], start=(a == 0), stop=True)
                last.then_inc(count_ready, 1)

            def sum_shared(k, matrices, v, w, done):
                for a in range(G):
                    for b in range(a, G):
                        last = nc.tensor.matmul(psum[:, 6 + k, a * w:(a + 1) * w], matrices[:, b, a * P:(a + 1) * P],
                                                v(b), start=(b == a), stop=(b == G - 1))
                last.then_inc(done, 1)

            def sum0(i, k):
                g = 2 * i + k
                pe.wait_ge(val_ready, g + 1)
                pe.wait_ge(same_ready, g + 1)
                pe.wait_ge(first_ready, g + 1)
                sum_shared(k, same16[k], lambda b: parts[:, b, :, :].rearrange("p c w -> p (c w)"),
                           PARTS * AW, sum_ready)

            def body0(i, k):
                if not is_last(i, k, 2):
                    turn0(i + 1, k)
                if not is_last(i, k, 1):
                    logits0(i + k, 1 - k)
                if not is_last(i, k, 2):
                    spline0(i + 1, k)
                sum0(i, k)
                if not is_last(i, k, 1):
                    count0(i + k, 1 - k)
                if not is_last(i, k, 2):
                    keys0(i + 1, k)

            keys0(0, 0)
            turn0(0, 0)
            pe.wait_ge(spline_in, 16 * (K + 1))
            spline0(0, 0)
            turn0(0, 1)
            logits0(0, 0)
            spline0(0, 1)
            count0(0, 0)
            keys0(0, 1)
            groups(pe, body0)

            def edges(l):
                def prepare(i, k):
                    g = (l - 1) * NG + 2 * i + k
                    pe.wait_ge(g_keys_at, g + 1)
                    wait(pe, g_same, g - 1)
                    rows_of(bank(k), key_at[k]).then_inc(g_key_row, 1)

                def body(i, k):
                    g = (l - 1) * NG + 2 * i + k
                    if not is_last(i, k, 1):
                        prepare(i + k, 1 - k)
                    pe.wait_ge(g_same, g + 1)
                    if l == 1:
                        pe.wait_ge(g_relu, g + 1)
                    else:
                        pe.wait_ge(g_got[k], transferred(l - 1, i + 1, k))
                    wait(pe, g_sum_sb, g - 1)
                    of = val[k] if l == 1 else xg[k]
                    sum_shared(k, same[k], lambda b: of[:, b, :], AW if l == 1 else D, g_sum)

                after_nodes(pe, l - 1)
                prepare(0, 0)
                groups(pe, body)

            def turn(step, k, c, n, s):
                rows, wide = sizes(n, c)
                wait(pe, m_turned_sb, step - 1)
                for b in range(0, wide, P):
                    last = nc.tensor.transpose(
                        psum[0:rows, k, b:b + P],
                        node_in[s][1].rearrange("p c w -> p (c w)")[:, c * D + b:c * D + b + rows], ident[:, :])
                last.then_inc(m_turned, 1)

            def hidden(step, k, c, n):
                rows, wide = sizes(n, c)
                pe.wait_ge(m_turned_sb, step + 1)
                wait(pe, m_hid_sb, step - 1)
                nc.tensor.matmul(psum[0:rows, 2 + k, 0:wide], w1[0:rows, 0:rows], xT[k][0:rows, 0:wide],
                                 start=True, stop=True).then_inc(m_hid, 1)

            def result(step, k, c, n):
                rows, wide = sizes(n, c)
                pe.wait_ge(m_hid_sb, step + 1)
                wait(pe, m_out_sb, step - 1)
                nc.tensor.matmul(psum[0:rows, 4 + k, 0:wide], w2[0:rows, 0:rows], hT[k][0:rows, 0:wide],
                                 start=True, stop=True).then_inc(m_out, 1)

            def turn_back(step, k, c, n):
                rows, wide = sizes(n, c)
                pe.wait_ge(m_out_sb, step + 1)
                wait(pe, m_back_used, step - 1)
                for b in range(0, wide, P):
                    last = nc.tensor.transpose(psum[:, 6 + k, b:b + rows], oT[k][0:rows, b:b + P],
                                               ident[0:rows, 0:rows])
                last.then_inc(m_back, 1)

            def mlp(i, s, n):
                pe.wait_ge(m_h, 2 * i + s + 1)
                for a, *rest in zip(*(steps_at(i, s, n, lag) for lag in range(4))):
                    turn(*a, s)
                    for stage, b in zip((hidden, result, turn_back), rest):
                        if b:
                            stage(*b)

            for l in (1, 2, 3):
                edges(l)
                if l == 1:
                    after_edges(pe, 1)
                    pe.wait_ge(mlp_in, 16 * (4 * B + 1))
                    chunks(pe, mlp)
                    for a, b, c in zip_longest(*(steps_left(lag) for lag in (1, 2, 3))):
                        if a:
                            hidden(*a)
                        if b:
                            result(*b)
                        turn_back(*c)

        @block.vector
        def _(dve):
            v = nc.vector
            begin = Chain(dve, setup_steps, 0)

            def link(ins):
                begin.step(ins)
                begin.wait()

            v.memset(src_row[:, MAIN:TILES], -1)
            v.memset(dst_row[:, MAIN:TILES], -1)
            for t in (root, w1, w2):
                v.memset(t[:, :], 0.0)
            v.memset(attr2[:, MAIN:TILES, :], 0.0).then_inc(cleared, 1)
            for s in range(2):
                link(v.memset(node_in[s][0], 0.0))
                link(v.memset(node_in[s][0][:, :, 1], NEG_BIG))
            dve.wait_ge(root_in, 16 * (B + 2))
            dve.wait_ge(pool_consts, 2)
            link(v.tensor_tensor(scratch[:, :, :], root[:, 0:P].rearrange("p (a b) -> p a b", a=B),
                                 att1[:, :].unsqueeze(1).to_broadcast([P, B, D]), ALU.mult))
            link(v.tensor_reduce(root[:, P:P + B], scratch[:, :, :], AX_X, ALU.add))
            link(v.tensor_tensor(root[:, 0:P], root[:, 0:P], ident[:, :], ALU.add))
            dve.sem_inc(root_ready, 1)
            dve.wait_ge(edges_in, 16 * 6)
            for row, key in ((src_row, src_key), (dst_row, dst_key)):
                v.tensor_copy(key[:, :], row[:, :])
            link(v.tensor_copy(spare[:, :], spare_i[:, :]))
            for row, key in ((src_row, src_key), (dst_row, dst_key)):
                v.tensor_scalar(row[:, :], key[:, :], 0.0, None, ALU.max)
            v.memset(one[:, :], 1.0)
            v.memset(ln_eps[:, :], LN_EPS)
            v.memset(one16[:, :], 1.0)
            link(v.tensor_copy(earlier_own[:, :], key_sb[:, 0:P]))
            for key, rel in ((src_key, src_rel), (dst_key, dst_rel)):
                link(v.tensor_tensor(rel[:, :].rearrange("p (n t) -> p n t", t=G),
                                     key[:, :].rearrange("p (n t) -> p n t", t=G),
                                     spare[:, :].unsqueeze(1).to_broadcast([P, NG, G]), ALU.subtract))
                link(v.scalar_tensor_tensor(out=rel[:, :], in0=key[:, :], scalar=0.0, in1=rel[:, :],
                                            op0=ALU.is_ge, op1=ALU.mult))
            dve.sem_inc(keys_ready, 1)

            def root_body(i, s, n):
                wait(dve, init_stored[s], 32 * i)
                for step, k, c, n in steps_at(i, s, n, 0):
                    w = min(STEP, n - c)
                    nb, per = -(-w // B), min(B, w)
                    dve.wait_ge(mixed, step + 1)
                    o = psum[:, 2 + k, 0:nb * (P + B)].rearrange("p (b f) -> p b f", f=P + B)
                    v.tensor_tensor(
                        xs[:, ds(cols(i, s) + c, w), :].rearrange("p (b a) d -> p b a d", b=nb),
                        o[:, :, 0:per * D].rearrange("p b (a d) -> p b a d", d=D),
                        bias_b[:, :].unsqueeze(1).unsqueeze(1).to_broadcast([P, nb, per, D]), ALU.add)
                    v.tensor_copy(node_in[s][0][:, c:c + w, 0].rearrange("p (b a) -> p b a", b=nb),
                                  o[:, :, P:P + per]).then_inc(unmixed, 1)
                dve.wait_ge(unmixed, step + 1)
                dve.sem_inc(rooted, 1)

            chunks(dve, root_body)

            c = Chain(dve, e0, 0)

            def first_edges(c, k, counts, rel, to, done):
                c.step(v.scalar_tensor_tensor(out=count[k][:, :], in0=counts, scalar=0.0, in1=rel,
                                              op0=ALU.is_equal, op1=ALU.mult))
                c.wait()
                for t in to[1:]:
                    v.tensor_tensor(t, count[k][:, :], spare[:, :], ALU.add)
                v.tensor_tensor(to[0], count[k][:, :], spare[:, :], ALU.add).then_inc(done, 1)

            def count_earlier(c, k):
                for a in range(G):
                    w = (a + 1) * P
                    at = a * (a + 1) // 2 * P
                    last = v.tensor_tensor_reduce(out=products[:, at:at + w], in0=same[k][:, a, 0:w],
                                                  in1=earlier[:, ROW - w:ROW], scale=1.0, scalar=0.0,
                                                  op0=ALU.mult, op1=ALU.add, accum_out=count[k][:, a:a + 1])
                c.step(last)

            def knots0(i, k):
                g = 2 * i + k
                dve.wait_ge(x_got[k], transferred(0, i + 1, k))
                wait(dve, z_turned, g)
                h = hat[0][:, ds(g * G, G), :]
                v.tensor_tensor(z, xg[k][:, :, :].unsqueeze(2).to_broadcast([P, G, K, D]),
                                h.unsqueeze(3).to_broadcast([P, G, K, D]), ALU.mult).then_inc(z_ready, 1)

            def apart0(i, k):
                g = 2 * i + k
                dve.wait_ge(key_copied, g + 1)
                wait(dve, same_ready, g)
                for a in range(G):
                    last = v.tensor_scalar(apart[:, a, :], key_sb, key_at[k][:, a:a + 1], NEG_BIG,
                                           ALU.not_equal, ALU.mult)
                last.then_inc(apart_ready, 1)

            def own0(i, k):
                g = 2 * i + k
                dve.wait_ge(same_ready, g + 1)
                wait(dve, count_ready, g)
                for a in range(G):
                    last = v.tensor_tensor(own[:, a, :], same16[k][:, a, a * P:(a + 1) * P], earlier_own[:, :], ALU.mult)
                last.then_inc(own_ready, 1)

            def message0(i, k):
                g = 2 * i + k
                dve.wait_ge(y_ready, g + 1)
                h = hat[1][:, ds(g * G, G), :]
                for b in range(2):
                    last = v.tensor_tensor(
                        ty[:, 2 * b:2 * b + 2, :, :],
                        psum[:, 4 + b, 0:2 * K * D].rearrange("p (t j o) -> p t j o", t=2, j=K),
                        h[:, 2 * b:2 * b + 2, :].unsqueeze(3).to_broadcast([P, 2, K, D]), ALU.mult)
                last.then_inc(y_used, 1)
                dve.wait_ge(y_used, g + 1)
                c.step(v.tensor_reduce(msg[k][:, :, :], ty.rearrange("p t j o -> p t o j"), AX_X, ALU.add))
                c.wait()
                c.step(v.tensor_tensor(lw, msg[k][:, :, :], att2[:, :].unsqueeze(1).to_broadcast([P, G, D]), ALU.mult))
                c.wait()
                v.tensor_reduce(tmax[k][:, 0, :], lw, AX_X, ALU.add).then_inc(t_ready, 1)

            def first0(i, k):
                dve.wait_ge(count_ready, 2 * i + k + 1)
                wait(dve, st_sent[k], transferred(0, i, k))
                first_edges(c, k, psum[:, 6 + k, 500:500 + G], src_rel[:, ds((2 * i + k) * G, G)],
                            [first_at[k][:, :]], first_ready)

            def max0(i, k):
                for a in range(G):
                    last = v.tensor_tensor_reduce(out=logits16[:, a, :], in0=apart[:, a, :], in1=bank(1), scale=1.0,
                                                  scalar=NEG_BIG, op0=ALU.add, op1=ALU.max,
                                                  accum_out=tmax[k][:, 1, a:a + 1])
                last.then_inc(max_ready, 1)

            def body0(i, k):
                g = 2 * i + k
                ahead = not is_last(i, k, 1)
                j, o = i + k, 1 - k
                c.body(g)
                if not is_last(i, k, 2):
                    knots0(i + 1, k)
                if ahead:
                    message0(j, o)
                first0(i, k)
                dve.wait_ge(st_got[k], transferred(0, i + 1, k))
                dve.wait_ge(max_ready, g + 1)
                u = tmax[k][:, :, :]
                old_max, new_max = st[k][:, :, 1], st_new[k][:, :, 1]
                c.step(v.tensor_tensor(u, u, st[k][:, :, 0].unsqueeze(1).to_broadcast([P, 2, G]), ALU.add))
                c.wait()
                c.step(v.scalar_tensor_tensor(out=u, in0=u, scalar=SLOPE, in1=u, op0=ALU.mult, op1=ALU.max))
                c.wait()
                c.step(v.tensor_tensor(new_max, u[:, 1, :], old_max, ALU.max))
                v.tensor_copy(st_new[k][:, :, 0], st[k][:, :, 0])
                c.wait()
                v.tensor_tensor(expo[k][:, 0, :], u[:, 0, :], new_max, ALU.subtract)
                v.tensor_tensor(expo[k][:, 1, :], old_max, new_max, ALU.subtract).then_inc(expo_in, 1)
                if ahead:
                    apart0(j, o)
                dve.wait_ge(expo_out, g + 1)
                wait(dve, sum_ready, g)
                v.tensor_tensor(val[k][:, :, 0:D], msg[k][:, :, :],
                                expo[k][:, 0, :].unsqueeze(2).to_broadcast([P, G, D]), ALU.mult)
                c.step(v.tensor_copy(val[k][:, :, D], expo[k][:, 0, :]))
                c.wait()
                c.step(v.tensor_copy(parts[:, :, 0, :], val[k][:, :, :]))
                c.wait()
                c.step(v.tensor_tensor(rest, val[k][:, :, :], parts[:, :, 0, :], ALU.subtract))
                c.wait()
                c.step(v.tensor_copy(parts[:, :, 1, :], rest))
                c.wait()
                v.tensor_tensor(parts[:, :, 2, :], rest, parts[:, :, 1, :], ALU.subtract).then_inc(val_ready, 1)
                if ahead:
                    dve.wait_ge(t_row, g + 2)
                    dve.wait_ge(max_ready, g + 1)
                c.step(v.tensor_tensor(st_new[k][:, :, 2:SW], st[k][:, :, 2:SW],
                                       expo[k][:, 1, :].unsqueeze(2).to_broadcast([P, G, AW]), ALU.mult))
                if ahead:
                    max0(j, o)
                    own0(j, o)
                dve.wait_ge(sum_ready, g + 1)
                c.step(v.tensor_reduce(rest, bank(6 + k, G * PARTS * AW).rearrange(
                    "p (t c w) -> p t w c", t=G, c=PARTS), AX_X, ALU.add))
                c.wait()
                v.tensor_tensor(st_new[k][:, :, 2:SW], st_new[k][:, :, 2:SW], rest, ALU.add).then_inc(st_ready, 1)
                assert c.n == E0_STEPS or is_last(i, k, 1), c.n

            dve.wait_ge(hats_ready, 1)
            v.memset(zeros, 0.0)
            knots0(0, 0)
            knots0(0, 1)
            dve.wait_ge(spline_in, 16 * (K + 1))
            message0(0, 0)
            after_initial(dve)
            apart0(0, 0)
            own0(0, 0)
            dve.wait_ge(t_row, 1)
            max0(0, 0)
            c.first, c.per = c.n, E0_STEPS
            groups(dve, body0)

            def nodes(l):
                c = Chain(dve, n_steps[l], N_STEPS)
                w = Chain(dve, n_weight_steps, WEIGHT_STEPS)

                def small_of(s, j, n):
                    return small[:, s, j, 0:n]

                def wide(a, n):
                    return a.unsqueeze(2).to_broadcast([P, n, D])

                def x_of(i, s, n):
                    return xs[:, ds(cols(i, s), n), :]

                def maxima(i, s, n):
                    w.body(2 * i + s)
                    a, b = (t[:, 0:n, :] for t in node_in[s])
                    dve.wait_ge(n_in[s], loaded(l, i, s))
                    w.step(v.tensor_tensor(small_of(s, 2, n), a[:, :, 1], b[:, :, 1], ALU.max))
                    w.wait()
                    v.tensor_tensor(small_of(s, 0, n), a[:, :, 1], small_of(s, 2, n), ALU.subtract)
                    v.tensor_tensor(small_of(s, 1, n), b[:, :, 1], small_of(s, 2, n), ALU.subtract).then_inc(n_expo_in, 1)

                def shares(i, s, n):
                    a, b = (t[:, 0:n, :] for t in node_in[s])
                    scale_a, scale_b, den = (small_of(s, j, n) for j in (0, 1, 2))
                    dve.wait_ge(n_expo_out, 2 * i + s + 1)
                    v.tensor_tensor(small_of(s, 8, n), a[:, :, 2 + D], scale_a, ALU.mult)
                    w.step(v.tensor_tensor(small_of(s, 9, n), b[:, :, 2 + D], scale_b, ALU.mult))
                    w.wait()
                    w.step(v.tensor_tensor(den, small_of(s, 8, n), small_of(s, 9, n), ALU.add))
                    w.wait()
                    w.step(v.tensor_scalar(den, den, DEN_EPS, None, ALU.add))
                    w.wait()
                    w.step(v.reciprocal(den, den))
                    w.wait()
                    v.tensor_tensor(small_of(s, 3, n), scale_b, den, ALU.mult).then_inc(n_share, 1)
                    w.step(v.tensor_tensor(small_of(s, 4, n), scale_a, den, ALU.mult))

                def scale_even(i, s, n):
                    w.wait()
                    sums_a = node_in[s][0][:, 0:n, 2:2 + D]
                    w.step(v.tensor_tensor(sums_a, sums_a, wide(small_of(s, 4, n), n), ALU.mult))
                    assert w.n == WEIGHT_STEPS

                def add(i, s, n):
                    dve.wait_ge(n_scaled, beside(l, i, s) + 1)
                    if l == 0:
                        dve.wait_ge(n_weight_steps, WEIGHT_STEPS * (2 * i + s + 1))
                        ins = v.tensor_tensor(x_of(i, s, n), node_in[s][0][:, 0:n, 2:2 + D],
                                              node_in[s][1][:, 0:n, 2:2 + D], ALU.add)
                    else:
                        a = node_in[s][0].rearrange("p c w -> p (c w)")[:, 0:n * D].rearrange("p (c w) -> p c w", w=D)
                        ins = v.tensor_tensor(x_of(i, s, n), a, x_of(i, s, n), ALU.add)
                    ins.then_inc(n_added, 1)

                def add_step(i, s, n, m):
                    steps = list(steps_at(i, s, n, 0))
                    if m < len(steps):
                        step, k, c0, n = steps[m]
                        some = min(STEP, n - c0)
                        x_now = xs[:, ds(cols(i, s) + c0, some), :]
                        dve.wait_ge(m_back, step + 1)
                        v.tensor_tensor(x_now, psum[:, 6 + k, 0:some * D].rearrange("p (c d) -> p c d", d=D),
                                        x_now, ALU.add).then_inc(m_back_used, 1)

                def total(i, s, n):
                    c.body(2 * i + s)
                    if l == 1:
                        dve.wait_ge(m_back_used, NSTEP if n == TAIL else (2 * i + s + 1) * len(STEPS[0]))
                    else:
                        dve.wait_ge(n_added, beside(l, i, s) + 1)
                    dve.sem_inc(dve_turns, 1)
                    c.step(v.tensor_reduce(small_of(s, 5, n), x_of(i, s, n), AX_X, ALU.add))

                def centre(i, s, n):
                    c.wait()
                    c.step(v.tensor_scalar(small_of(s, 5, n), small_of(s, 5, n), 1.0 / D, None, ALU.mult))
                    assert c.n == N_STEPS
                    c.wait()
                    wait(dve, n_done, in_layer(l, i, s) - 1)
                    v.tensor_tensor(y[s][:, 0:n, :], x_of(i, s, n), wide(small_of(s, 5, n), n),
                                    ALU.subtract).then_inc(n_centred, 1)

                def variance(i, s, n):
                    dve.wait_ge(n_squared, in_layer(l, i, s) + 1)
                    v.tensor_reduce(small_of(s, 6, n), sq[s][:, 0:n, :], AX_X, ALU.add).then_inc(n_var, 1)

                def invert(i, s, n):
                    dve.wait_ge(n_std, in_layer(l, i, s) + 1)
                    v.reciprocal(small_of(s, 7, n), small_of(s, 7, n)).then_inc(n_rstd, 1)

                def mlp_input(i, s, n):
                    dve.wait_ge(n_in[s], loaded(l, i, s))
                    wait(dve, m_turned, (2 * i + s - 1) * len(STEPS[0]))
                    a = node_in[s][0].rearrange("p c w -> p (c w)")[:, 0:n * AW].rearrange("p (c w) -> p c w", w=AW)
                    v.tensor_copy(deg[:, ds(cols(i, s), n)], a[:, :, D])
                    v.scalar_tensor_tensor(
                        out=node_in[s][1].rearrange("p c w -> p (c w)")[:, 0:n * D].rearrange("p (c w) -> p c w", w=D),
                        in0=x_of(i, s, n), scalar=eps1[:, 0:1], in1=a[:, :, 0:D],
                        op0=ALU.mult, op1=ALU.add).then_inc(m_h, 1)

                def body_mlp(i, s, n):
                    last = before(i, s)
                    add_step(i, s, n, 0)
                    if last:
                        total(*last)
                    add_step(i, s, n, 1)
                    if last:
                        centre(*last)
                    add_step(i, s, n, 2)
                    if not (isinstance(i, int) and 2 * i + s + 2 > CHUNKS):
                        mlp_input(i + 1, s, TAIL if isinstance(i, int) and i == HALF - 1 else CH)
                    if last:
                        variance(*last)
                    add_step(i, s, n, 3)
                    if last:
                        invert(*last)

                def body(i, s, n):
                    last, next_ = before(i, s), behind(i, s)
                    if l == 0 and next_:
                        maxima(*next_)
                    add(i, s, n)
                    if l == 0 and next_:
                        shares(*next_)
                    if last:
                        variance(*last)
                    total(i, s, n)
                    if last:
                        invert(*last)
                    centre(i, s, n)
                    if l == 0 and next_:
                        scale_even(*next_)

                tail = (HALF, 0, TAIL)
                if l == 1:
                    link(v.tensor_scalar(eps1[:, :], eps1[:, :], 1.0, None, ALU.add))
                    mlp_input(0, 0, CH)
                    mlp_input(0, 1, CH)
                    chunks(dve, body_mlp)
                    total(*tail)
                    centre(*tail)
                else:
                    if l == 0:
                        for stage in (maxima, shares, scale_even):
                            stage(0, 0, CH)
                    chunks(dve, body)
                variance(*tail)
                invert(*tail)

            after_states(dve)
            dve.wait_ge(mlp_in, 16 * (4 * B + 1))
            nodes(0)
            for f in (cj, ci):
                last = v.memset(f[P - 32:P, LASTP:COLS], 0.0)
            last.then_inc(factors_cleared, 1)
            for k in range(2):
                v.memset(val[k][:, :, D], 1.0)

            def edges(l):
                c = Chain(dve, ge[l], 2)

                def body(i, k):
                    c.body(2 * i + k)
                    g = (l - 1) * NG + 2 * i + k
                    dve.wait_ge(g_key_row, g + 1)
                    wait(dve, g_sum, g - 1)
                    for a in range(G):
                        w = (a + 1) * P
                        last = v.tensor_scalar(same[k][:, a, 0:w], bank(k)[:, 0:w], key_at[k][:, a:a + 1], None,
                                               ALU.is_equal)
                    last.then_inc(g_same, 1)
                    if l == 1:
                        dve.wait_ge(attr_in[k], attr_loaded(i, k))
                        dve.wait_ge(g_got[k], transferred(0, i + 1, k))
                        v.tensor_tensor(xg[k][:, :, :], xg[k][:, :, :], attr[k][:, :, :], ALU.add).then_inc(g_sent_in, 1)
                        dve.wait_ge(g_same, g + 1)
                        count_earlier(c, k)
                        c.wait()
                        wait(dve, agg_sent[k], transferred(0, i, k))
                        cs = ds((2 * i + k) * G, G)
                        first_edges(c, k, count[k][:, :], dst_rel[:, cs], [first_at[k][:, :], dst_first[:, cs]], g_firsts_at)

                after_nodes(dve, l - 1)
                groups(dve, body)

            for l in (1, 2, 3):
                edges(l)
                after_edges(dve, l)
                nodes(l)
                if l == 1:
                    after_nodes(dve, 1)
                    link(v.tensor_scalar(deg[:, :], deg[:, :], 1.0, None, ALU.max))
                    v.reciprocal(deg[:, :], deg[:, :]).then_inc(n_share, 1)


_INS = ['x', 'src', 'dst', 'edge_attr_2', 'edge_attr_32', 'node_vec1', 'node_vec1_n2', 'L0_gnn_weight',
        'L0_gnn_root_weight', 'L0_gnn_att_weight', 'L0_gnn_bias', 'L1_gnn_eps', 'L1_gnn_W1', 'L1_gnn_b1',
        'L1_gnn_W2', 'L1_gnn_b2']
_OUTS = [((100000, 32), 'float32')]


def kernel(**inputs):
    import numpy as _np
    import concourse.bacc as _bacc
    from concourse import mybir as _mybir
    from concourse.bass_utils import run_bass_kernel_spmd as _run

    nc = _bacc.Bacc("TRN2", target_bir_lowering=False, num_devices=1)
    arrays, args = {}, []
    for name in _INS:
        a = _np.ascontiguousarray(inputs[name])
        arrays[f"in_{name}_dram"] = a
        args.append(nc.dram_tensor(f"in_{name}_dram", a.shape, _mybir.dt.from_np(a.dtype), kind="ExternalInput").ap())
    for i, (shape, dtype) in enumerate(_OUTS):
        dt = _mybir.dt.from_np(_np.dtype(dtype))
        args.append(nc.dram_tensor(f"out_{i}_dram", shape, dt, kind="ExternalOutput").ap())
    gnn_program(nc, *args)
    r = _run(nc, [arrays], core_ids=[0])
    got = tuple(r.results[0][f"out_{i}_dram"] for i in range(len(_OUTS)))
    return got[0]
```
